# Optimizing a Trainium2 kernel written in Bass

```python
import numpy as np
import jax
import jax.numpy as jnp

def _softmax(x, axis=-1):
    return jax.nn.softmax(x, axis=axis)

def _gelu(x):
    return jax.nn.gelu(x, approximate=True)

def _silu(x):
    return jax.nn.silu(x)

def _sigmoid(x):
    return jax.nn.sigmoid(x)

def _layernorm(x, axis=-1, eps=1e-05):
    m = jnp.mean(x, axis=axis, keepdims=True)
    v = jnp.var(x, axis=axis, keepdims=True)
    return (x - m) / jnp.sqrt(v + eps)

def _scatter_add(tgt, idx, src, axis=0):
    return tgt.at[idx].add(src)

def _segment_sum(src, seg, n):
    return jax.ops.segment_sum(src, seg, n)
kernel_name = 'mk_early_fusion_d1_tok_img1024_r4_fcfea9'

def setup_inputs(seed: int=0):
    np.random.seed(seed)
    _w = jnp.asarray

    def _rec_inputs():
        import jax
        import jax.numpy as jnp
        _rk = jax.random.key(seed)
        x = -0.000348323 + 0.999952 * jax.random.normal(jax.random.fold_in(_rk, 1), (32, 3, 96, 96), jnp.float32)
        txt = -0.000563189 + 0.999639 * jax.random.normal(jax.random.fold_in(_rk, 2), (32, 128, 256), jnp.float32)
        return (x, txt)
    x, txt = _rec_inputs()

    def _L0_tok_setup():
        import jax, jax.numpy as jnp
        import numpy as np
        from jax import lax
        PATCH = 16
        key = jax.random.key(seed)
        k1, k2 = jax.random.split(key)
        B, C, IMG, HID = (32, 3, 96, 256)
        inputs = jax.random.normal(k1, (B, C, IMG, IMG), dtype=jnp.float32)
        flat = C * PATCH * PATCH
        W = jax.random.normal(k2, (flat, HID), dtype=jnp.float32) / np.sqrt(flat)
        return {'inputs': inputs, 'W': W}
    _L0_tok_all = _L0_tok_setup()
    _L0_tok_in = {k: v for k, v in _L0_tok_all.items() if k in ('W',)}
    del _L0_tok_all

    def _L0_attn_setup():
        import jax, jax.numpy as jnp
        import numpy as np
        B, S, IN_DIM, D_MODEL, NUM_HEADS = (4, 512, 256, 256, 16)
        HEAD_DIM = D_MODEL // NUM_HEADS
        CAUSAL = True
        NEG = -9000000000000000.0

        def _xavier(key, shape):
            fan_out, fan_in = shape
            limit = (6.0 / (fan_in + fan_out)) ** 0.5
            return jax.random.uniform(key, shape, jnp.float32, -limit, limit)
        key = jax.random.key(seed)
        ks = jax.random.split(key, 5)
        x = jax.random.normal(ks[0], (B, S, IN_DIM), jnp.float32)
        Wq = _xavier(ks[1], (D_MODEL, IN_DIM))
        Wk = _xavier(ks[2], (D_MODEL, IN_DIM))
        Wv = _xavier(ks[3], (D_MODEL, IN_DIM))
        Wo = _xavier(ks[4], (D_MODEL, D_MODEL))
        bq = jnp.zeros((D_MODEL,), jnp.float32)
        bk = jnp.zeros((D_MODEL,), jnp.float32)
        bv = jnp.zeros((D_MODEL,), jnp.float32)
        bo = jnp.zeros((D_MODEL,), jnp.float32)
        return {'x': x, 'Wq': Wq, 'bq': bq, 'Wk': Wk, 'bk': bk, 'Wv': Wv, 'bv': bv, 'Wo': Wo, 'bo': bo}
    _L0_attn_all = _L0_attn_setup()
    _L0_attn_in = {k: v for k, v in _L0_attn_all.items() if k in ('Wq', 'bq', 'Wk', 'bk', 'Wv', 'bv', 'Wo', 'bo')}
    del _L0_attn_all

    def _L0_ffn_setup():
        import jax, jax.numpy as jnp
        import numpy as np
        B, T, C = (2, 256, 256)
        H = 1024
        E_R, E_S, K = (8, 2, 2)

        def _rmsnorm(x, g):
            eps = jnp.finfo(x.dtype).eps
            return x * jax.lax.rsqrt(jnp.mean(x * x, axis=-1, keepdims=True) + eps) * g

        def _experts_mlp(x, g, W1, b1, W2, b2):
            xn = _rmsnorm(x, g)
            h = jnp.einsum('btc,ech->bteh', xn, W1) + b1
            h = jax.nn.gelu(h, approximate=False)
            return jnp.einsum('bteh,ehc->btec', h, W2) + b2
        key = jax.random.key(seed)
        ks = jax.random.split(key, 12)
        s = 0.02
        return {'u': jax.random.normal(ks[0], (B, T, C), dtype=jnp.float32), 'g_shared': jnp.ones((C,), jnp.float32), 'W1_s': jax.random.normal(ks[1], (E_S, C, H), jnp.float32) * s, 'b1_s': jax.random.normal(ks[2], (E_S, H), jnp.float32) * s, 'W2_s': jax.random.normal(ks[3], (E_S, H, C), jnp.float32) * s, 'b2_s': jax.random.normal(ks[4], (E_S, C), jnp.float32) * s, 'g_routed': jnp.ones((C,), jnp.float32), 'W1_r': jax.random.normal(ks[5], (E_R, C, H), jnp.float32) * s, 'b1_r': jax.random.normal(ks[6], (E_R, H), jnp.float32) * s, 'W2_r': jax.random.normal(ks[7], (E_R, H, C), jnp.float32) * s, 'b2_r': jax.random.normal(ks[8], (E_R, C), jnp.float32) * s, 'centroids': jax.random.normal(ks[9], (C, E_R), jnp.float32) * s}
    _L0_ffn_all = _L0_ffn_setup()
    _L0_ffn_in = {k: v for k, v in _L0_ffn_all.items() if k in ('g_shared', 'W1_s', 'b1_s', 'W2_s', 'b2_s', 'g_routed', 'W1_r', 'b1_r', 'W2_r', 'b2_r', 'centroids')}
    del _L0_ffn_all
    return {'x': x, 'txt': txt, 'L0_tok_W': _L0_tok_in['W'], 'L0_attn_Wq': _L0_attn_in['Wq'], 'L0_attn_bq': _L0_attn_in['bq'], 'L0_attn_Wk': _L0_attn_in['Wk'], 'L0_attn_bk': _L0_attn_in['bk'], 'L0_attn_Wv': _L0_attn_in['Wv'], 'L0_attn_bv': _L0_attn_in['bv'], 'L0_attn_Wo': _L0_attn_in['Wo'], 'L0_attn_bo': _L0_attn_in['bo'], 'L0_ffn_g_shared': _L0_ffn_in['g_shared'], 'L0_ffn_W1_s': _L0_ffn_in['W1_s'], 'L0_ffn_b1_s': _L0_ffn_in['b1_s'], 'L0_ffn_W2_s': _L0_ffn_in['W2_s'], 'L0_ffn_b2_s': _L0_ffn_in['b2_s'], 'L0_ffn_g_routed': _L0_ffn_in['g_routed'], 'L0_ffn_W1_r': _L0_ffn_in['W1_r'], 'L0_ffn_b1_r': _L0_ffn_in['b1_r'], 'L0_ffn_W2_r': _L0_ffn_in['W2_r'], 'L0_ffn_b2_r': _L0_ffn_in['b2_r'], 'L0_ffn_centroids': _L0_ffn_in['centroids']}

def reference(x, txt, L0_tok_W, L0_attn_Wq, L0_attn_bq, L0_attn_Wk, L0_attn_bk, L0_attn_Wv, L0_attn_bv, L0_attn_Wo, L0_attn_bo, L0_ffn_g_shared, L0_ffn_W1_s, L0_ffn_b1_s, L0_ffn_W2_s, L0_ffn_b2_s, L0_ffn_g_routed, L0_ffn_W1_r, L0_ffn_b1_r, L0_ffn_W2_r, L0_ffn_b2_r, L0_ffn_centroids):
    import jax
    import jax.numpy as jnp

    def _L0_tok_ref(inputs, W):
        import jax, jax.numpy as jnp
        import numpy as np
        from jax import lax
        PATCH = 16
        B, C, H, Wimg = inputs.shape
        patches = lax.conv_general_dilated_patches(inputs, filter_shape=[PATCH, PATCH], window_strides=[PATCH, PATCH], padding='VALID', dimension_numbers=('NCHW', 'HWIO', 'NCHW'))
        patches = patches.reshape(B, -1, C * PATCH * PATCH)
        return jnp.einsum('bnf,fh->bnh', patches, W)

    def _L0_attn_ref(x, Wq, bq, Wk, bk, Wv, bv, Wo, bo):
        import jax, jax.numpy as jnp
        import numpy as np
        B, S, IN_DIM, D_MODEL, NUM_HEADS = (4, 512, 256, 256, 16)
        HEAD_DIM = D_MODEL // NUM_HEADS
        CAUSAL = True
        NEG = -9000000000000000.0

        def _xavier(key, shape):
            fan_out, fan_in = shape
            limit = (6.0 / (fan_in + fan_out)) ** 0.5
            return jax.random.uniform(key, shape, jnp.float32, -limit, limit)
        batch, seq, _ = x.shape
        q = x @ Wq.T + bq
        k = x @ Wk.T + bk
        v = x @ Wv.T + bv

        def split(t):
            return t.reshape(batch, seq, NUM_HEADS, HEAD_DIM).transpose(0, 2, 1, 3)
        q, k, v = (split(q), split(k), split(v))
        scores = jnp.einsum('bhqd,bhkd->bhqk', q, k) / jnp.sqrt(jnp.float32(HEAD_DIM))
        if CAUSAL:
            mask = jnp.tril(jnp.ones((seq, seq), bool))
            scores = jnp.where(mask, scores, jnp.float32(NEG))
        attn = jax.nn.softmax(scores, axis=-1)
        out = jnp.einsum('bhqk,bhkd->bhqd', attn, v)
        out = out.transpose(0, 2, 1, 3).reshape(batch, seq, D_MODEL)
        return out @ Wo.T + bo

    def _L0_ffn_ref(u, g_shared, W1_s, b1_s, W2_s, b2_s, g_routed, W1_r, b1_r, W2_r, b2_r, centroids):
        import jax, jax.numpy as jnp
        import numpy as np
        B, T, C = (2, 256, 256)
        H = 1024
        E_R, E_S, K = (8, 2, 2)

        def _rmsnorm(x, g):
            eps = jnp.finfo(x.dtype).eps
            return x * jax.lax.rsqrt(jnp.mean(x * x, axis=-1, keepdims=True) + eps) * g

        def _experts_mlp(x, g, W1, b1, W2, b2):
            xn = _rmsnorm(x, g)
            h = jnp.einsum('btc,ech->bteh', xn, W1) + b1
            h = jax.nn.gelu(h, approximate=False)
            return jnp.einsum('bteh,ehc->btec', h, W2) + b2
        h_s = _experts_mlp(u, g_shared, W1_s, b1_s, W2_s, b2_s).sum(axis=-2)
        scores = jax.nn.sigmoid(u @ centroids)
        gpk, i_topk = jax.lax.top_k(scores, K)
        gk = gpk / scores.sum(axis=-1, keepdims=True)
        routed_all = _experts_mlp(u, g_routed, W1_r, b1_r, W2_r, b2_r)
        routed_topk = jnp.take_along_axis(routed_all, i_topk[..., None], axis=2)
        h_r = (gk[..., None] * routed_topk).sum(axis=-2)
        return u + h_s + h_r
    h = _L0_tok_ref(x, L0_tok_W)
    h = jnp.concatenate([h, txt], axis=1)
    h = h + _L0_attn_ref(_layernorm(h, axis=-1), L0_attn_Wq, L0_attn_bq, L0_attn_Wk, L0_attn_bk, L0_attn_Wv, L0_attn_bv, L0_attn_Wo, L0_attn_bo)
    h = h + _L0_ffn_ref(_layernorm(h, axis=-1), L0_ffn_g_shared, L0_ffn_W1_s, L0_ffn_b1_s, L0_ffn_W2_s, L0_ffn_b2_s, L0_ffn_g_routed, L0_ffn_W1_r, L0_ffn_b1_r, L0_ffn_W2_r, L0_ffn_b2_r, L0_ffn_centroids)
    return h

_drawn_inputs = setup_inputs


def setup_inputs(seed=0):
    import zlib

    import numpy as np

    out = dict(_drawn_inputs(seed))
    spreads = {'L0_attn_bq': (0.0, 0.376),
     'L0_attn_bk': (0.0, 2.0),
     'L0_attn_bv': (0.0, 0.1),
     'L0_attn_bo': (0.0, 0.1),
     'L0_ffn_g_shared': (1.0, 0.6),
     'L0_ffn_g_routed': (1.0, 0.6)}
    factors = {'L0_ffn_b1_s': 8.0,
     'L0_ffn_b2_s': 4.549,
     'L0_ffn_W1_r': 5.011,
     'L0_ffn_b1_r': 8.0,
     'L0_ffn_W2_r': 4.872,
     'L0_ffn_b2_r': 23.063,
     'L0_ffn_centroids': 5.506}
    for name, (base, spread) in spreads.items():
        noise = np.random.default_rng([zlib.crc32(name.encode()), seed]).standard_normal(out[name].shape)
        drawn = base * np.exp(spread * noise) if base else spread * noise
        out[name] = jnp.asarray(drawn.astype(out[name].dtype))
    for name, factor in factors.items():
        out[name] = (out[name] * factor).astype(out[name].dtype)
    return out
```

```python
import concourse.bass as bass
from concourse import mybir
from contextlib import ExitStack

F32 = mybir.dt.float32
F16 = mybir.dt.float16
BF16 = mybir.dt.bfloat16
I32 = mybir.dt.int32
ACT = mybir.ActivationFunctionType
ALU = mybir.AluOpType
AX = mybir.AxisListType.X

P = 128
BATCH, CHANNELS, IMAGE, PATCH = 32, 3, 96, 16
GRID = IMAGE // PATCH
NPATCH = GRID * GRID
FLAT = CHANNELS * PATCH * PATCH
TEXT = 128
SEQ = NPATCH + TEXT
D = 256
KD = D // P
HEADS, HD = 16, 16
HG = P // HD
TOKENS = BATCH * SEQ
TT = TOKENS // P
LN_EPS = 1e-5
NEG = -9.0e15


def reached(value, n):
    return not isinstance(value, int) or value >= n


def patch_embed(nc, x, W, patches, T):
    NT = BATCH * NPATCH // P
    PER = 3
    with ExitStack() as ctx:
        sb = lambda n, s, d=F32: ctx.enter_context(nc.sbuf_tensor(n, s, d))
        sem = lambda n: ctx.enter_context(nc.semaphore(n))
        planes = sb("planes", [BATCH * CHANNELS, IMAGE * IMAGE])
        ordered = sb("ordered", [BATCH * CHANNELS, IMAGE * IMAGE])
        w_sb = sb("tok_w", [P, FLAT // P, D])
        rows = sb("patch_rows", [P, NT, FLAT])
        rowsT = sb("patch_rows_T", [P, PER, FLAT])
        h_out = sb("patch_h_rows", [P, NT, D])
        ps = [ctx.enter_context(nc.psum_tensor(f"pe_ps{i}", [P, 512], F32)) for i in range(8)]
        plane_in = [sem(f"plane_in{i}") for i in range(GRID)]
        w_in, row_in, patches_out = sem("w_in"), sem("row_in"), sem("patches_out")
        reordered_v, reordered_a = sem("reordered_v"), sem("reordered_a")
        t_done, t_copied, mm_done, h_copied, h_stored = (
            sem("t_done"), sem("t_copied"), sem("mm_done"), sem("h_copied"), sem("h_stored"))
        x_v = x.rearrange("b c h w -> (b c) (h w)")
        BAND = PATCH * IMAGE
        src = planes[:].rearrange("p (y i x j) -> p y i j x", y=GRID, i=PATCH, x=GRID)
        dst = ordered[:].rearrange("p (i j y x) -> p y i j x", i=PATCH, j=PATCH, y=GRID)
        with nc.Block() as block:
            @block.sync
            def _(sp):
                for y in range(GRID):
                    sp.dma_start(planes[:, y * BAND:(y + 1) * BAND],
                                 x_v[:, y * BAND:(y + 1) * BAND]).then_inc(plane_in[y], 16)
                sp.dma_start(w_sb[:], W.rearrange("(k p) d -> p k d", p=P)).then_inc(w_in, 16)
                sp.wait_ge(reordered_v, GRID // 2)
                sp.wait_ge(reordered_a, GRID // 2)
                sp.dma_start(patches, ordered[:]).then_inc(patches_out, 16)
                sp.wait_ge(patches_out, 16)
                sp.dma_start(rows[:], patches.rearrange("a b -> (a b)").rearrange(
                    "(t p f) -> p t f", p=P, f=FLAT)).then_inc(row_in, 16)
                sp.wait_ge(h_copied, NT)
                sp.dma_start(T["patch_h"].rearrange("(t p) d -> p t d", p=P), h_out[:]).then_inc(h_stored, 16)
                sp.wait_ge(h_stored, 16)

            @block.vector
            def _(dve):
                for n, y in enumerate(range(0, GRID, 2)):
                    dve.wait_ge(plane_in[y], 16)
                    dve.tensor_copy(dst[:, y], src[:, y]).then_inc(reordered_v, 1)
                with dve.Fori(0, NT // PER) as r:
                    for u in range(PER):
                        dve.wait_ge(t_done, r * PER + u + 1)
                        dve.tensor_copy(rowsT[:, u, 0:512], ps[2 * u][:, :])
                        dve.tensor_copy(rowsT[:, u, 512:FLAT], ps[2 * u + 1][:, 0:FLAT - 512]).then_inc(t_copied, 1)

            @block.scalar
            def _(act):
                for n, y in enumerate(range(1, GRID, 2)):
                    act.wait_ge(plane_in[y], 16)
                    act.activation(dst[:, y], src[:, y], ACT.Copy).then_inc(reordered_a, 1)
                with act.Fori(0, NT // PER) as r:
                    for u in range(PER):
                        act.wait_ge(mm_done, r * PER + u + 1)
                        act.activation(h_out[:, bass.ds(r * PER + u, 1), :].rearrange("p a d -> p (a d)"),
                                       ps[6 + u % 2][:, 0:D], ACT.Copy).then_inc(h_copied, 1)

            @block.tensor
            def _(pe):
                pe.wait_ge(row_in, 16)
                pe.wait_ge(w_in, 16)
                for r in range(NT // PER):
                    for u in range(PER):
                        for k in range(FLAT // P):
                            o = ps[2 * u + k // 4][:, (k % 4) * P:(k % 4 + 1) * P]
                            if k == 0 and r:
                                pe.wait_ge(t_copied, (r - 1) * PER + u + 1)
                            mm = pe.transpose(o, rows[:, r * PER + u, k * P:(k + 1) * P], T["ident"][:])
                        mm.then_inc(t_done, 1)
                    for u in range(PER):
                        n = r * PER + u
                        pe.wait_ge(t_copied, n + 1)
                        if n >= 2:
                            pe.wait_ge(h_copied, n if u == 0 else n - 1)
                        for k in range(FLAT // P):
                            mm = pe.matmul(ps[6 + u % 2][:, 0:D], rowsT[:, u, k * P:(k + 1) * P], w_sb[:, k, :],
                                           start=k == 0, stop=k == FLAT // P - 1)
                        mm.then_inc(mm_done, 1)


def moments_of(dve, stats, mean, squares, gap, sem, count):
    dve.tensor_tensor(gap[:], stats[:, :, 1], stats[:, :, 4], ALU.subtract)
    dve.tensor_tensor(mean[:], stats[:, :, 1], stats[:, :, 4], ALU.add)
    dve.tensor_tensor(squares[:], stats[:, :, 2], stats[:, :, 5], ALU.add).then_inc(sem, 1)
    dve.wait_ge(sem, count + 1)
    dve.tensor_tensor(gap[:], gap[:], gap[:], ALU.mult)
    dve.tensor_scalar(mean[:], mean[:], 0.5, None, ALU.mult).then_inc(sem, 1)
    dve.wait_ge(sem, count + 2)
    dve.scalar_tensor_tensor(squares[:], gap[:], D / 4, squares[:], ALU.mult, ALU.add).then_inc(sem, 1)
    dve.wait_ge(sem, count + 3)


def attention(nc, txt, A, T):
    STEPS = 2 * BATCH
    GD = HG * HD
    with ExitStack() as ctx:
        sb = lambda n, s, d=F32: ctx.enter_context(nc.sbuf_tensor(n, s, d))
        sem = lambda n: ctx.enter_context(nc.semaphore(n))
        NB = BATCH + 1
        h_text = sb("h_text", [P, NB, D])
        h_patch = sb("h_patch", [NPATCH, NB, D])
        stats = sb("ln_stats", [P, 2, NB, 6])
        mean = sb("ln_mean", [P, 2 * NB])
        mean_gap = sb("ln_mean_gap", [P, 2 * NB])
        rstd = sb("ln_rstd", [P, 2 * NB])
        expo = sb("ln_expo", [P, 2 * NB])
        w_in = sb("attn_w_in", [P, 4, KD, D])
        wT = sb("attn_wT", [P, 4, KD, D])
        bq = sb("bq", [P, KD])
        bk = sb("bk", [P, KD])
        bv = sb("bv", [P, D])
        bo = sb("bo", [P, D])
        head_of = sb("head_of", [P, HG])
        causal = sb("causal", [P, 3, SEQ], BF16)
        causal_p = sb("causal_p", [NPATCH, HG, NPATCH], BF16)
        identb = sb("identb", [P, P], BF16)
        xn = [sb(f"xn{i}", [P, D]) for i in range(2)]
        xn_p = [sb(f"xn_p{i}", [NPATCH, D]) for i in range(2)]
        xnT = sb("xnT", [P, KD, SEQ])
        qT = [sb(f"qT{i}", [P, SEQ]) for i in range(2)]
        kT = [sb(f"kT{i}", [P, SEQ]) for i in range(2)]
        kbd = [sb(f"kbd{i}", [P, HG, SEQ]) for i in range(2)]
        vbd = [sb(f"vbd{i}", [P, HG * (GD + HD)]) for i in range(4)]
        vbd_p = [sb(f"vbd_p{i}", [NPATCH, HG * (GD + HD)]) for i in range(4)]
        prob = [sb(f"prob{i}", [P, HG, SEQ]) for i in range(2)]
        prob_p = [sb(f"prob_p{i}", [NPATCH, HG, NPATCH]) for i in range(2)]
        top = [sb(f"top{i}", [P, HG]) for i in range(2)]
        top_p = [sb(f"top_p{i}", [NPATCH, HG]) for i in range(2)]
        inv = [sb(f"inv{i}", [P, HG]) for i in range(2)]
        inv_p = [sb(f"inv_p{i}", [NPATCH, HG]) for i in range(2)]
        pT = sb("pT", [P, HG, TEXT])
        pT_p = sb("pT_p", [NPATCH, HG, SEQ])
        oT = [sb(f"oT{i}", [P, SEQ]) for i in range(2)]
        hb = [sb(f"hb{i}", [P, D]) for i in range(2)]
        hb_p = [sb(f"hb_p{i}", [NPATCH, D]) for i in range(2)]
        h2 = [sb(f"h2_{i}", [P, D]) for i in range(2)]
        h2_p = [sb(f"h2_p{i}", [NPATCH, D]) for i in range(2)]
        bank = [ctx.enter_context(nc.psum_tensor(f"at_ps{i}", [P, 512], F32)) for i in range(3, 8)]
        sc = ctx.enter_context(nc.psum_tensor("at_scores", [P, 3, 512], F32))
        sc_p, turn, qk_ps, vo_ps = bank[0], [bank[1], bank[2]], bank[3], bank[4]

        names = ("text_in patch_in attn_w_in_s bias_in w_turned w_copied bn_done bn_aggr_done pad_done eps_done rstd_done "
                 "consts_done selected vzero xn_ready xt_done xnT_ready qk_done qk_ready v_done v_ready kbd_ready s_done "
                 "maxed shifted exp_done summed inv_ready pn_ready t_done t_ready pv_done oT_ready wo_done "
                 "hb_ready h2_ready h2_stored bias_scaled").split()
        S = {n: sem(n) for n in names}
        h2_stored = [sem(f"h2_stored{i}") for i in range(2)]

        with nc.Block() as block:
            @block.sync
            def _(sp):
                for n, name in enumerate(("Wq", "Wk", "Wv", "Wo")):
                    sp.dma_start(w_in[:, n], A[name].rearrange("(m p) c -> p m c", p=P)).then_inc(S["attn_w_in_s"], 16)
                with nc.allow_non_contiguous_dma(reason="256 biases onto partitions"):
                    sp.dma_start(bq[:], A["bq"].rearrange("(m p) -> p m", p=P)).then_inc(S["bias_in"], 16)
                    sp.dma_start(bk[:], A["bk"].rearrange("(m p) -> p m", p=P)).then_inc(S["bias_in"], 16)
                sp.dma_start(bv[:], A["bv"].partition_broadcast(P)).then_inc(S["bias_in"], 16)
                sp.dma_start(bo[:], A["bo"].partition_broadcast(P)).then_inc(S["bias_in"], 16)
                sp.dma_start(h_text[:, 0:BATCH], txt.rearrange("b p d -> p b d")).then_inc(S["text_in"], 16)
                sp.dma_start(h_patch[:, 0:BATCH], T["patch_h"].rearrange("(b p) d -> p b d", p=NPATCH)).then_inc(S["patch_in"], 16)

            @block.gpsimd
            def _(g):
                g.memset(causal[:], 0.0)
                g.memset(causal_p[:], 0.0)
                g.memset(head_of[:], 1.0)
                g.memset(identb[:], 0.0)
                g.memset(expo[:], -0.5)
                g.memset(stats[:], 1.0)
                g.memset(h_text[:, BATCH], 0.0)
                g.memset(h_patch[:, BATCH], 0.0)
                for i in range(4):
                    g.memset(vbd[i][:], 0.0)
                    last = g.memset(vbd_p[i][:], 0.0)
                last.then_inc(S["consts_done"], 1)
                g.wait_ge(S["consts_done"], 1)
                g.affine_select(out=causal[:, :, NPATCH:], in_=causal[:, :, NPATCH:], compare_op=ALU.is_ge, fill=NEG,
                                base=0, pattern=[[0, 3], [-1, TEXT]], channel_multiplier=1)
                g.affine_select(out=causal_p[:], in_=causal_p[:], compare_op=ALU.is_ge, fill=NEG,
                                base=0, pattern=[[0, HG], [-1, NPATCH]], channel_multiplier=1)
                g.affine_select(out=identb[:], in_=identb[:], compare_op=ALU.not_equal, fill=1.0,
                                base=0, pattern=[[-1, P]], channel_multiplier=1)
                g.affine_select(out=head_of[:], in_=head_of[:], compare_op=ALU.is_ge, fill=0.0,
                                base=0, pattern=[[-HD, HG]], channel_multiplier=1).then_inc(S["selected"], 1)
                g.wait_ge(S["selected"], 1)
                g.affine_select(out=head_of[:], in_=head_of[:], compare_op=ALU.is_ge, fill=0.0,
                                base=HD - 1, pattern=[[HD, HG]], channel_multiplier=-1).then_inc(S["selected"], 1)
                g.wait_ge(S["eps_done"], 1)
                g.tensor_tensor(rstd[:], rstd[:], expo[:], ALU.pow).then_inc(S["rstd_done"], 1)

            @block.vector
            def _(dve):
                dve.wait_ge(S["consts_done"], 1)
                dve.wait_ge(S["text_in"], 16)
                dve.wait_ge(S["patch_in"], 16)
                with dve.Fori(0, NB) as b:
                    row = lambda t: t[:, bass.ds(b, 1), :].rearrange("p a d -> p (a d)")
                    dve.bn_stats(row(stats[:, 0]), row(h_text)).then_inc(S["bn_done"], 1)
                    dve.bn_stats(row(stats[0:NPATCH, 1]), row(h_patch)).then_inc(S["bn_done"], 1)
                dve.wait_ge(S["bn_done"], 2 * NB)
                moments_of(dve, stats[:].rearrange("p r b s -> p (r b) s"), mean, rstd, mean_gap, S["bn_done"], 2 * NB)
                dve.tensor_scalar(rstd[:], rstd[:], 1.0 / D, LN_EPS, ALU.mult, ALU.add).then_inc(S["eps_done"], 1)
                dve.wait_ge(S["bias_in"], 64)
                dve.tensor_scalar(bq[:], bq[:], HD ** -0.5, None, ALU.mult).then_inc(S["bias_scaled"], 1)

            @block.scalar
            def _(act):
                for n in range(4):
                    act.wait_ge(S["w_turned"], n + 1)
                    act.activation(wT[:, n].rearrange("p k d -> p (k d)"), bank[n][:, :], ACT.Copy).then_inc(S["w_copied"], 1)

            @block.tensor
            def _(pe):
                pe.wait_ge(S["attn_w_in_s"], 64)
                for n in range(4):
                    for k in range(KD):
                        for m in range(KD):
                            mm = pe.transpose(bank[n][:, k * D + m * P:k * D + (m + 1) * P],
                                              w_in[:, n, m, k * P:(k + 1) * P], T["ident"][:])
                    mm.then_inc(S["w_turned"], 1)

        WQ, WK, WV, WO = range(4)
        TURN_HEADS = [range(0, 4), range(0, 4), range(4, HG), range(4, HG), range(HG)]

        def run(eng, step, tail):
            for i in range(2):
                for u in range(4):
                    step(4 * i + u, 2 * i + u // 2, u, i)
            with eng.Fori(2, STEPS // 4) as i:
                for u in range(4):
                    step(4 * i + u, 2 * i + u // 2, u, i)
            for u in range(2):
                tail(STEPS + u, BATCH, u)

        with nc.Block() as block:
            @block.tensor
            def _(pe):
                def turn_xn(b, par):
                    pe.wait_ge(S["xn_ready"], b + 1)
                    for k in range(KD):
                        pe.transpose(qk_ps[:, k * SEQ + NPATCH:(k + 1) * SEQ], xn[par][:, k * P:(k + 1) * P],
                                     T["ident"][:])
                        mm = pe.transpose(qk_ps[:, k * SEQ:k * SEQ + NPATCH], xn_p[par][:, k * P:(k + 1) * P],
                                          T["ident"][0:NPATCH, 0:NPATCH])
                    mm.then_inc(S["xt_done"], 1)

                def out_project(b):
                    pe.wait_ge(S["oT_ready"], 2 * b + 2)
                    for rows, o in ((slice(NPATCH, SEQ), vo_ps[:, 0:D]), (slice(0, NPATCH), vo_ps[0:NPATCH, D:2 * D])):
                        for g in range(2):
                            mm = pe.matmul(o, oT[g][:, rows], wT[:, WO, g, :], start=g == 0, stop=g == 1)
                    mm.then_inc(S["wo_done"], 1)

                def attend(s, slot, v_count):
                    q = slot % 2
                    pe.wait_ge(S["qk_ready"], v_count)
                    pe.wait_ge(S["pn_ready"], s + 1)
                    for n in range(5):
                        if n == 2:
                            pe.wait_ge(S["t_ready"], 5 * s + 2)
                        for h in TURN_HEADS[n]:
                            if n == 4:
                                mm = pe.transpose(qk_ps[0:NPATCH, h * NPATCH:(h + 1) * NPATCH], prob_p[q][:, h, :],
                                                  T["ident"][0:NPATCH, 0:NPATCH])
                            elif n % 2:
                                mm = pe.transpose(turn[1][0:NPATCH, h % 4 * TEXT:(h % 4 + 1) * TEXT],
                                                  prob[q][:, h, 0:NPATCH], T["ident"][:])
                            else:
                                mm = pe.transpose(turn[0][:, h % 4 * TEXT:(h % 4 + 1) * TEXT], prob[q][:, h, NPATCH:],
                                                  T["ident"][:])
                        mm.then_inc(S["t_done"], 1)
                    pe.wait_ge(S["t_ready"], 5 * s + 5)
                    pe.wait_ge(S["v_ready"], v_count)
                    for h in range(HG):
                        pe.matmul(vo_ps[:, 0:SEQ], vbd_p[slot][:, h * GD:(h + 1) * GD], pT_p[:, h, :], start=h == 0, stop=False)
                        mm = pe.matmul(vo_ps[:, NPATCH:SEQ], vbd[slot][:, h * GD:(h + 1) * GD], pT[:, h, :], start=False, stop=h == HG - 1)
                    mm.then_inc(S["pv_done"], 1)

                def project(s, b, u):
                    g = u % 2
                    cols = slice(g * GD, (g + 1) * GD)
                    pe.wait_ge(S["xnT_ready"], b + 1)
                    if reached(s, 1):
                        pe.wait_ge(S["qk_ready"], s)
                    for w, c in ((WQ, 0), (WK, SEQ)):
                        for k in range(KD):
                            mm = pe.matmul(qk_ps[:, c:c + SEQ], wT[:, w, k, cols], xnT[:, k, :],
                                           start=k == 0, stop=k == KD - 1)
                    mm.then_inc(S["qk_done"], 1)
                    if g == 0 and reached(s, 4):
                        pe.wait_ge(S["h2_ready"], b - 1)
                    if reached(s, 3):
                        pe.wait_ge(S["oT_ready"], s - 2)
                    elif s >= 1:
                        pe.wait_ge(S["v_ready"], s)
                    for rows, o in ((slice(NPATCH, SEQ), vo_ps[:, 0:GD]), (slice(0, NPATCH), vo_ps[0:NPATCH, GD:2 * GD])):
                        for k in range(KD):
                            mm = pe.matmul(o, xnT[:, k, rows], wT[:, WV, k, cols], start=k == 0, stop=k == KD - 1)
                    mm.then_inc(S["v_done"], 1)

                def scores(s, u):
                    q = u % 2
                    pe.wait_ge(S["kbd_ready"], s + 1)
                    if reached(s, 1):
                        pe.wait_ge(S["shifted"], s)
                    for j, n in ((0, 3), (1, 3), (2, 2)):
                        o = sc[:, j, 0:n * SEQ]
                        pe.matmul(o, identb[:], causal[:, 0:n, :].rearrange("p h k -> p (h k)"), start=True, stop=False)
                        pe.matmul(o, qT[q][:, NPATCH:], kbd[q][:, 3 * j:3 * j + n, :].rearrange("p h k -> p (h k)"),
                                  start=False, stop=True)
                    o = sc_p[0:NPATCH, 0:HG * NPATCH]
                    pe.matmul(o, identb[0:NPATCH, 0:NPATCH], causal_p[:].rearrange("p h k -> p (h k)"), start=True, stop=False)
                    pe.matmul(o, qT[q][:, 0:NPATCH], kbd[q][:, :, 0:NPATCH], start=False, stop=True).then_inc(S["s_done"], 1)

                def step(s, b, u, i):
                    project(s, b, u)
                    if reached(s, 2):
                        attend(s - 2, (u - 2) % 4, s + 1)
                        if u % 2:
                            out_project(b - 1)
                    if u % 2:
                        pe.wait_ge(S["qk_ready"], s + 1)
                        turn_xn(b + 1, (u // 2 + 1) % 2)
                    scores(s, u)

                def tail(s, b, u):
                    if u == 0:
                        pe.wait_ge(S["h2_ready"], BATCH - 1)
                    else:
                        pe.wait_ge(S["oT_ready"], STEPS - 1)
                    attend(s - 2, (u - 2) % 4, STEPS)
                    if u % 2:
                        out_project(b - 1)

                turn_xn(0, 0)
                run(pe, step, tail)

            @block.scalar
            def _(act):
                def step(s, b, u, i):
                    q, g = u % 2, u % 2
                    act.wait_ge(S["qk_done"], s + 1)
                    act.activation(qT[q][:], qk_ps[:, 0:SEQ], ACT.Identity, bias=bq[:, g:g + 1], scale=HD ** -0.5)
                    act.activation(kT[q][:], qk_ps[:, SEQ:2 * SEQ], ACT.Identity, bias=bk[:, g:g + 1]).then_inc(S["qk_ready"], 1)
                    lagged(s, u, reached(s, 2), reached(s, 1))
                    if u % 2:
                        turned_xn(b + 1)

                def turned_xn(b):
                    act.wait_ge(S["xt_done"], b + 1)
                    act.activation(xnT[:].rearrange("p k c -> p (k c)"), qk_ps[:, 0:KD * SEQ], ACT.Copy).then_inc(S["xnT_ready"], 1)

                def lagged(s, u, two, one):
                    if two:
                        for n in range(5):
                            act.wait_ge(S["t_done"], 5 * (s - 2) + n + 1)
                            heads = slice(TURN_HEADS[n][0], TURN_HEADS[n][-1] + 1)
                            if n == 4:
                                o = pT_p[:, :, 0:NPATCH]
                                i = qk_ps[0:NPATCH, 0:HG * NPATCH].rearrange("p (h q) -> p h q", h=HG)
                            elif n % 2:
                                o, i = pT_p[:, heads, NPATCH:], turn[1][0:NPATCH, :].rearrange("p (h q) -> p h q", h=4)
                            else:
                                o, i = pT[:, heads, :], turn[0][:, :].rearrange("p (h q) -> p h q", h=4)
                            act.activation(o, i, ACT.Copy).then_inc(S["t_ready"], 1)
                    if one:
                        q = (u - 1) % 2
                        act.wait_ge(S["shifted"], s)
                        act.activation(prob[q][:].rearrange("p h k -> p (h k)"), prob[q][:].rearrange("p h k -> p (h k)"), ACT.Exp)
                        act.activation(prob_p[q][:].rearrange("p h k -> p (h k)"), prob_p[q][:].rearrange("p h k -> p (h k)"),
                                       ACT.Exp).then_inc(S["exp_done"], 1)
                    if two:
                        act.wait_ge(S["pv_done"], s - 1)
                        act.activation(oT[u % 2][:], vo_ps[:, 0:SEQ], ACT.Copy).then_inc(S["oT_ready"], 1)

                turned_xn(0)
                run(act, step, lambda s, b, u: lagged(s, u, True, u == 0))

            @block.gpsimd
            def _(g):
                def step(s, b, u, i):
                    q = u % 2
                    if u % 2 == 0:
                        if reached(b, 2):
                            g.wait_ge(S["h2_ready"], b - 1)
                        row = lambda t: t[:, bass.ds(b, 1), :].rearrange("p a d -> p (a d)")
                        g.tensor_tensor(hb[u // 2][:], row(h_text), bo[:], ALU.add)
                        g.tensor_tensor(hb_p[u // 2][:], row(h_patch), bo[0:NPATCH], ALU.add).then_inc(S["hb_ready"], 1)
                    g.wait_ge(S["qk_ready"], s + 1)
                    g.tensor_tensor(kbd[q][:], kT[q][:].unsqueeze(1).to_broadcast([P, HG, SEQ]),
                                    head_of[:].unsqueeze(2).to_broadcast([P, HG, SEQ]), ALU.mult).then_inc(S["kbd_ready"], 1)
                    if reached(s, 1):
                        normalise(s - 1, (u - 1) % 2)

                def normalise(s, q):
                    g.wait_ge(S["inv_ready"], s + 1)
                    g.tensor_tensor(prob[q][:], prob[q][:], inv[q][:].unsqueeze(2).to_broadcast([P, HG, SEQ]), ALU.mult)
                    g.tensor_tensor(prob_p[q][:], prob_p[q][:], inv_p[q][:].unsqueeze(2).to_broadcast([NPATCH, HG, NPATCH]),
                                    ALU.mult).then_inc(S["pn_ready"], 1)

                run(g, step, lambda s, b, u: normalise(s - 1, 1) if u == 0 else None)

            @block.vector
            def _(dve):
                def normed(b, par):
                    row = lambda t: t[:, bass.ds(b, 1), :].rearrange("p a d -> p (a d)")
                    for o, src, col, n in ((xn[par], h_text, b, P), (xn_p[par], h_patch, NB + b, NPATCH)):
                        last = dve.tensor_scalar(o[:], row(src), mean[0:n, bass.ds(col, 1)], rstd[0:n, bass.ds(col, 1)], ALU.subtract, ALU.mult)
                    last.then_inc(S["xn_ready"], 1)

                def shift(s, q):
                    dve.wait_ge(S["s_done"], s + 1)
                    six = sc[:, 0:2, 0:3 * SEQ].rearrange("p j (h k) -> p j h k", h=3)
                    two = sc[:, 2, 0:2 * SEQ].rearrange("p (h k) -> p h k", h=2)
                    pat = sc_p[0:NPATCH, 0:HG * NPATCH].rearrange("p (h k) -> p h k", h=HG)
                    dve.tensor_reduce(top[q][:, 0:6].rearrange("p (j h) -> p j h", j=2), six, AX, ALU.max)
                    dve.tensor_reduce(top[q][:, 6:8], two, AX, ALU.max)
                    dve.tensor_reduce(top_p[q][:], pat, AX, ALU.max).then_inc(S["maxed"], 1)
                    dve.wait_ge(S["maxed"], s + 1)
                    dve.tensor_tensor(prob[q][:, 0:6, :].rearrange("p (j h) k -> p j h k", j=2), six,
                                      top[q][:, 0:6].rearrange("p (j h) -> p j h", j=2).unsqueeze(3).to_broadcast([P, 2, 3, SEQ]), ALU.subtract)
                    dve.tensor_tensor(prob[q][:, 6:8, :], two, top[q][:, 6:8].unsqueeze(2).to_broadcast([P, 2, SEQ]), ALU.subtract)
                    dve.tensor_tensor(prob_p[q][:], pat, top_p[q][:].unsqueeze(2).to_broadcast([NPATCH, HG, NPATCH]),
                                      ALU.subtract).then_inc(S["shifted"], 1)

                def total(s, q):
                    dve.wait_ge(S["exp_done"], s + 1)
                    dve.tensor_reduce(inv[q][:], prob[q][:], AX, ALU.add)
                    dve.tensor_reduce(inv_p[q][:], prob_p[q][:], AX, ALU.add).then_inc(S["summed"], 1)
                    dve.wait_ge(S["summed"], s + 1)
                    dve.reciprocal(inv[q][:], inv[q][:])
                    dve.reciprocal(inv_p[q][:], inv_p[q][:]).then_inc(S["inv_ready"], 1)

                def residual(b, par, old):
                    dve.wait_ge(S["wo_done"], b + 1)
                    dve.wait_ge(S["hb_ready"], b + 1)
                    if reached(old, 1):
                        dve.wait_ge(h2_stored[par], 32 * old)
                    dve.tensor_tensor(h2[par][:], vo_ps[:, 0:D], hb[par][:], ALU.add)
                    dve.tensor_tensor(h2_p[par][:], vo_ps[0:NPATCH, D:2 * D], hb_p[par][:], ALU.add).then_inc(S["h2_ready"], 1)

                def step(s, b, u, i):
                    g = u % 2
                    if reached(s, 1):
                        shift(s - 1, (u - 1) % 2)
                    dve.wait_ge(S["v_done"], s + 1)
                    for t, src, n in ((vbd[u], vo_ps[:, 0:GD], P), (vbd_p[u], vo_ps[0:NPATCH, GD:2 * GD], NPATCH)):
                        own = t[:].rearrange("p (h c) -> p h c", c=GD + HD)[:, :, 0:HD]
                        last = dve.tensor_tensor(own, src.rearrange("p (h c) -> p h c", h=HG),
                                                 bv[0:n, g * GD:(g + 1) * GD].rearrange("p (h c) -> p h c", h=HG), ALU.add)
                    last.then_inc(S["v_ready"], 1)
                    if g == 0:
                        normed(b + 1, (u // 2 + 1) % 2)
                    if reached(s, 1):
                        total(s - 1, (u - 1) % 2)
                    if g == 1 and reached(s, 2):
                        residual(b - 1, (u // 2 + 1) % 2, i - (u == 1))

                def tail(s, b, u):
                    if u == 0:
                        shift(s - 1, 1)
                        total(s - 1, 1)
                    else:
                        residual(b - 1, 1, BATCH // 2 - 1)

                normed(0, 0)
                run(dve, step, tail)

            @block.sync
            def _(sp):
                with sp.Fori(0, BATCH // 2) as i:
                    for par in range(2):
                        b = 2 * i + par
                        sp.wait_ge(S["h2_ready"], b + 1)
                        sp.dma_start(T["h2"][bass.ds(b * SEQ + NPATCH, TEXT), :], h2[par][:]).then_inc(h2_stored[par], 16)
                        sp.dma_start(T["h2"][bass.ds(b * SEQ, NPATCH), :], h2_p[par][:]).then_inc(h2_stored[par], 16)
                for par in range(2):
                    sp.wait_ge(h2_stored[par], 16 * BATCH)


EXPERTS, SHARED, TOP = 8, 2, 2
HID = 1024
HJ = HID // P
TILE = 256
BLK = TILE // P
NT = (TOP * TOKENS + EXPERTS * (TILE - 1)) // TILE
GROUPS = -(-TOKENS // TILE)
RMS_EPS = 1.1920929e-07
X_SCALE = 1024.0


def router(nc, A, T):
    with ExitStack() as ctx:
        sb = lambda n, s, d=F32: ctx.enter_context(nc.sbuf_tensor(n, s, d))
        h2 = sb("r_h2", [P, TT, D])
        stats = sb("r_stats", [P, TT, 6])
        mean, var, gap, ms = (sb(f"r_{n}", [P, TT]) for n in ("mean", "var", "gap", "ms"))
        a, r, inv_r, ar, opa, nma = (sb(f"r_{n}", [P, TT]) for n in ("a", "r", "inv_r", "ar", "opa", "nma"))
        minus_half, half = sb("r_minus_half", [P, TT]), sb("r_half", [P, TT])
        xr = [sb(f"r_xn{i}", [P, D]) for i in range(2)]
        xT = [sb(f"r_xT{i}", [P, KD, P]) for i in range(2)]
        cent = sb("r_cent", [P, KD, EXPERTS])
        b2s = sb("r_b2s", [P, SHARED, D])
        zeros = sb("r_zeros", [P, 2048])
        score = sb("r_score", [P, TT, EXPERTS])
        lower = sb("r_lower", [P, EXPERTS, EXPERTS])
        above = sb("r_above", [P, TT, EXPERTS, EXPERTS])
        equal = sb("r_equal", [P, TT, EXPERTS, EXPERTS])
        rank, sel, gate, pos, cnt, run_a, run_b, slot, pick = (
            sb(f"r_{n}", [P, TT, EXPERTS]) for n in ("rank", "sel", "gate", "pos", "cnt", "run_a", "run_b", "slot", "pick"))
        total, inv_total, both = (sb(f"r_{n}", [P, TT]) for n in ("total", "inv_total", "both"))
        slot_f = sb("r_slot_f", [P, 2, TT])
        before, ones = sb("r_before", [P, P]), sb("r_ones", [P, P])
        padded_i = sb("r_padded_i", [P, EXPERTS], I32)
        padded, base_a, base_b = (sb(f"r_{n}", [P, EXPERTS]) for n in ("padded", "base_a", "base_b"))
        start_i, start = sb("r_start_i", [P, NT], I32), sb("r_start", [P, NT])
        passed, tile_e = sb("r_passed", [P, NT, EXPERTS - 1]), sb("r_tile_e", [P, NT])
        ps = [ctx.enter_context(nc.psum_tensor(f"r_ps{i}", [P, 512], F32)) for i in range(6)]
        names = ("h2_in_base h2_in small_in consts bn_done moments eps_done root_done root_used xn_ready turned xT_ready "
                 "logits_done scored chain sel_ready counted base_ready base_stored zeroed consts_b").split()
        S = {n: ctx.enter_context(nc.semaphore(n)) for n in names}
        xn_stored = [ctx.enter_context(nc.semaphore(f"xn_stored{i}")) for i in range(2)]

        def run(step):
            for u in range(2):
                step(u, u, 0)
            return step

        with nc.Block() as block:
            @block.sync
            def _(sp):
                sp.dma_start(h2[:], T["h2"].rearrange("(t p) d -> p t d", p=P)).then_inc(S["h2_in"], 16)
                sp.dma_start(cent[:], A["centroids"].rearrange("(k p) e -> p k e", p=P)).then_inc(S["small_in"], 16)
                sp.dma_start(b2s[:].rearrange("p s d -> p (s d)"), A["b2_s"].rearrange("s d -> (s d)").partition_broadcast(P)).then_inc(S["small_in"], 16)
                sp.wait_ge(S["consts"], 1)
                zrows = P * 2048 // D
                for n in range(-(-(NT + 1) * TILE // zrows)):
                    lo, hi = n * zrows, min((n + 1) * zrows, (NT + 1) * TILE)
                    sp.dma_start(T["xg"][lo:hi].rearrange("(p q) d -> p (q d)", p=P), zeros[:, 0:(hi - lo) * D // P]).then_inc(S["zeroed"], 16)
                rest = T["xn"][TOKENS:, :]
                sp.dma_start(rest.rearrange("(p q) d -> p (q d)", p=P), zeros[:, 0:rest.shape[0] * D // P]).then_inc(S["zeroed"], 16)
                rest = T["base"][TOKENS:, :]
                sp.dma_start(rest.rearrange("(p q) d -> p (q d)", p=P), zeros[:, 0:rest.shape[0] * D // P]).then_inc(S["zeroed"], 16)
                zs = (-(-(NT + 1) * TILE // zrows) + 2) * 16

                def store(t, u):
                    sp.wait_ge(S["xn_ready"], t + 1)
                    sp.dma_start(T["xn"][bass.ds(t * P, P), :], xr[u][:]).then_inc(xn_stored[u], 16)
                with sp.Fori(0, TT // 2) as i:
                    for u in range(2):
                        store(2 * i + u, u)
                store(TT - 1, 0)
                sp.wait_ge(S["base_ready"], 1)
                sp.dma_start(T["base"][0:TOKENS].rearrange("(t p) d -> p t d", p=P), h2[:]).then_inc(S["base_stored"], 16)
                sp.wait_ge(S["base_stored"], 16)
                sp.wait_ge(S["zeroed"], zs)
                sp.wait_ge(xn_stored[0], 16 * (TT // 2 + 1))
                sp.wait_ge(xn_stored[1], 16 * (TT // 2))

            @block.gpsimd
            def _(g):
                g.memset(zeros[:], 0.0).then_inc(S["consts"], 1)
                g.memset(minus_half[:], -0.5)
                g.memset(half[:], 0.5)
                g.memset(lower[:], 1.0)
                g.memset(before[:], 1.0)
                g.memset(ones[:], 1.0)
                g.iota(start_i[:], pattern=[[TILE, NT]], base=0, channel_multiplier=0).then_inc(S["consts"], 1)
                g.wait_ge(S["consts"], 2)
                g.affine_select(out=lower[:], in_=lower[:], compare_op=ALU.is_gt, fill=0.0, base=0,
                                pattern=[[1, EXPERTS], [-1, EXPERTS]], channel_multiplier=0)
                g.affine_select(out=before[:], in_=before[:], compare_op=ALU.is_gt, fill=0.0, base=0,
                                pattern=[[1, P]], channel_multiplier=-1)
                g.tensor_copy(start[:], start_i[:]).then_inc(S["consts_b"], 1)
                g.wait_ge(S["eps_done"], 1)
                g.tensor_tensor(a[:], var[:], minus_half[:], ALU.pow).then_inc(S["root_done"], 1)
                g.wait_ge(S["eps_done"], 2)
                g.tensor_tensor(r[:], ms[:], minus_half[:], ALU.pow)
                g.tensor_tensor(inv_r[:], ms[:], half[:], ALU.pow).then_inc(S["root_done"], 1)
                g.wait_ge(S["eps_done"], 3)
                g.wait_ge(S["small_in"], 32)
                g.tensor_tensor(b2s[:, 0], b2s[:, 0], b2s[:, 1], ALU.add).then_inc(S["consts_b"], 1)
                g.wait_ge(S["h2_in_base"], TT)
                g.wait_ge(S["consts_b"], 2)
                g.tensor_tensor(h2[:], h2[:], b2s[:, 0].unsqueeze(1).to_broadcast([P, TT, D]), ALU.add).then_inc(S["base_ready"], 1)

            @block.tensor
            def _(pe):
                pe.wait_ge(S["small_in"], 32)

                def tile(t, u, n):
                    pe.wait_ge(S["xn_ready"], t + 1)
                    if n >= 2:
                        pe.wait_ge(S["xT_ready"], t - 1)
                    for k in range(KD):
                        mm = pe.transpose(ps[u][:, k * P:(k + 1) * P], xr[u][:, k * P:(k + 1) * P], T["ident"][:])
                    mm.then_inc(S["turned"], 1)
                    pe.wait_ge(S["xT_ready"], t + 1)
                    if n >= 2:
                        pe.wait_ge(S["scored"], t - 1)
                    for k in range(KD):
                        mm = pe.matmul(ps[2 + u][:, 0:EXPERTS], xT[u][:, k, :], cent[:, k, :], start=k == 0, stop=k == KD - 1)
                    mm.then_inc(S["logits_done"], 1)
                for u in range(2):
                    tile(u, u, u)
                with pe.Fori(1, TT // 2) as i:
                    for u in range(2):
                        tile(2 * i + u, u, 2)
                tile(TT - 1, 0, 2)
                pe.wait_ge(S["sel_ready"], 1)
                pe.wait_ge(S["consts_b"], 1)
                flat = sel[:].rearrange("p t e -> p (t e)")
                pe.matmul(ps[4][:, 0:TT * EXPERTS], before[:], flat, start=True, stop=True)
                pe.matmul(ps[5][:, 0:TT * EXPERTS], ones[:], flat, start=True, stop=True).then_inc(S["counted"], 1)

            @block.scalar
            def _(act):
                def tile(t, u, n):
                    act.wait_ge(S["turned"], t + 1)
                    act.activation(xT[u][:].rearrange("p k c -> p (k c)"), ps[u][:, 0:D], ACT.Copy).then_inc(S["xT_ready"], 1)
                    act.wait_ge(S["logits_done"], t + 1)
                    act.activation(score[:, bass.ds(t, 1), :].rearrange("p a e -> p (a e)"), ps[2 + u][:, 0:EXPERTS],
                                   ACT.Sigmoid, scale=inv_r[:, bass.ds(t, 1)]).then_inc(S["scored"], 1)
                with act.Fori(0, TT // 2) as i:
                    for u in range(2):
                        tile(2 * i + u, u, 2)
                tile(TT - 1, 0, 2)

            @block.vector
            def _(dve):
                dve.wait_ge(S["h2_in"], 16)
                with dve.Fori(0, TT) as t:
                    row = lambda x: x[:, bass.ds(t, 1), :].rearrange("p a d -> p (a d)")
                    dve.bn_stats(row(stats), row(h2)).then_inc(S["bn_done"], 1)
                dve.wait_ge(S["bn_done"], TT)
                moments_of(dve, stats[:], mean, var, gap, S["bn_done"], TT)
                n = [0]

                def link(ins):
                    ins.then_inc(S["chain"], 1)
                    n[0] += 1
                    dve.wait_ge(S["chain"], n[0])
                link(dve.tensor_scalar(ms[:], var[:], 1.0 / D, None, ALU.mult))
                dve.tensor_scalar(var[:], var[:], 1.0 / D, LN_EPS, ALU.mult, ALU.add).then_inc(S["eps_done"], 1)
                dve.wait_ge(S["root_done"], 1)
                link(dve.tensor_tensor(ms[:], ms[:], a[:], ALU.mult))
                link(dve.tensor_tensor(ms[:], ms[:], a[:], ALU.mult))
                dve.tensor_scalar(ms[:], ms[:], RMS_EPS, None, ALU.add).then_inc(S["eps_done"], 1)
                dve.tensor_scalar(opa[:], a[:], 1.0, None, ALU.add)
                link(dve.scalar_tensor_tensor(nma[:], mean[:], -1.0, a[:], ALU.mult, ALU.mult))
                dve.wait_ge(S["root_done"], 2)
                dve.tensor_tensor(ar[:], a[:], r[:], ALU.mult).then_inc(S["eps_done"], 1)
                dve.wait_ge(S["eps_done"], 3)

                def tile(t, u, stored):
                    if stored is not None:
                        dve.wait_ge(xn_stored[u], 16 * stored)
                        dve.wait_ge(S["turned"], t - 1)
                    row = h2[:, bass.ds(t, 1), :].rearrange("p a d -> p (a d)")
                    dve.tensor_scalar(xr[u][:], row, mean[:, bass.ds(t, 1)], ar[:, bass.ds(t, 1)],
                                      ALU.subtract, ALU.mult).then_inc(S["xn_ready"], 1)
                    dve.tensor_scalar(row, row, opa[:, bass.ds(t, 1)], nma[:, bass.ds(t, 1)], ALU.mult,
                                      ALU.add).then_inc(S["h2_in_base"], 1)
                for u in range(2):
                    tile(u, u, None)
                with dve.Fori(1, TT // 2) as i:
                    for u in range(2):
                        tile(2 * i + u, u, i)
                tile(TT - 1, 0, TT // 2)

                dve.wait_ge(S["scored"], TT)
                dve.wait_ge(S["consts_b"], 1)
                per = [P, TT, EXPERTS, EXPERTS]
                other, own = score[:].unsqueeze(2).to_broadcast(per), score[:].unsqueeze(3).to_broadcast(per)
                dve.tensor_tensor(above[:], other, own, ALU.is_gt)
                link(dve.tensor_tensor(equal[:], other, own, ALU.is_equal))
                link(dve.tensor_tensor(equal[:], equal[:], lower[:].unsqueeze(1).to_broadcast(per), ALU.mult))
                link(dve.tensor_tensor(above[:], above[:], equal[:], ALU.add))
                link(dve.tensor_reduce(rank[:], above[:], AX, ALU.add))
                link(dve.tensor_scalar(sel[:], rank[:], float(TOP), None, ALU.is_lt))
                dve.tensor_scalar(pick[:], sel[:], 1.0, None, ALU.mult).then_inc(S["sel_ready"], 1)
                link(dve.tensor_reduce(total[:], score[:], AX, ALU.add))
                link(dve.reciprocal(inv_total[:], total[:]))
                link(dve.tensor_tensor(gate[:], score[:], sel[:], ALU.mult))
                per = [P, TT, EXPERTS]
                link(dve.tensor_tensor(gate[:], gate[:], inv_total[:].unsqueeze(2).to_broadcast(per), ALU.mult))
                dve.wait_ge(S["counted"], 1)
                link(dve.tensor_copy(pos[:].rearrange("p t e -> p (t e)"), ps[4][:, 0:TT * EXPERTS]))
                dve.tensor_copy(cnt[:].rearrange("p t e -> p (t e)"), ps[5][:, 0:TT * EXPERTS])
                link(dve.tensor_copy(run_a[:].rearrange("p t e -> p (t e)"), ps[5][:, 0:TT * EXPERTS]))
                x, y, d = run_a, run_b, 1
                while d < TT:
                    dve.tensor_copy(y[:, 0:d], x[:, 0:d])
                    link(dve.tensor_tensor(y[:, d:], x[:, d:], x[:, 0:TT - d], ALU.add))
                    x, y, d = y, x, 2 * d
                link(dve.tensor_scalar(padded_i[:], x[:, TT - 1], float(TILE - 1), None, ALU.add))
                link(dve.tensor_scalar(padded_i[:], padded_i[:], -TILE, None, ALU.bitwise_and))
                link(dve.tensor_copy(padded[:], padded_i[:]))
                link(dve.tensor_copy(base_a[:], padded[:]))
                xb, yb, d = base_a, base_b, 1
                while d < EXPERTS:
                    dve.tensor_copy(yb[:, 0:d], xb[:, 0:d])
                    link(dve.tensor_tensor(yb[:, d:], xb[:, d:], xb[:, 0:EXPERTS - d], ALU.add))
                    xb, yb, d = yb, xb, 2 * d
                link(dve.tensor_tensor(yb[:], xb[:], padded[:], ALU.subtract))
                dve.tensor_tensor(pos[:], pos[:], x[:], ALU.add)
                per7 = [P, NT, EXPERTS - 1]
                link(dve.tensor_tensor(passed[:], yb[:, 1:].unsqueeze(1).to_broadcast(per7),
                                       start[:].unsqueeze(2).to_broadcast(per7), ALU.is_le))
                link(dve.tensor_reduce(tile_e[:], passed[:], AX, ALU.add))
                link(dve.tensor_copy(T["tile_expert"][:], tile_e[:]))
                link(dve.tensor_tensor(pos[:], pos[:], cnt[:], ALU.subtract))
                link(dve.tensor_tensor(slot[:], pos[:], yb[:].unsqueeze(1).to_broadcast(per), ALU.add))
                far = float(4 * NT * TILE)
                for n_slot, sign in ((0, 1.0), (1, -1.0)):
                    link(dve.tensor_scalar(pick[:], sel[:], -sign * far, sign * far, ALU.mult, ALU.add))
                    link(dve.tensor_tensor(pick[:], pick[:], slot[:], ALU.add))
                    link(dve.tensor_reduce(slot_f[:, n_slot], pick[:], AX, ALU.min if n_slot == 0 else ALU.max))
                    link(dve.tensor_tensor(pick[:], pick[:], slot_f[:, n_slot].unsqueeze(2).to_broadcast(per), ALU.is_equal))
                    link(dve.tensor_tensor(pick[:], pick[:], gate[:], ALU.mult))
                    link(dve.tensor_reduce(T["gate"][:, n_slot], pick[:], AX, ALU.add))
                link(dve.tensor_copy(T["slot"][:], slot_f[:]))


class Weights:

    PARTS = 4

    def __init__(self, nc, ctx, A, T, which, w1, w2, count):
        sb = lambda n, s, d=F32: ctx.enter_context(nc.sbuf_tensor(n + which, s, d))
        self.A, self.which, self.w1, self.w2, self.count = A, which, w1, w2, count
        self.scale, self.b1 = T["scale" + which], T["b1" + which]
        self.raw = [sb(f"raw{i}", [P, HID]) for i in range(self.PARTS)]
        self.top = sb("top", [P, self.PARTS * count])
        self.gain, self.gains = sb("gain", [P, KD]), sb("gains", [P, KD])
        self.pair, self.big, self.big_all, self.power = (sb(n, [P, c]) for n, c in (("pair", KD), ("big", 3), ("big_all", 3), ("power", 3)))
        self.raw_in = [ctx.enter_context(nc.semaphore(f"raw_in{i}{which}")) for i in range(self.PARTS)]
        self.S = {n: ctx.enter_context(nc.semaphore(n + which)) for n in
                  "gain_in topped chain bigs reduced scaled hi_done lo_done".split()}

    def load_gain(self, nc, sp):
        with nc.allow_non_contiguous_dma(reason="256 gains onto partitions"):
            sp.dma_start(self.gain[:], self.A["g" + self.which].rearrange("(k p) -> p k", p=P)).then_inc(self.S["gain_in"], 16)

    def of(self, tensor, e):
        return tensor[e] if isinstance(e, int) else tensor[bass.ds(e, 1)].rearrange("a b c -> (a b) c")

    def load(self, sp, e, second):
        for part in range(self.PARTS):
            before = self.count if second else 0
            if second:
                if isinstance(e, int) and e == 0:
                    sp.wait_ge(self.S["topped"], self.PARTS * self.count)
                else:
                    sp.wait_ge(self.S["lo_done"], self.PARTS * (e - 1) + part + 1)
            elif reached(e, 1):
                sp.wait_ge(self.S["topped"], self.PARTS * (e - 1) + part + 1)
            o = self.raw[part][:]
            if part < KD:
                src = self.of(self.A["W1" + self.which], e)[part * P:(part + 1) * P, :]
            else:
                o = o.rearrange("p (j d) -> p j d", j=HJ // 2)
                half = (part - KD) * (HJ // 2)
                src = self.of(self.A["W2" + self.which], e).rearrange("(j p) d -> p j d", p=P)[:, half:half + HJ // 2, :]
            sp.dma_start(o, src).then_inc(self.raw_in[part], 16)

    def largest(self, dve, e, part):
        dve.wait_ge(self.raw_in[part], 16 * (e + 1))
        o = self.top[:, bass.ds(part * self.count + e, 1)]
        dve.tensor_reduce(o, self.raw[part][:], AX, ALU.max, apply_absolute_value=True).then_inc(self.S["topped"], 1)

    def reduce(self, g):
        g.wait_ge(self.S["bigs"], 1)
        g.partition_all_reduce(self.big_all[:], self.big[:], P, bass.bass_isa.ReduceOp.max).then_inc(self.S["reduced"], 1)

    def find_scales(self, dve):
        S, top, big, big_all, power, scale, count = self.S, self.top, self.big, self.big_all, self.power, self.scale, self.count
        n_link = [0]

        def link(ins):
            ins.then_inc(S["chain"], 1)
            n_link[0] += 1
            dve.wait_ge(S["chain"], n_link[0])
        dve.wait_ge(S["gain_in"], 16)
        dve.wait_ge(S["topped"], self.PARTS * count)
        dve.tensor_reduce(self.pair[:], top[:, 0:KD * count].rearrange("p (k e) -> p k e", k=KD), AX, ALU.max)
        dve.tensor_reduce(big[:, 1:2], top[:, KD * count:], AX, ALU.max)
        link(dve.tensor_reduce(big[:, 2:3], self.b1[:], AX, ALU.max, apply_absolute_value=True))
        link(dve.tensor_tensor(self.pair[:], self.pair[:], self.gain[:], ALU.mult))
        dve.tensor_reduce(big[:, 0:1], self.pair[:], AX, ALU.max, apply_absolute_value=True).then_inc(S["bigs"], 1)
        dve.wait_ge(S["reduced"], 1)
        link(dve.scalar_tensor_tensor(big_all[:, 2:3], big_all[:, 0:1], float(D), big_all[:, 2:3], ALU.mult, ALU.add))
        link(dve.tensor_scalar(big_all[:], big_all[:], 1e-30, None, ALU.max))
        link(dve.tensor_scalar(power[:].bitcast(I32), big_all[:].bitcast(I32), 0x7F800000, None, ALU.bitwise_and))
        link(dve.reciprocal(big_all[:], power[:]))
        dve.tensor_scalar(scale[:, 0:1], big_all[:, 0:1], 2.0 ** 13, None, ALU.mult)
        dve.tensor_scalar(scale[:, 1:2], power[:, 0:1], 2.0 ** -13 / X_SCALE, None, ALU.mult)
        dve.tensor_scalar(scale[:, 2:3], big_all[:, 2:3], 2.0 ** 14, None, ALU.mult)
        dve.tensor_scalar(scale[:, 3:4], big_all[:, 1:2], 2.0 ** 13, None, ALU.mult)
        link(dve.scalar_tensor_tensor(scale[:, 4:5], power[:, 1:2], 2.0 ** -27, power[:, 2:3], ALU.mult, ALU.mult))
        dve.tensor_scalar(self.gains[:], self.gain[:], scale[:, 0:1], None, ALU.mult).then_inc(S["scaled"], 1)
        dve.wait_ge(S["scaled"], 1)

    def halves(self, e, part):
        if part < KD:
            to = lambda n: (self.w1[:, e, n, part, :] if isinstance(e, int) else
                            self.w1[:, bass.ds(e, 1), n, part, :].rearrange("p a c -> p (a c)"))
            return self.raw[part][:], self.gains[:, part:part + 1], to
        rows = slice((part - KD) * (HJ // 2), (part - KD + 1) * (HJ // 2))
        to = lambda n: (self.w2[:, e, n, rows, :].rearrange("p j d -> p (j d)") if isinstance(e, int) else
                        self.w2[:, bass.ds(e, 1), n, rows, :].rearrange("p a j d -> p (a j d)"))
        return self.raw[part][:], self.scale[:, 3:4], to

    def high(self, act, e, part):
        if isinstance(e, int) and e == 0 and part == 0:
            act.wait_ge(self.S["scaled"], 1)
        act.wait_ge(self.raw_in[part], 16 * (self.count + e + 1))
        src, factor, to = self.halves(e, part)
        act.activation(to(0), src, ACT.Copy, scale=factor).then_inc(self.S["hi_done"], 1)

    def low(self, dve, e, part):
        dve.wait_ge(self.S["hi_done"], self.PARTS * e + part + 1)
        src, factor, to = self.halves(e, part)
        dve.scalar_tensor_tensor(to(1), src, factor, to(0), ALU.mult, ALU.subtract).then_inc(self.S["lo_done"], 1)


def shared_weights(nc, A, T, w1, w2):
    with ExitStack() as ctx:
        W = Weights(nc, ctx, A, T, "_s", w1, w2, SHARED)
        SETS = (("_s", SHARED), ("_r", EXPERTS))
        rows = {w: ctx.enter_context(nc.sbuf_tensor("b1_rows" + w, [c * HJ, P], F32)) for w, c in SETS}
        ps = {w: ctx.enter_context(nc.psum_tensor("b1_ps" + w, [P, c * HJ], F32)) for w, c in SETS}
        b1_in, b1_turned, b1_ready = (ctx.enter_context(nc.semaphore(n)) for n in ("b1_in", "b1_turned", "b1_ready"))
        EP = [(e, part) for e in range(SHARED) for part in range(W.PARTS)]
        with nc.Block() as block:
            @block.sync
            def _(sp):
                W.load_gain(nc, sp)
                for w, _ in SETS:
                    sp.dma_start(rows[w][:], A["b1" + w].rearrange("e (j p) -> (e j) p", p=P)).then_inc(b1_in, 16)
                for second in (False, True):
                    for e in range(SHARED):
                        W.load(sp, e, second)

            @block.tensor
            def _(pe):
                pe.wait_ge(b1_in, 32)
                for w, c in SETS:
                    pe.transpose(ps[w][:], rows[w][:], T["ident"][0:c * HJ, 0:c * HJ]).then_inc(b1_turned, 1)

            @block.gpsimd
            def _(g):
                W.reduce(g)

            @block.scalar
            def _(act):
                for e, part in EP:
                    W.high(act, e, part)

            @block.vector
            def _(dve):
                dve.wait_ge(b1_turned, 2)
                for w, _ in SETS:
                    dve.tensor_copy(T["b1" + w][:], ps[w][:]).then_inc(b1_ready, 1)
                dve.wait_ge(b1_ready, 2)
                for e, part in EP:
                    W.largest(dve, e, part)
                W.find_scales(dve)
                for e, part in EP:
                    W.low(dve, e, part)
                dve.wait_ge(W.S["lo_done"], len(EP))


def ffn(nc, A, T, which, w1, w2, rounds, units, routed, routed_w=None):
    HI, LO = 0, 1
    src = T["xg"] if routed else T["xn"]
    with ExitStack() as ctx:
        sb = lambda n, s, d=F32: ctx.enter_context(nc.sbuf_tensor(n + which, s, d))
        sem = lambda n: ctx.enter_context(nc.semaphore(n + which))
        rows = sb("rows", [P, BLK, D])
        xh, xl = sb("xh", [P, KD, TILE], F16), sb("xl", [P, KD, TILE], F16)
        hf = [sb(f"hf{i}", [P, 2, TILE]) for i in range(2)]
        hh = [sb(f"hh{i}", [P, HJ, TILE], F16) for i in range(2)]
        hl = [sb(f"hl{i}", [P, HJ, TILE], F16) for i in range(2)]
        out = sb("out", [P, BLK, D])
        base = out
        b2 = sb("b2bc", [P, EXPERTS, D]) if routed else None
        pair = [ctx.enter_context(nc.psum_tensor(f"f_ps{i}{which}", [P, 2, TILE], F32)) for i in range(4)]
        y_ps = ctx.enter_context(nc.psum_tensor("f_y" + which, [P, BLK, D], F32))
        t_ps = ctx.enter_context(nc.psum_tensor("f_t" + which, [P, KD, TILE], F32))
        S = {n: sem(n) for n in "row_in base_in b2_in x_turned xh_ready xl_ready h_done gelu_done h_ready y_done y_ready y_stored staged".split()}
        scattered = [sem(f"scattered{i}") for i in range(2)]
        scale, b1 = T["scale" + which], T["b1" + which]
        TILES = rounds * units if routed else rounds
        UNITS = rounds * units

        R = Weights(nc, ctx, A, T, "_r", *routed_w, EXPERTS) if routed_w else None
        FIND, SPLIT, LEFT = 2, 2 + EXPERTS, 2 + 2 * EXPERTS

        def run(eng, unit, tail, find=None, between=None, split=None):
            def one(i, extra, e):
                for u in range(units):
                    unit(units * i + u, u, i)
                    if extra:
                        extra(e, u)
            for i in range(2):
                one(i, None, 0)
            if R is None:
                with eng.Fori(2, rounds) as i:
                    one(i, None, 0)
            else:
                one(FIND, find, 0)
                with eng.Fori(FIND + 1, SPLIT) as i:
                    one(i, find, i - FIND)
                if between:
                    between()
                one(SPLIT, split, 0)
                with eng.Fori(SPLIT + 1, LEFT) as i:
                    one(i, split, i - SPLIT)
                with eng.Fori(LEFT, rounds) as i:
                    one(i, None, 0)
            tail()

        def tile_of(n, i):
            return n if routed else i

        def turns(u):
            return routed or u == units - 1

        with nc.Block() as block:
            @block.sync
            def _(sp):
                if routed:
                    sp.dma_start(b2[:].rearrange("p e d -> p (e d)"), A["b2" + which].rearrange("e d -> (e d)").partition_broadcast(P)).then_inc(S["b2_in"], 16)

                def load(t):
                    sp.dma_start(rows[:], src[bass.ds(t * TILE, TILE), :].rearrange("(b p) d -> p b d", p=P)).then_inc(S["row_in"], 16)
                load(0)
                if not routed:
                    sp.dma_start(base[:], T["base"][0:TILE, :].rearrange("(b p) d -> p b d", p=P)).then_inc(S["base_in"], 16)

                def store(t):
                    sp.wait_ge(S["y_ready"], t + 1)
                    dst = T["y"] if routed else T["part"]
                    sp.dma_start(dst[bass.ds(t * TILE, TILE), :].rearrange("(b p) d -> p b d", p=P), out[:]).then_inc(S["y_stored"], 16)
                sp.wait_ge(S["x_turned"], 1)
                load(1)

                def tile(t):
                    sp.wait_ge(S["x_turned"], t + 1)
                    load(t + 1)
                    store(t - 1)
                    if not routed:
                        sp.wait_ge(S["y_stored"], 16 * t)
                        sp.dma_start(base[:], T["base"][bass.ds(t * TILE, TILE), :].rearrange("(b p) d -> p b d", p=P)).then_inc(S["base_in"], 16)
                if R is None:
                    with sp.Fori(1, TILES) as t:
                        tile(t)
                else:
                    R.load_gain(nc, sp)
                    tile(1)
                    for second, begin in ((False, FIND), (True, SPLIT)):
                        R.load(sp, 0, second)
                        tile(begin)
                        with sp.Fori(begin + 1, begin + EXPERTS) as t:
                            R.load(sp, t - begin, second)
                            tile(t)
                    with sp.Fori(LEFT, TILES) as t:
                        tile(t)
                store(TILES - 1)
                sp.wait_ge(S["y_stored"], 16 * TILES)
                sp.wait_ge(S["row_in"], 16 * (TILES + 1))
                if not routed:
                    sp.wait_ge(S["base_in"], 16 * TILES)

            @block.tensor
            def _(pe):
                def turn(t):
                    pe.wait_ge(S["row_in"], 16 * (t + 1))
                    for k in range(KD):
                        for b in range(BLK):
                            mm = pe.transpose(t_ps[:, k, b * P:(b + 1) * P], rows[:, b, k * P:(k + 1) * P], T["ident"][:])
                    mm.then_inc(S["x_turned"], 1)

                def up(n, u, i):
                    e = expert(n) if routed else u
                    pe.wait_ge(S["xl_ready"], tile_of(n, i) + 1)
                    for p in range(4):
                        if reached(n, 1):
                            pe.wait_ge(S["gelu_done"], 4 * n + p - 3)
                        for j2 in range(2):
                            o = pair[p][:, j2, :]
                            col = slice((2 * p + j2) * P, (2 * p + j2 + 1) * P)
                            for k in range(KD):
                                pe.matmul(o, w1_at(e, HI, k, col), xh[:, k, :], start=k == 0, stop=False)
                                pe.matmul(o, w1_at(e, HI, k, col), xl[:, k, :], start=False, stop=False)
                                mm = pe.matmul(o, w1_at(e, LO, k, col), xh[:, k, :], start=False, stop=k == KD - 1)
                        mm.then_inc(S["h_done"], 1)

                def down(n, u, tile):
                    e = expert(n) if routed else u
                    first, last = routed or u == 0, routed or u == units - 1
                    pe.wait_ge(S["h_ready"], 4 * n + 4)
                    if first and reached(tile, 1):
                        pe.wait_ge(S["y_ready"], tile)
                    q = u % 2
                    for j in range(HJ):
                        for b in range(BLK):
                            o, col = y_ps[:, b, :], slice(b * P, (b + 1) * P)
                            pe.matmul(o, hh[q][:, j, col], w2_at(e, HI, j), start=first and j == 0 and b == 0, stop=False)
                            pe.matmul(o, hh[q][:, j, col], w2_at(e, LO, j), start=False, stop=False)
                            mm = pe.matmul(o, hl[q][:, j, col], w2_at(e, HI, j), start=False, stop=last and j == HJ - 1 and b == BLK - 1)
                    if last:
                        mm.then_inc(S["y_done"], 1)

                def w1_at(e, part, k, col):
                    if routed:
                        return w1[:, bass.ds(e, 1), part, k, col].rearrange("p a c -> p (a c)")
                    return w1[:, e, part, k, col]

                def w2_at(e, part, j):
                    if routed:
                        return w2[:, bass.ds(e, 1), part, j, :].rearrange("p a c -> p (a c)")
                    return w2[:, e, part, j, :]

                def expert(n):
                    return pe.value_load(T["tile_expert"][0:1, bass.ds(n, 1)], min_val=0, max_val=EXPERTS - 1)

                def unit(n, u, i):
                    up(n, u, i)
                    if turns(u):
                        turn(tile_of(n, i) + 1)
                    if reached(n, 1):
                        pu = (u - 1) % units
                        down(n - 1, pu, tile_of(n - 1, i if u else i - 1))
                turn(0)
                run(pe, unit, lambda: down(UNITS - 1, units - 1, TILES - 1))

            @block.scalar
            def _(act):
                def split(t):
                    act.wait_ge(S["x_turned"], t + 1)
                    act.activation(xh[:].rearrange("p k c -> p (k c)"), t_ps[:].rearrange("p k c -> p (k c)"), ACT.Copy, scale=X_SCALE).then_inc(S["xh_ready"], 1)

                def unit(n, u, i):
                    if routed:
                        e = act.value_load(T["tile_expert"][0:1, bass.ds(n, 1)], min_val=0, max_val=EXPERTS - 1)
                    for p in range(4):
                        act.wait_ge(S["h_done"], 4 * n + p + 1)
                        if reached(n, 1) or p >= 2:
                            act.wait_ge(S["h_ready"], 4 * n + p - 1)
                        for j2 in range(2):
                            j = 2 * p + j2
                            bias = b1[:, bass.ds(e * HJ + j, 1)] if routed else b1[:, u * HJ + j:u * HJ + j + 1]
                            last = act.activation(hf[p % 2][:, j2, :], pair[p][:, j2, :], ACT.Gelu, bias=bias, scale=scale[:, 1:2])
                        last.then_inc(S["gelu_done"], 1)
                    if turns(u):
                        split(tile_of(n, i) + 1)
                split(0)
                per = Weights.PARTS // units
                run(act, unit, lambda: None,
                    split=lambda e, u: [R.high(act, e, part) for part in range(u * per, (u + 1) * per)])

            @block.vector
            def _(dve):
                def split(t):
                    dve.wait_ge(S["xh_ready"], t + 1)
                    dve.scalar_tensor_tensor(xl[:].rearrange("p k c -> p (k c)"), t_ps[:].rearrange("p k c -> p (k c)"), X_SCALE,
                                             xh[:].rearrange("p k c -> p (k c)"), ALU.mult, ALU.subtract).then_inc(S["xl_ready"], 1)

                def finish(n, tile):
                    dve.wait_ge(S["y_done"], tile + 1)
                    if reached(tile, 1):
                        dve.wait_ge(S["y_stored"], 16 * tile)
                    if routed:
                        e = dve.value_load(T["tile_expert"][0:1, bass.ds(n, 1)], min_val=0, max_val=EXPERTS - 1)
                        for b in range(BLK):
                            last = dve.scalar_tensor_tensor(out[:, b, :], y_ps[:, b, :], scale[:, 4:5],
                                                            b2[:, bass.ds(e, 1), :].rearrange("p a d -> p (a d)"), ALU.mult, ALU.add)
                    else:
                        dve.wait_ge(S["base_in"], 16 * (tile + 1))
                        last = dve.scalar_tensor_tensor(out[:], y_ps[:], scale[:, 4:5], base[:], ALU.mult, ALU.add)
                    last.then_inc(S["y_ready"], 1)

                def unit(n, u, i):
                    q = u % 2
                    for p in range(4):
                        dve.wait_ge(S["gelu_done"], 4 * n + p + 1)
                        o = slice(2 * p, 2 * p + 2)
                        dve.tensor_scalar(hh[q][:, o, :], hf[p % 2][:], scale[:, 2:3], None, ALU.mult).then_inc(S["staged"], 1)
                        dve.wait_ge(S["staged"], 4 * n + p + 1)
                        dve.scalar_tensor_tensor(hl[q][:, o, :], hf[p % 2][:], scale[:, 2:3], hh[q][:, o, :],
                                                 ALU.mult, ALU.subtract).then_inc(S["h_ready"], 1)
                    if turns(u):
                        split(tile_of(n, i) + 1)
                    pu = (u - 1) % units
                    if reached(n, 1) and (routed or pu == units - 1):
                        finish(n - 1, tile_of(n - 1, i if u else i - 1))
                if routed:
                    dve.wait_ge(S["b2_in"], 16)
                split(0)
                per = Weights.PARTS // units
                parts = lambda f: lambda e, u: [f(dve, e, part) for part in range(u * per, (u + 1) * per)]
                if R is None:
                    run(dve, unit, lambda: finish(UNITS - 1, TILES - 1))
                else:
                    run(dve, unit, lambda: finish(UNITS - 1, TILES - 1), parts(R.largest), lambda: R.find_scales(dve), parts(R.low))
                    dve.wait_ge(R.S["lo_done"], R.PARTS * EXPERTS)

            if not routed:
                @block.gpsimd
                def _(g):
                    scatter(g, nc, T, scattered, ctx)
                    R.reduce(g)


def scatter(g, nc, T, scattered, ctx):
    xr = [ctx.enter_context(nc.sbuf_tensor(f"sc_x{i}", [P, D], F32)) for i in range(2)]
    xr_in = [ctx.enter_context(nc.semaphore(f"sc_in{i}")) for i in range(2)]
    for t in range(TT):
        q = t % 2
        if t >= 2:
            g.wait_ge(scattered[q], 32 * (t // 2))
        g.dma_start(xr[q][:], T["xn"][t * P:(t + 1) * P, :]).then_inc(xr_in[q], 16)
        if t >= 1:
            send(g, T, xr, xr_in, scattered, t - 1)
    send(g, T, xr, xr_in, scattered, TT - 1)
    g.wait_ge(scattered[0], 32 * (TT // 2 + 1))
    g.wait_ge(scattered[1], 32 * (TT // 2))


def send(g, T, xr, xr_in, scattered, t):
    q = t % 2
    g.wait_ge(xr_in[q], 16 * (t // 2 + 1))
    for which in range(2):
        g.indirect_dma_start(T["xg"][:, :], bass.IndirectOffsetOnAxis(ap=T["slot"][:, which, t:t + 1], axis=0),
                             xr[q][:], None, bounds_check=NT * TILE - 1).then_inc(scattered[q], 16)


def combine(nc, T, out):
    with ExitStack() as ctx:
        RING = 4
        sb = lambda n, s, d=F32: ctx.enter_context(nc.sbuf_tensor(n, s, d))
        sem = lambda n: ctx.enter_context(nc.semaphore(n))
        part = [sb(f"c_part{i}", [P, D]) for i in range(RING)]
        ya = [sb(f"c_ya{i}", [P, D]) for i in range(RING)]
        yb = [sb(f"c_yb{i}", [P, D]) for i in range(RING)]
        part_in = [sem(f"c_part_in{i}") for i in range(RING)]
        y_in = [sem(f"c_y_in{i}") for i in range(RING)]
        stored = [sem(f"c_stored{i}") for i in range(RING)]
        half_done, done = sem("c_half_done"), sem("c_done")
        with nc.Block() as block:
            @block.gpsimd
            def _(g):
                for t in range(TT):
                    q = t % RING
                    if t >= RING:
                        g.wait_ge(done, t - RING + 1)
                    for which, y in ((0, ya), (1, yb)):
                        g.indirect_dma_start(y[q][:], None, T["y"][:, :], bass.IndirectOffsetOnAxis(ap=T["slot"][:, which, t:t + 1], axis=0),
                                             bounds_check=NT * TILE - 1).then_inc(y_in[q], 16)

            @block.sync
            def _(sp):
                for t in range(TT + 2):
                    if t < TT:
                        q = t % RING
                        if t >= RING:
                            sp.wait_ge(stored[q], 16 * (t // RING))
                        sp.dma_start(part[q][:], T["part"][t * P:(t + 1) * P, :]).then_inc(part_in[q], 16)
                    if t >= 2:
                        d = t - 2
                        sp.wait_ge(done, d + 1)
                        sp.dma_start(out[d * P:(d + 1) * P, :], part[d % RING][:]).then_inc(stored[d % RING], 16)
                for q in range(RING):
                    sp.wait_ge(stored[q], 16 * len(range(q, TT, RING)))

            @block.vector
            def _(dve):
                for t in range(TT):
                    q = t % RING
                    dve.wait_ge(part_in[q], 16 * (t // RING + 1))
                    dve.wait_ge(y_in[q], 32 * (t // RING + 1))
                    dve.scalar_tensor_tensor(part[q][:], ya[q][:], T["gate"][:, 0, t:t + 1], part[q][:], ALU.mult, ALU.add).then_inc(half_done, 1)
                    dve.wait_ge(half_done, t + 1)
                    dve.scalar_tensor_tensor(part[q][:], yb[q][:], T["gate"][:, 1, t:t + 1], part[q][:], ALU.mult, ALU.add).then_inc(done, 1)


def early_fusion_block(nc, x, txt, tok_W, Wq, bq, Wk, bk, Wv, bv, Wo, bo, g_shared, W1_s, b1_s, W2_s, b2_s,
                       g_routed, W1_r, b1_r, W2_r, b2_r, centroids, out):
    A = {"Wq": Wq, "Wk": Wk, "Wv": Wv, "Wo": Wo, "bq": bq, "bk": bk, "bv": bv, "bo": bo, "centroids": centroids,
         "g_s": g_shared, "W1_s": W1_s, "b1_s": b1_s, "W2_s": W2_s, "b2_s": b2_s,
         "g_r": g_routed, "W1_r": W1_r, "b1_r": b1_r, "W2_r": W2_r, "b2_r": b2_r}
    with ExitStack() as ctx:
        sb = lambda n, s, d=F32: ctx.enter_context(nc.sbuf_tensor(n, s, d))
        rows = lambda n, count: nc.dram_tensor(n, [count, D], F32, kind="Internal").ap()
        T = {
            "ident": sb("ident", [P, P]),
            "slot": sb("slot", [P, TOP, TT], I32), "gate": sb("gate", [P, TOP, TT]),
            "tile_expert": sb("tile_expert", [P, NT], I32),
            "scale_s": sb("scale_s", [P, 5]), "scale_r": sb("scale_r", [P, 5]),
            "b1_s": sb("b1T_s", [P, SHARED * HJ]), "b1_r": sb("b1T_r", [P, EXPERTS * HJ]),
            "patch_h": rows("patch_h", BATCH * NPATCH), "h2": rows("h2_rows", TOKENS),
            "xn": rows("xn_rows", (GROUPS + 1) * TILE), "base": rows("base_rows", (GROUPS + 1) * TILE),
            "part": rows("part_rows", GROUPS * TILE),
            "xg": rows("slot_rows", (NT + 1) * TILE), "y": rows("y_rows", NT * TILE),
        }
        patches = nc.dram_tensor("patches", [BATCH * CHANNELS, IMAGE * IMAGE], F32, kind="Internal").ap()
        ident_done = ctx.enter_context(nc.semaphore("ident_done"))
        with nc.Block() as block:
            @block.gpsimd
            def _(g):
                g.memset(T["ident"][:], 0.0).then_inc(ident_done, 1)
                g.wait_ge(ident_done, 1)
                g.affine_select(out=T["ident"][:], in_=T["ident"][:], compare_op=ALU.not_equal, fill=1.0,
                                base=0, pattern=[[-1, P]], channel_multiplier=1).then_inc(ident_done, 1)
                g.wait_ge(ident_done, 2)
        patch_embed(nc, x, tok_W, patches, T)
        attention(nc, txt, A, T)
        router(nc, A, T)
        w1s, w2s = sb("w1s", [P, SHARED, 2, KD, HID], F16), sb("w2s", [P, SHARED, 2, HJ, D], F16)
        w1r, w2r = sb("w1r", [P, EXPERTS, 2, KD, HID], F16), sb("w2r", [P, EXPERTS, 2, HJ, D], F16)
        shared_weights(nc, A, T, w1s, w2s)
        ffn(nc, A, T, "_s", w1s, w2s, GROUPS, SHARED, False, (w1r, w2r))
        ffn(nc, A, T, "_r", w1r, w2r, NT // 2, 2, True)
        combine(nc, T, out)


_INS = ['x', 'txt', 'L0_tok_W', 'L0_attn_Wq', 'L0_attn_bq', 'L0_attn_Wk', 'L0_attn_bk', 'L0_attn_Wv', 'L0_attn_bv',
        'L0_attn_Wo', 'L0_attn_bo', 'L0_ffn_g_shared', 'L0_ffn_W1_s', 'L0_ffn_b1_s', 'L0_ffn_W2_s', 'L0_ffn_b2_s',
        'L0_ffn_g_routed', 'L0_ffn_W1_r', 'L0_ffn_b1_r', 'L0_ffn_W2_r', 'L0_ffn_b2_r', 'L0_ffn_centroids']


def kernel(**inputs):
    import numpy as _np
    import concourse.bacc as _bacc
    from concourse import mybir as _mybir
    from concourse.bass_utils import run_bass_kernel_spmd as _run

    nc = _bacc.Bacc("TRN2", target_bir_lowering=False, num_devices=1)
    arrays, args = {}, []
    for name in _INS:
        a = _np.ascontiguousarray(inputs[name])
        arrays[f"in_{name}_dram"] = a
        args.append(nc.dram_tensor(f"in_{name}_dram", a.shape, _mybir.dt.from_np(a.dtype), kind="ExternalInput").ap())
    args.append(nc.dram_tensor("out_0_dram", (TOKENS, D), _mybir.dt.float32, kind="ExternalOutput").ap())
    early_fusion_block(nc, *args)
    r = _run(nc, [arrays], core_ids=[0])
    return _np.asarray(r.results[0]["out_0_dram"]).reshape(BATCH, SEQ, D)
```

```python
import concourse.bass as bass
from concourse import mybir
from contextlib import ExitStack

F32 = mybir.dt.float32
F16 = mybir.dt.float16
BF16 = mybir.dt.bfloat16
I32 = mybir.dt.int32
ACT = mybir.ActivationFunctionType
ALU = mybir.AluOpType
AX = mybir.AxisListType.X

P = 128
BATCH, CHANNELS, IMAGE, PATCH = 32, 3, 96, 16
GRID = IMAGE // PATCH
NPATCH = GRID * GRID
FLAT = CHANNELS * PATCH * PATCH
TEXT = 128
SEQ = NPATCH + TEXT
D = 256
KD = D // P
HEADS, HD = 16, 16
HG = P // HD
TOKENS = BATCH * SEQ
TT = TOKENS // P
LN_EPS = 1e-5
MASK = -1.0e30
XA_SCALE, QKV_SCALE, WO_SCALE, E_SCALE = 2.0 ** 5, 2.0 ** 14, 2.0 ** 13, 2.0 ** 14


def reached(value, n):
    return not isinstance(value, int) or value >= n


def patch_embed(nc, x, W, patches, T):
    NT = BATCH * NPATCH // P
    PER = 3
    with ExitStack() as ctx:
        sb = lambda n, s, d=F32: ctx.enter_context(nc.sbuf_tensor(n, s, d))
        sem = lambda n: ctx.enter_context(nc.semaphore(n))
        planes = sb("planes", [BATCH * CHANNELS, IMAGE * IMAGE])
        ordered = sb("ordered", [BATCH * CHANNELS, IMAGE * IMAGE])
        w_sb = sb("tok_w", [P, FLAT // P, D])
        rows = sb("patch_rows", [P, NT, FLAT])
        rowsT = sb("patch_rows_T", [P, PER, FLAT])
        h_out = sb("patch_h_rows", [P, NT, D])
        ps = [ctx.enter_context(nc.psum_tensor(f"pe_ps{i}", [P, 512], F32)) for i in range(8)]
        plane_in = [sem(f"plane_in{i}") for i in range(GRID)]
        w_in, row_in, patches_out = sem("w_in"), sem("row_in"), sem("patches_out")
        reordered_v, reordered_a = sem("reordered_v"), sem("reordered_a")
        t_done, t_copied, mm_done, h_copied, h_stored = (
            sem("t_done"), sem("t_copied"), sem("mm_done"), sem("h_copied"), sem("h_stored"))
        x_v = x.rearrange("b c h w -> (b c) (h w)")
        BAND = PATCH * IMAGE
        src = planes[:].rearrange("p (y i x j) -> p y i j x", y=GRID, i=PATCH, x=GRID)
        dst = ordered[:].rearrange("p (i j y x) -> p y i j x", i=PATCH, j=PATCH, y=GRID)
        with nc.Block() as block:
            @block.sync
            def _(sp):
                for y in range(GRID):
                    sp.dma_start(planes[:, y * BAND:(y + 1) * BAND],
                                 x_v[:, y * BAND:(y + 1) * BAND]).then_inc(plane_in[y], 16)
                sp.dma_start(w_sb[:], W.rearrange("(k p) d -> p k d", p=P)).then_inc(w_in, 16)
                sp.wait_ge(reordered_v, GRID // 2)
                sp.wait_ge(reordered_a, GRID // 2)
                sp.dma_start(patches, ordered[:]).then_inc(patches_out, 16)
                sp.wait_ge(patches_out, 16)
                sp.dma_start(rows[:], patches.rearrange("a b -> (a b)").rearrange(
                    "(t p f) -> p t f", p=P, f=FLAT)).then_inc(row_in, 16)
                sp.wait_ge(h_copied, NT)
                sp.dma_start(T["patch_h"].rearrange("(t p) d -> p t d", p=P), h_out[:]).then_inc(h_stored, 16)
                sp.wait_ge(h_stored, 16)

            @block.vector
            def _(dve):
                for n, y in enumerate(range(0, GRID, 2)):
                    dve.wait_ge(plane_in[y], 16)
                    dve.tensor_copy(dst[:, y], src[:, y]).then_inc(reordered_v, 1)
                with dve.Fori(0, NT // PER) as r:
                    for u in range(PER):
                        dve.wait_ge(t_done, r * PER + u + 1)
                        dve.tensor_copy(rowsT[:, u, 0:512], ps[2 * u][:, :])
                        dve.tensor_copy(rowsT[:, u, 512:FLAT], ps[2 * u + 1][:, 0:FLAT - 512]).then_inc(t_copied, 1)

            @block.scalar
            def _(act):
                for n, y in enumerate(range(1, GRID, 2)):
                    act.wait_ge(plane_in[y], 16)
                    act.activation(dst[:, y], src[:, y], ACT.Copy).then_inc(reordered_a, 1)
                with act.Fori(0, NT // PER) as r:
                    for u in range(PER):
                        act.wait_ge(mm_done, r * PER + u + 1)
                        act.activation(h_out[:, bass.ds(r * PER + u, 1), :].rearrange("p a d -> p (a d)"),
                                       ps[6 + u % 2][:, 0:D], ACT.Copy).then_inc(h_copied, 1)

            @block.tensor
            def _(pe):
                pe.wait_ge(row_in, 16)
                pe.wait_ge(w_in, 16)
                for r in range(NT // PER):
                    for u in range(PER):
                        for k in range(FLAT // P):
                            o = ps[2 * u + k // 4][:, (k % 4) * P:(k % 4 + 1) * P]
                            if k == 0 and r:
                                pe.wait_ge(t_copied, (r - 1) * PER + u + 1)
                            mm = pe.transpose(o, rows[:, r * PER + u, k * P:(k + 1) * P], T["ident"][:])
                        mm.then_inc(t_done, 1)
                    for u in range(PER):
                        n = r * PER + u
                        pe.wait_ge(t_copied, n + 1)
                        if n >= 2:
                            pe.wait_ge(h_copied, n if u == 0 else n - 1)
                        for k in range(FLAT // P):
                            mm = pe.matmul(ps[6 + u % 2][:, 0:D], rowsT[:, u, k * P:(k + 1) * P], w_sb[:, k, :],
                                           start=k == 0, stop=k == FLAT // P - 1)
                        mm.then_inc(mm_done, 1)


def moments_of(dve, stats, mean, squares, gap, sem, count):
    dve.tensor_tensor(gap[:], stats[:, :, 1], stats[:, :, 4], ALU.subtract)
    dve.tensor_tensor(mean[:], stats[:, :, 1], stats[:, :, 4], ALU.add)
    dve.tensor_tensor(squares[:], stats[:, :, 2], stats[:, :, 5], ALU.add).then_inc(sem, 1)
    dve.wait_ge(sem, count + 1)
    dve.tensor_tensor(gap[:], gap[:], gap[:], ALU.mult)
    dve.tensor_scalar(mean[:], mean[:], 0.5, None, ALU.mult).then_inc(sem, 1)
    dve.wait_ge(sem, count + 2)
    dve.scalar_tensor_tensor(squares[:], gap[:], D / 4, squares[:], ALU.mult, ALU.add).then_inc(sem, 1)
    dve.wait_ge(sem, count + 3)


def attention(nc, txt, A, T):
    STEPS = 2 * BATCH
    GD = HG * HD
    PAIRS = HG // 2
    HALF = P // 2
    VW = HD + 1
    HI, LO = 0, 1
    with ExitStack() as ctx:
        sb = lambda n, s, d=F32: ctx.enter_context(nc.sbuf_tensor(n, s, d))
        sem = lambda n: ctx.enter_context(nc.semaphore(n))
        NB = BATCH + 2
        h_text = sb("h_text", [P, NB, D])
        h_patch = sb("h_patch", [NPATCH, NB, D])
        stats = sb("ln_stats", [P, 2, NB, 6])
        mean = sb("ln_mean", [P, 2 * NB])
        mean_gap = sb("ln_mean_gap", [P, 2 * NB])
        rstd = sb("ln_rstd", [P, 2 * NB])
        expo = sb("ln_expo", [P, 2 * NB])
        w_in = sb("attn_w_in", [P, 4, KD, D])
        w = sb("attn_w", [P, 4, 2, KD, D], F16)
        b_in = sb("attn_b", [P, 3, KD])
        bo = sb("bo", [P, D])
        big, big_all = sb("attn_big", [P, 7]), sb("attn_big_all", [P, 7])
        power, inv_power = sb("attn_power", [P, 4]), sb("attn_inv_power", [P, 4])
        w_scale, b_scale, back = sb("attn_w_scale", [P, 4]), sb("attn_b_scale", [P, 3]), sb("attn_back", [P, 2])
        head_of = sb("head_of", [P, HG], F16)
        one = sb("attn_one", [P, 2 * KD], F16)
        causal = sb("causal", [P, 4, TEXT], BF16)
        causal_p = sb("causal_p", [NPATCH, HG, NPATCH], BF16)
        identb = sb("identb", [P, P], BF16)
        xn = sb("xn", [P, D])
        xn_p = sb("xn_p", [NPATCH, D])
        x = [sb(f"xT{i}", [P, 2, KD, 2 * P], F16) for i in range(2)]
        qk = [sb(f"qk{i}", [P, 2, 2, SEQ], F16) for i in range(2)]
        kbd = [sb(f"kbd{i}", [P, 2, HG, SEQ], F16) for i in range(2)]
        v_t = [sb(f"v_t{i}", [P, 2, HEADS, VW], F16) for i in range(2)]
        v_p = [sb(f"v_p{i}", [P, 2, HEADS // 2, 2, VW], F16) for i in range(2)]
        e_tt = [sb(f"e_tt{i}", [P, HG, TEXT]) for i in range(2)]
        e_tp = [sb(f"e_tp{i}", [P, HG, HALF]) for i in range(2)]
        e_pp = [sb(f"e_pp{i}", [NPATCH, HG, HALF]) for i in range(2)]
        top, top_b, top_p = sb("top", [P, HG]), sb("top_b", [P, HG]), sb("top_p", [NPATCH, HG])
        eT_tt = sb("eT_tt", [P, 2, HG, P], F16)
        eT_tp = sb("eT_tp", [P, 2, PAIRS, P], F16)
        eT_pp = sb("eT_pp", [P, 2, PAIRS, NPATCH], F16)
        inv, inv_p = sb("inv", [P, HG]), sb("inv_p", [NPATCH, HG])
        o, o_p = sb("attn_o", [P, D]), sb("attn_o_p", [NPATCH, D])
        oT = sb("attn_oT", [P, 2, KD, SEQ], F16)
        hb = [sb(f"hb{i}", [P, D]) for i in range(2)]
        hb_p = [sb(f"hb_p{i}", [NPATCH, D]) for i in range(2)]
        h2 = [sb(f"h2_{i}", [P, D]) for i in range(2)]
        h2_p = [sb(f"h2_p{i}", [NPATCH, D]) for i in range(2)]
        sc = ctx.enter_context(nc.psum_tensor("at_scores", [P, HG, TEXT], F32))
        bank = [ctx.enter_context(nc.psum_tensor(f"at_ps{i}", [P, 512], F32)) for i in range(2, 8)]
        sc_tp, sc_pp, turn, x_ps, v_ps = bank[0], bank[1], [bank[2], bank[3]], bank[4], bank[5]

        names = ("rows_in attn_w_in_s bias_in w_turned w_high w_low bn_done eps_done consts_done selected "
                 "bigs reduced chain xn_ready xt_done x_hi x_lo x_doubled qk_done qk_hi qk_lo kbd_ready v_done v_hi v_lo "
                 "s_done maxed shifted exp_done t_done t_hi t_lo o_done inverted o_ready ot_done ot_hi ot_lo wo_done "
                 "hb_ready h2_ready").split()
        S = {n: sem(n) for n in names}
        h2_stored = [sem(f"h2_stored{i}") for i in range(2)]

        with nc.Block() as block:
            @block.sync
            def _(sp):
                for n, name in enumerate(("Wq", "Wk", "Wv", "Wo")):
                    sp.dma_start(w_in[:, n], A[name].rearrange("(m p) c -> p m c", p=P)).then_inc(S["attn_w_in_s"], 16)
                with nc.allow_non_contiguous_dma(reason="256 biases onto partitions"):
                    for n, name in enumerate(("bq", "bk", "bv")):
                        sp.dma_start(b_in[:, n], A[name].rearrange("(m p) -> p m", p=P)).then_inc(S["bias_in"], 16)
                sp.dma_start(bo[:], A["bo"].partition_broadcast(P)).then_inc(S["bias_in"], 16)
                sp.dma_start(h_text[:, 0:BATCH], txt.rearrange("b p d -> p b d")).then_inc(S["rows_in"], 16)
                sp.dma_start(h_patch[:, 0:BATCH], T["patch_h"].rearrange("(b p) d -> p b d", p=NPATCH)).then_inc(S["rows_in"], 16)

            @block.gpsimd
            def _(g):
                g.memset(stats[:], 1.0)
                g.memset(h_text[:, BATCH:], 0.0)
                g.memset(h_patch[:, BATCH:], 0.0)
                g.memset(causal[:], 0.0)
                g.memset(causal_p[:], 0.0)
                g.memset(head_of[:], 1.0)
                g.memset(one[:], 1.0)
                g.memset(identb[:], 0.0)
                g.memset(expo[:], -0.5)
                for i in range(2):
                    g.memset(x[i][:], 0.0)
                    g.memset(e_tp[i][:], 0.0)
                    g.memset(e_pp[i][:], 0.0)
                    g.memset(v_t[i][:, LO], 0.0)
                    g.memset(v_t[i][:, HI], 1.0)
                    last = g.memset(v_p[i][:], 0.0)
                last.then_inc(S["consts_done"], 1)
                g.wait_ge(S["consts_done"], 1)
                g.affine_select(out=causal[:], in_=causal[:], compare_op=ALU.is_ge, fill=MASK,
                                base=0, pattern=[[0, 4], [-1, TEXT]], channel_multiplier=1)
                g.affine_select(out=causal_p[:], in_=causal_p[:], compare_op=ALU.is_ge, fill=MASK,
                                base=0, pattern=[[0, HG], [-1, NPATCH]], channel_multiplier=1)
                g.affine_select(out=identb[:], in_=identb[:], compare_op=ALU.not_equal, fill=1.0,
                                base=0, pattern=[[-1, P]], channel_multiplier=1)
                g.affine_select(out=head_of[:], in_=head_of[:], compare_op=ALU.is_ge, fill=0.0,
                                base=0, pattern=[[-HD, HG]], channel_multiplier=1).then_inc(S["selected"], 1)
                g.wait_ge(S["selected"], 1)
                g.affine_select(out=head_of[:], in_=head_of[:], compare_op=ALU.is_ge, fill=0.0,
                                base=HD - 1, pattern=[[HD, HG]], channel_multiplier=-1).then_inc(S["selected"], 1)
                g.wait_ge(S["bigs"], 1)
                g.partition_all_reduce(big_all[:], big[:], P, bass.bass_isa.ReduceOp.max).then_inc(S["reduced"], 1)
                g.wait_ge(S["eps_done"], 1)
                g.tensor_tensor(rstd[:], rstd[:], expo[:], ALU.pow)

            @block.vector
            def _(dve):
                n_link = [0]

                def link(ins):
                    ins.then_inc(S["chain"], 1)
                    n_link[0] += 1
                    dve.wait_ge(S["chain"], n_link[0])
                dve.wait_ge(S["attn_w_in_s"], 64)
                dve.wait_ge(S["bias_in"], 64)
                dve.tensor_reduce(big[:, 0:4], w_in[:].rearrange("p n k d -> p n (k d)"), AX, ALU.max, apply_absolute_value=True)
                dve.tensor_reduce(big[:, 4:7], b_in[:], AX, ALU.max, apply_absolute_value=True).then_inc(S["bigs"], 1)
                dve.wait_ge(S["reduced"], 1)
                link(dve.scalar_tensor_tensor(big_all[:, 0:3], big_all[:, 0:3], float(D), big_all[:, 4:7], ALU.mult, ALU.add))
                dve.tensor_scalar(big_all[:, 0:2], big_all[:, 0:2], 1e-5, None, ALU.max)
                link(dve.tensor_scalar(big_all[:, 2:4], big_all[:, 2:4], 1e-15, None, ALU.max))
                link(dve.tensor_scalar(power[:].bitcast(I32), big_all[:, 0:4].bitcast(I32), 0x7F800000, None, ALU.bitwise_and))
                link(dve.reciprocal(inv_power[:], power[:]))
                dve.tensor_scalar(w_scale[:, 0:3], inv_power[:, 0:3], QKV_SCALE / XA_SCALE, None, ALU.mult)
                dve.tensor_scalar(w_scale[:, 3:4], inv_power[:, 3:4], WO_SCALE, None, ALU.mult)
                dve.tensor_scalar(b_scale[:], inv_power[:, 0:3], QKV_SCALE, None, ALU.mult)
                dve.scalar_tensor_tensor(back[:, 0:1], power[:, 0:1], HD ** -0.5 / QKV_SCALE ** 2, power[:, 1:2], ALU.mult, ALU.mult)
                link(dve.scalar_tensor_tensor(back[:, 1:2], power[:, 2:3], 1 / (QKV_SCALE * WO_SCALE), power[:, 3:4], ALU.mult, ALU.mult))
                link(dve.tensor_tensor(b_in[:], b_in[:], b_scale[:].unsqueeze(2).to_broadcast([P, 3, KD]), ALU.mult))
                dve.wait_ge(S["consts_done"], 1)
                for i in range(2):
                    for n in range(2):
                        dve.memset(v_p[i][n * HALF:(n + 1) * HALF, HI, :, n, HD:VW], 1.0)
                dve.wait_ge(S["rows_in"], 32)
                with dve.Fori(0, NB) as b:
                    row = lambda t: t[:, bass.ds(b, 1), :].rearrange("p a d -> p (a d)")
                    dve.bn_stats(row(stats[:, 0]), row(h_text)).then_inc(S["bn_done"], 1)
                    dve.bn_stats(row(stats[0:NPATCH, 1]), row(h_patch)).then_inc(S["bn_done"], 1)
                dve.wait_ge(S["bn_done"], 2 * NB)
                moments_of(dve, stats[:].rearrange("p r b s -> p (r b) s"), mean, rstd, mean_gap, S["bn_done"], 2 * NB)
                dve.tensor_scalar(rstd[:], rstd[:], 1.0 / D, LN_EPS, ALU.mult, ALU.add).then_inc(S["eps_done"], 1)
                for n in range(4):
                    dve.wait_ge(S["w_high"], n + 1)
                    flat = lambda part: w[:, n, part].rearrange("p k d -> p (k d)")
                    dve.scalar_tensor_tensor(flat(LO), bank[n][:], w_scale[:, n:n + 1], flat(HI), ALU.mult, ALU.subtract).then_inc(S["w_low"], 1)

            @block.scalar
            def _(act):
                act.wait_ge(S["chain"], 6)
                for n in range(4):
                    act.wait_ge(S["w_turned"], n + 1)
                    act.activation(w[:, n, HI].rearrange("p k d -> p (k d)"), bank[n][:, :], ACT.Copy, scale=w_scale[:, n:n + 1]).then_inc(S["w_high"], 1)

            @block.tensor
            def _(pe):
                pe.wait_ge(S["attn_w_in_s"], 64)
                for n in range(4):
                    for k in range(KD):
                        for m in range(KD):
                            mm = pe.transpose(bank[n][:, k * D + m * P:k * D + (m + 1) * P],
                                              w_in[:, n, m, k * P:(k + 1) * P], T["ident"][:])
                    mm.then_inc(S["w_turned"], 1)

        WQ, WK, WV, WO = range(4)
        PASSES = ((HI, HI), (HI, LO), (LO, HI))
        TXT, PAT = slice(0, TEXT), slice(TEXT, SEQ)
        ROUNDS = 4
        QUADS = (slice(0, 4), slice(4, 8))

        def run(eng, step, tail):
            for i in range(2):
                for u in range(4):
                    step(4 * i + u, 2 * i + u // 2, u, i)
            with eng.Fori(2, STEPS // 4) as i:
                for u in range(4):
                    step(4 * i + u, 2 * i + u // 2, u, i)
            for u in range(3):
                tail(STEPS + u, BATCH + u // 2, u)

        def exponents(q):
            return (e_tt[q][:].rearrange("p h k -> p (h k)"), e_tp[q][:, :, 0:NPATCH], e_pp[q][:, :, 0:NPATCH])

        def turned(part, n):
            if n < 2:
                return eT_tt[:, part, 4 * n:4 * n + 4, :].rearrange("p h q -> p (h q)"), turn[n][:]
            if n == 2:
                return eT_tp[:, part].rearrange("p j q -> p (j q)"), turn[0][:]
            return eT_pp[:, part].rearrange("p j q -> p (j q)"), turn[1][:, 0:PAIRS * NPATCH]

        def values_of(part, par):
            both = [(v_t[par][:, part, :, 0:HD], v_ps[:, 0:D].rearrange("p (h c) -> p h c", h=HEADS))]
            for n in range(2):
                rows = slice(n * HALF, (n + 1) * HALF)
                src = v_ps[rows, D:2 * D].rearrange("p (j h c) -> p j h c", h=2, c=HD)
                both.append((v_p[par][rows, part, :, n, 0:HD], src[:, :, n, :]))
            return both

        with nc.Block() as block:
            @block.tensor
            def _(pe):
                def product(out, left, right, first=True, last=True):
                    for n, (a, c) in enumerate(PASSES):
                        mm = pe.matmul(out, left(a), right(c), start=first and n == 0, stop=last and n == 2)
                    return mm

                def turn_xn(b):
                    pe.wait_ge(S["xn_ready"], b + 1)
                    for k in range(KD):
                        pe.transpose(x_ps[:, k * SEQ:k * SEQ + TEXT], xn[:, k * P:(k + 1) * P], T["ident"][:])
                        mm = pe.transpose(x_ps[:, k * SEQ + TEXT:(k + 1) * SEQ], xn_p[:, k * P:(k + 1) * P],
                                          T["ident"][0:NPATCH, 0:NPATCH])
                    mm.then_inc(S["xt_done"], 1)

                def queries_keys(par, g):
                    cols = slice(g * GD, (g + 1) * GD)
                    for n, of in enumerate((WQ, WK)):
                        for k in range(KD):
                            mm = product(x_ps[:, n * SEQ:(n + 1) * SEQ], lambda a: w[:, of, a, k, cols],
                                         lambda c: x[par][:, c, k, 0:SEQ], k == 0, k == KD - 1)
                    mm.then_inc(S["qk_done"], 1)

                def values(par):
                    for n in range(2):
                        for k in range(KD):
                            mm = product(v_ps[:, n * D:(n + 1) * D], lambda a: x[par][:, a, k, n * P:(n + 1) * P],
                                         lambda c: w[:, WV, c, k, :], k == 0, k == KD - 1)
                    mm.then_inc(S["v_done"], 1)

                def turn_text(q):
                    for n in range(2):
                        for h in range(4):
                            mm = pe.transpose(turn[n][:, h * TEXT:(h + 1) * TEXT], e_tt[q][:, 4 * n + h, :], T["ident"][:])
                        mm.then_inc(S["t_done"], 1)

                def turn_patches(q):
                    for j in range(PAIRS):
                        mm = pe.transpose(turn[0][:, j * TEXT:(j + 1) * TEXT],
                                          e_tp[q][:, 2 * j:2 * j + 2, :].rearrange("p h k -> p (h k)"), T["ident"][:])
                    mm.then_inc(S["t_done"], 1)
                    for j in range(PAIRS):
                        mm = pe.transpose(turn[1][:, j * NPATCH:(j + 1) * NPATCH],
                                          e_pp[q][:, 2 * j:2 * j + 2, :].rearrange("p h k -> p (h k)"),
                                          T["ident"][0:NPATCH, 0:NPATCH])
                    mm.then_inc(S["t_done"], 1)

                def attend_text(par, g):
                    for h in range(HG):
                        product(v_ps[:, h * VW:(h + 1) * VW], lambda p: eT_tt[:, p, h, :],
                                lambda c: v_t[par][:, c, g * HG + h, :], h == 0, False)

                def attend_patches(par, g):
                    for rows, turned, at in ((slice(0, NPATCH), eT_pp, HG * VW), (slice(0, P), eT_tp, 0)):
                        for j in range(PAIRS):
                            pair = v_ps[rows, at + 2 * j * VW:at + 2 * (j + 1) * VW]
                            mm = product(pair, lambda p: turned[:, p, j, :],
                                         lambda c: v_p[par][:, c, g * PAIRS + j].rearrange("p h c -> p (h c)"),
                                         False, at == 0 and j == PAIRS - 1)
                    mm.then_inc(S["o_done"], 1)

                def turn_o():
                    for k in range(KD):
                        pe.transpose(v_ps[:, k * SEQ:k * SEQ + TEXT], o[:, k * P:(k + 1) * P], T["ident"][:])
                        mm = pe.transpose(v_ps[:, k * SEQ + TEXT:(k + 1) * SEQ], o_p[:, k * P:(k + 1) * P],
                                          T["ident"][0:NPATCH, 0:NPATCH])
                    mm.then_inc(S["ot_done"], 1)

                def out_project():
                    for rows, out in ((TXT, v_ps[:, 0:D]), (PAT, v_ps[0:NPATCH, D:2 * D])):
                        for k in range(KD):
                            mm = product(out, lambda a: oT[:, a, k, rows], lambda c: w[:, WO, c, k, :], k == 0, k == KD - 1)
                    mm.then_inc(S["wo_done"], 1)

                def scores(s, u):
                    q = u % 2
                    pe.wait_ge(S["kbd_ready"], s + 1)
                    if reached(s, 1):
                        pe.wait_ge(S["shifted"], s)
                    product(sc_tp[:, 0:HG * NPATCH], lambda a: qk[q][:, 0, a, TXT], lambda c: kbd[q][:, c, :, PAT])
                    out = sc_pp[0:NPATCH, 0:HG * NPATCH]
                    pe.matmul(out, identb[0:NPATCH, 0:NPATCH], causal_p[:].rearrange("p h k -> p (h k)"), start=True, stop=False)
                    product(out, lambda a: qk[q][:, 0, a, PAT], lambda c: kbd[q][:, c, :, PAT], False).then_inc(S["s_done"], 1)
                    for heads in QUADS:
                        pe.matmul(sc[:, heads, :], identb[:], causal[:], start=True, stop=False)
                        product(sc[:, heads, :], lambda a: qk[q][:, 0, a, TXT], lambda c: kbd[q][:, c, heads, TXT], False).then_inc(S["s_done"], 1)

                def step(s, b, u, i, live=True):
                    g, a, q = u % 2, s - 2, u % 2
                    lagged = reached(s, 2) and not (isinstance(s, int) and s >= STEPS + 2)
                    if lagged:
                        pe.wait_ge(S["exp_done"], a + 1)
                        turn_text(q)
                    if reached(s, 3):
                        pe.wait_ge(S["o_ready"], s - 2)
                    if g == 0 and reached(b, 2):
                        turn_o()
                    if g == 1 and live:
                        pe.wait_ge(S["x_doubled"], b + 1)
                        values((u // 2) % 2)
                    if live:
                        pe.wait_ge(S["x_lo"], b + 1 + g)
                        pe.wait_ge(S["qk_lo"], s + 1)
                        queries_keys((u + 1) // 2 % 2, (u + 1) % 2)
                        scores(s, u)
                    if g == 0 and reached(b, 2):
                        pe.wait_ge(S["ot_lo"], b - 1)
                        out_project()
                    if lagged:
                        pe.wait_ge(S["t_lo"], ROUNDS * a + 2)
                        turn_patches(q)
                        if g == 0:
                            pe.wait_ge(S["v_lo"], b)
                            if reached(b, 2):
                                pe.wait_ge(S["h2_ready"], b - 1)
                        elif live:
                            pe.wait_ge(S["v_lo"], b + 1)
                        attend_text((u // 2 + 1) % 2, g)
                    if g == 0 and live:
                        pe.wait_ge(S["qk_lo"], s + 2)
                        turn_xn(b + 1)
                    if lagged:
                        pe.wait_ge(S["t_lo"], ROUNDS * a + 4)
                        attend_patches((u // 2 + 1) % 2, g)

                turn_xn(0)
                pe.wait_ge(S["x_lo"], 1)
                queries_keys(0, 0)
                run(pe, step, lambda s, b, u: step(s, b, u, 0, False))

            @block.scalar
            def _(act):
                def turned_high(a, n):
                    act.wait_ge(S["t_done"], ROUNDS * a + n + 1)
                    to, src = turned(HI, n)
                    act.activation(to, src, ACT.Copy, scale=E_SCALE).then_inc(S["t_hi"], 1)

                def x_high(b, par):
                    act.wait_ge(S["xt_done"], b + 1)
                    act.activation(x[par][:, HI, :, 0:SEQ], x_ps[:, 0:KD * SEQ].rearrange("p (k c) -> p k c", k=KD),
                                   ACT.Copy, scale=XA_SCALE).then_inc(S["x_hi"], 1)

                def qk_high(s, q):
                    act.wait_ge(S["qk_done"], s + 1)
                    for n in range(2):
                        last = act.activation(qk[q][:, n, HI, :], x_ps[:, n * SEQ:(n + 1) * SEQ], ACT.Identity, bias=b_in[:, n, q:q + 1])
                    last.then_inc(S["qk_hi"], 1)

                def step(s, b, u, i, live=True):
                    g, a = u % 2, s - 2
                    lagged = reached(s, 2) and not (isinstance(s, int) and s >= STEPS + 2)
                    if lagged:
                        turned_high(a, 0)
                        turned_high(a, 1)
                    if g == 0 and reached(b, 2):
                        act.wait_ge(S["ot_done"], b - 1)
                        for k in range(KD):
                            last = act.activation(oT[:, HI, k], v_ps[:, k * SEQ:(k + 1) * SEQ], ACT.Identity, bias=b_in[:, 2, k:k + 1])
                        last.then_inc(S["ot_hi"], 1)
                    if g == 1 and live:
                        act.wait_ge(S["v_done"], b + 1)
                        for to, src in values_of(HI, u // 2 % 2):
                            last = act.activation(to, src, ACT.Copy)
                        last.then_inc(S["v_hi"], 1)
                    if live:
                        qk_high(s + 1, (u + 1) % 2)
                    if reached(s, 1) and (live or u == 0):
                        act.wait_ge(S["shifted"], s)
                        for t in exponents((u + 1) % 2):
                            last = act.activation(t, t, ACT.Exp, scale=back[0:t.shape[0], 0:1])
                        last.then_inc(S["exp_done"], 1)
                    if lagged:
                        turned_high(a, 2)
                        turned_high(a, 3)
                    if g == 0 and live:
                        x_high(b + 1, (u // 2 + 1) % 2)

                x_high(0, 0)
                qk_high(0, 0)
                run(act, step, lambda s, b, u: step(s, b, u, 0, False))

            @block.gpsimd
            def _(g):
                def blocks(s, q):
                    g.wait_ge(S["qk_lo"], s + 1)
                    for part in (HI, LO):
                        last = g.tensor_tensor(kbd[q][:, part], qk[q][:, 1, part].unsqueeze(1).to_broadcast([P, HG, SEQ]),
                                               head_of[:].unsqueeze(2).to_broadcast([P, HG, SEQ]), ALU.mult)
                    last.then_inc(S["kbd_ready"], 1)

                def doubled(b, par):
                    g.wait_ge(S["x_lo"], b + 1)
                    t = x[par][:].rearrange("p a k c -> p (a k) c")
                    g.tensor_tensor(t[:, :, P + HALF:P + HALF + NPATCH], t[:, :, PAT],
                                    one[:].unsqueeze(2).to_broadcast([P, 2 * KD, NPATCH]), ALU.mult).then_inc(S["x_doubled"], 1)

                def step(s, b, u, i):
                    blocks(s + 1, (u + 1) % 2)
                    if u % 2 == 0:
                        doubled(b + 1, (u // 2 + 1) % 2)
                    else:
                        if reached(b, 2):
                            g.wait_ge(S["h2_ready"], b - 1)
                        row = lambda t: t[:, bass.ds(b, 1), :].rearrange("p a d -> p (a d)")
                        g.tensor_tensor(hb[u // 2][:], row(h_text), bo[:], ALU.add)
                        g.tensor_tensor(hb_p[u // 2][:], row(h_patch), bo[0:NPATCH], ALU.add).then_inc(S["hb_ready"], 1)

                doubled(0, 0)
                blocks(0, 0)
                run(g, step, lambda s, b, u: None)

            @block.vector
            def _(dve):
                def normed(b):
                    row = lambda t: t[:, bass.ds(b, 1), :].rearrange("p a d -> p (a d)")
                    for out, src, col, n in ((xn, h_text, b, P), (xn_p, h_patch, NB + b, NPATCH)):
                        last = dve.tensor_scalar(out[:], row(src), mean[0:n, bass.ds(col, 1)], rstd[0:n, bass.ds(col, 1)], ALU.subtract, ALU.mult)
                    last.then_inc(S["xn_ready"], 1)

                def low(to, src, high, factor=None, bias=None):
                    if bias is not None:
                        return dve.scalar_tensor_tensor(to, src, bias, high, ALU.add, ALU.subtract)
                    return dve.scalar_tensor_tensor(to, src, factor, high, ALU.mult, ALU.subtract)

                def turned_low(a, n):
                    dve.wait_ge(S["t_hi"], ROUNDS * a + n + 1)
                    (to, src), (high, _) = turned(LO, n), turned(HI, n)
                    low(to, src, high, E_SCALE).then_inc(S["t_lo"], 1)

                def x_low(b, par):
                    dve.wait_ge(S["x_hi"], b + 1)
                    low(x[par][:, LO, :, 0:SEQ], x_ps[:, 0:KD * SEQ].rearrange("p (k c) -> p k c", k=KD),
                        x[par][:, HI, :, 0:SEQ], XA_SCALE).then_inc(S["x_lo"], 1)

                def qk_low(s, q):
                    dve.wait_ge(S["qk_hi"], s + 1)
                    for n in range(2):
                        last = low(qk[q][:, n, LO, :], x_ps[:, n * SEQ:(n + 1) * SEQ], qk[q][:, n, HI, :], bias=b_in[:, n, q:q + 1])
                    last.then_inc(S["qk_lo"], 1)

                tp = sc_tp[:, 0:HG * NPATCH].rearrange("p (h k) -> p h k", h=HG)
                pp = sc_pp[0:NPATCH, 0:HG * NPATCH].rearrange("p (h k) -> p h k", h=HG)

                def largest(s):
                    dve.wait_ge(S["s_done"], 3 * s + 1)
                    dve.tensor_reduce(top_b[:], tp, AX, ALU.max)
                    dve.tensor_reduce(top_p[:], pp, AX, ALU.max)
                    for n, heads in enumerate(QUADS):
                        dve.wait_ge(S["s_done"], 3 * s + 2 + n)
                        last = dve.tensor_reduce(top[:, heads], sc[:, heads, :], AX, ALU.max)
                    last.then_inc(S["maxed"], 1)
                    dve.wait_ge(S["maxed"], 2 * s + 1)
                    dve.tensor_tensor(top[:], top[:], top_b[:], ALU.max).then_inc(S["maxed"], 1)

                def shift(s, q):
                    dve.wait_ge(S["maxed"], 2 * s + 2)
                    dve.tensor_tensor(e_tt[q][:], sc[:], top[:].unsqueeze(2).to_broadcast([P, HG, TEXT]), ALU.subtract)
                    dve.tensor_tensor(e_tp[q][:, :, 0:NPATCH], tp, top[:].unsqueeze(2).to_broadcast([P, HG, NPATCH]), ALU.subtract)
                    dve.tensor_tensor(e_pp[q][:, :, 0:NPATCH], pp, top_p[:].unsqueeze(2).to_broadcast([NPATCH, HG, NPATCH]),
                                      ALU.subtract).then_inc(S["shifted"], 1)

                def divide(a, g):
                    dve.wait_ge(S["o_done"], a + 1)
                    sets = ((o, inv, v_ps[:, 0:HG * VW], P), (o_p, inv_p, v_ps[0:NPATCH, HG * VW:2 * HG * VW], NPATCH))
                    for _, r, src, n in sets:
                        last = dve.reciprocal(r[:], src.rearrange("p (h c) -> p h c", c=VW)[:, :, HD])
                    last.then_inc(S["inverted"], 1)
                    dve.wait_ge(S["inverted"], a + 1)
                    for out, r, src, n in sets:
                        last = dve.tensor_tensor(out[:, g * GD:(g + 1) * GD].rearrange("p (h c) -> p h c", h=HG),
                                                 src.rearrange("p (h c) -> p h c", c=VW)[:, :, 0:HD],
                                                 r[:].unsqueeze(2).to_broadcast([n, HG, HD]), ALU.mult)
                    last.then_inc(S["o_ready"], 1)

                def residual(b, par, old):
                    dve.wait_ge(S["wo_done"], b + 1)
                    dve.wait_ge(S["hb_ready"], b + 1)
                    if reached(old, 1):
                        dve.wait_ge(h2_stored[par], 32 * old)
                    dve.scalar_tensor_tensor(h2[par][:], v_ps[:, 0:D], back[:, 1:2], hb[par][:], ALU.mult, ALU.add)
                    dve.scalar_tensor_tensor(h2_p[par][:], v_ps[0:NPATCH, D:2 * D], back[0:NPATCH, 1:2], hb_p[par][:],
                                             ALU.mult, ALU.add).then_inc(S["h2_ready"], 1)

                def step(s, b, u, i, live=True):
                    g, a = u % 2, s - 2
                    lagged = reached(s, 2) and not (isinstance(s, int) and s >= STEPS + 2)
                    if reached(s, 3):
                        divide(s - 3, (u + 1) % 2)
                    if reached(s, 1) and (live or u == 0):
                        shift(s - 1, (u + 1) % 2)
                    if lagged:
                        turned_low(a, 0)
                        turned_low(a, 1)
                    if g == 0 and reached(b, 2):
                        dve.wait_ge(S["ot_hi"], b - 1)
                        for k in range(KD):
                            last = low(oT[:, LO, k], v_ps[:, k * SEQ:(k + 1) * SEQ], oT[:, HI, k], bias=b_in[:, 2, k:k + 1])
                        last.then_inc(S["ot_lo"], 1)
                    if g == 1 and live:
                        dve.wait_ge(S["v_hi"], b + 1)
                        for (to, src), (high, _) in zip(values_of(LO, u // 2 % 2), values_of(HI, u // 2 % 2)):
                            last = dve.tensor_tensor(to, src, high, ALU.subtract)
                        last.then_inc(S["v_lo"], 1)
                    if live:
                        qk_low(s + 1, (u + 1) % 2)
                        largest(s)
                    if g == 0 and reached(b, 2):
                        residual(b - 2, u // 2 % 2, i - 1)
                    if lagged:
                        turned_low(a, 2)
                        turned_low(a, 3)
                    if g == 0 and live:
                        x_low(b + 1, (u // 2 + 1) % 2)
                    if g == 1 and live:
                        dve.wait_ge(S["xt_done"], b + 2)
                        normed(b + 2)

                normed(0)
                x_low(0, 0)
                dve.wait_ge(S["xt_done"], 1)
                normed(1)
                qk_low(0, 0)
                run(dve, step, lambda s, b, u: step(s, b, u, BATCH // 2, False))

            @block.sync
            def _(sp):
                with sp.Fori(0, BATCH // 2) as i:
                    for par in range(2):
                        b = 2 * i + par
                        sp.wait_ge(S["h2_ready"], b + 1)
                        sp.dma_start(T["h2"][bass.ds(b * SEQ + NPATCH, TEXT), :], h2[par][:]).then_inc(h2_stored[par], 16)
                        sp.dma_start(T["h2"][bass.ds(b * SEQ, NPATCH), :], h2_p[par][:]).then_inc(h2_stored[par], 16)
                for par in range(2):
                    sp.wait_ge(h2_stored[par], 16 * BATCH)



EXPERTS, SHARED, TOP = 8, 2, 2
HID = 1024
HJ = HID // P
TILE = 256
BLK = TILE // P
NT = (TOP * TOKENS + EXPERTS * (TILE - 1)) // TILE
GROUPS = -(-TOKENS // TILE)
RMS_EPS = 1.1920929e-07
X_SCALE = 1024.0


def router(nc, A, T):
    with ExitStack() as ctx:
        sb = lambda n, s, d=F32: ctx.enter_context(nc.sbuf_tensor(n, s, d))
        h2 = sb("r_h2", [P, TT, D])
        stats = sb("r_stats", [P, TT, 6])
        mean, var, gap, ms = (sb(f"r_{n}", [P, TT]) for n in ("mean", "var", "gap", "ms"))
        a, r, inv_r, ar, opa, nma = (sb(f"r_{n}", [P, TT]) for n in ("a", "r", "inv_r", "ar", "opa", "nma"))
        minus_half, half = sb("r_minus_half", [P, TT]), sb("r_half", [P, TT])
        xr = [sb(f"r_xn{i}", [P, D]) for i in range(2)]
        xT = [sb(f"r_xT{i}", [P, KD, P]) for i in range(2)]
        cent = sb("r_cent", [P, KD, EXPERTS])
        b2s = sb("r_b2s", [P, SHARED, D])
        zeros = sb("r_zeros", [P, 2048])
        score = sb("r_score", [P, TT, EXPERTS])
        lower = sb("r_lower", [P, EXPERTS, EXPERTS])
        above = sb("r_above", [P, TT, EXPERTS, EXPERTS])
        equal = sb("r_equal", [P, TT, EXPERTS, EXPERTS])
        rank, sel, gate, pos, cnt, run_a, run_b, slot, pick = (
            sb(f"r_{n}", [P, TT, EXPERTS]) for n in ("rank", "sel", "gate", "pos", "cnt", "run_a", "run_b", "slot", "pick"))
        total, inv_total, both = (sb(f"r_{n}", [P, TT]) for n in ("total", "inv_total", "both"))
        slot_f = sb("r_slot_f", [P, 2, TT])
        before, ones = sb("r_before", [P, P]), sb("r_ones", [P, P])
        padded_i = sb("r_padded_i", [P, EXPERTS], I32)
        padded, base_a, base_b = (sb(f"r_{n}", [P, EXPERTS]) for n in ("padded", "base_a", "base_b"))
        start_i, start = sb("r_start_i", [P, NT], I32), sb("r_start", [P, NT])
        passed, tile_e = sb("r_passed", [P, NT, EXPERTS - 1]), sb("r_tile_e", [P, NT])
        ps = [ctx.enter_context(nc.psum_tensor(f"r_ps{i}", [P, 512], F32)) for i in range(6)]
        names = ("h2_in_base h2_in small_in consts bn_done moments eps_done root_done root_used xn_ready turned xT_ready "
                 "logits_done scored chain sel_ready counted base_ready base_stored zeroed consts_b").split()
        S = {n: ctx.enter_context(nc.semaphore(n)) for n in names}
        xn_stored = [ctx.enter_context(nc.semaphore(f"xn_stored{i}")) for i in range(2)]

        def run(step):
            for u in range(2):
                step(u, u, 0)
            return step

        with nc.Block() as block:
            @block.sync
            def _(sp):
                sp.dma_start(h2[:], T["h2"].rearrange("(t p) d -> p t d", p=P)).then_inc(S["h2_in"], 16)
                sp.dma_start(cent[:], A["centroids"].rearrange("(k p) e -> p k e", p=P)).then_inc(S["small_in"], 16)
                sp.dma_start(b2s[:].rearrange("p s d -> p (s d)"), A["b2_s"].rearrange("s d -> (s d)").partition_broadcast(P)).then_inc(S["small_in"], 16)
                sp.wait_ge(S["consts"], 1)
                zrows = P * 2048 // D
                for n in range(-(-(NT + 1) * TILE // zrows)):
                    lo, hi = n * zrows, min((n + 1) * zrows, (NT + 1) * TILE)
                    sp.dma_start(T["xg"][lo:hi].rearrange("(p q) d -> p (q d)", p=P), zeros[:, 0:(hi - lo) * D // P]).then_inc(S["zeroed"], 16)
                rest = T["xn"][TOKENS:, :]
                sp.dma_start(rest.rearrange("(p q) d -> p (q d)", p=P), zeros[:, 0:rest.shape[0] * D // P]).then_inc(S["zeroed"], 16)
                rest = T["base"][TOKENS:, :]
                sp.dma_start(rest.rearrange("(p q) d -> p (q d)", p=P), zeros[:, 0:rest.shape[0] * D // P]).then_inc(S["zeroed"], 16)
                zs = (-(-(NT + 1) * TILE // zrows) + 2) * 16

                def store(t, u):
                    sp.wait_ge(S["xn_ready"], t + 1)
                    sp.dma_start(T["xn"][bass.ds(t * P, P), :], xr[u][:]).then_inc(xn_stored[u], 16)
                with sp.Fori(0, TT // 2) as i:
                    for u in range(2):
                        store(2 * i + u, u)
                store(TT - 1, 0)
                sp.wait_ge(S["base_ready"], 1)
                sp.dma_start(T["base"][0:TOKENS].rearrange("(t p) d -> p t d", p=P), h2[:]).then_inc(S["base_stored"], 16)
                sp.wait_ge(S["base_stored"], 16)
                sp.wait_ge(S["zeroed"], zs)
                sp.wait_ge(xn_stored[0], 16 * (TT // 2 + 1))
                sp.wait_ge(xn_stored[1], 16 * (TT // 2))

            @block.gpsimd
            def _(g):
                g.memset(zeros[:], 0.0).then_inc(S["consts"], 1)
                g.memset(minus_half[:], -0.5)
                g.memset(half[:], 0.5)
                g.memset(lower[:], 1.0)
                g.memset(before[:], 1.0)
                g.memset(ones[:], 1.0)
                g.iota(start_i[:], pattern=[[TILE, NT]], base=0, channel_multiplier=0).then_inc(S["consts"], 1)
                g.wait_ge(S["consts"], 2)
                g.affine_select(out=lower[:], in_=lower[:], compare_op=ALU.is_gt, fill=0.0, base=0,
                                pattern=[[1, EXPERTS], [-1, EXPERTS]], channel_multiplier=0)
                g.affine_select(out=before[:], in_=before[:], compare_op=ALU.is_gt, fill=0.0, base=0,
                                pattern=[[1, P]], channel_multiplier=-1)
                g.tensor_copy(start[:], start_i[:]).then_inc(S["consts_b"], 1)
                g.wait_ge(S["eps_done"], 1)
                g.tensor_tensor(a[:], var[:], minus_half[:], ALU.pow).then_inc(S["root_done"], 1)
                g.wait_ge(S["eps_done"], 2)
                g.tensor_tensor(r[:], ms[:], minus_half[:], ALU.pow)
                g.tensor_tensor(inv_r[:], ms[:], half[:], ALU.pow).then_inc(S["root_done"], 1)
                g.wait_ge(S["eps_done"], 3)
                g.wait_ge(S["small_in"], 32)
                g.tensor_tensor(b2s[:, 0], b2s[:, 0], b2s[:, 1], ALU.add).then_inc(S["consts_b"], 1)
                g.wait_ge(S["h2_in_base"], TT)
                g.wait_ge(S["consts_b"], 2)
                g.tensor_tensor(h2[:], h2[:], b2s[:, 0].unsqueeze(1).to_broadcast([P, TT, D]), ALU.add).then_inc(S["base_ready"], 1)

            @block.tensor
            def _(pe):
                pe.wait_ge(S["small_in"], 32)

                def tile(t, u, n):
                    pe.wait_ge(S["xn_ready"], t + 1)
                    if n >= 2:
                        pe.wait_ge(S["xT_ready"], t - 1)
                    for k in range(KD):
                        mm = pe.transpose(ps[u][:, k * P:(k + 1) * P], xr[u][:, k * P:(k + 1) * P], T["ident"][:])
                    mm.then_inc(S["turned"], 1)
                    pe.wait_ge(S["xT_ready"], t + 1)
                    if n >= 2:
                        pe.wait_ge(S["scored"], t - 1)
                    for k in range(KD):
                        mm = pe.matmul(ps[2 + u][:, 0:EXPERTS], xT[u][:, k, :], cent[:, k, :], start=k == 0, stop=k == KD - 1)
                    mm.then_inc(S["logits_done"], 1)
                for u in range(2):
                    tile(u, u, u)
                with pe.Fori(1, TT // 2) as i:
                    for u in range(2):
                        tile(2 * i + u, u, 2)
                tile(TT - 1, 0, 2)
                pe.wait_ge(S["sel_ready"], 1)
                pe.wait_ge(S["consts_b"], 1)
                flat = sel[:].rearrange("p t e -> p (t e)")
                pe.matmul(ps[4][:, 0:TT * EXPERTS], before[:], flat, start=True, stop=True)
                pe.matmul(ps[5][:, 0:TT * EXPERTS], ones[:], flat, start=True, stop=True).then_inc(S["counted"], 1)

            @block.scalar
            def _(act):
                def tile(t, u, n):
                    act.wait_ge(S["turned"], t + 1)
                    act.activation(xT[u][:].rearrange("p k c -> p (k c)"), ps[u][:, 0:D], ACT.Copy).then_inc(S["xT_ready"], 1)
                    act.wait_ge(S["logits_done"], t + 1)
                    act.activation(score[:, bass.ds(t, 1), :].rearrange("p a e -> p (a e)"), ps[2 + u][:, 0:EXPERTS],
                                   ACT.Sigmoid, scale=inv_r[:, bass.ds(t, 1)]).then_inc(S["scored"], 1)
                with act.Fori(0, TT // 2) as i:
                    for u in range(2):
                        tile(2 * i + u, u, 2)
                tile(TT - 1, 0, 2)

            @block.vector
            def _(dve):
                dve.wait_ge(S["h2_in"], 16)
                with dve.Fori(0, TT) as t:
                    row = lambda x: x[:, bass.ds(t, 1), :].rearrange("p a d -> p (a d)")
                    dve.bn_stats(row(stats), row(h2)).then_inc(S["bn_done"], 1)
                dve.wait_ge(S["bn_done"], TT)
                moments_of(dve, stats[:], mean, var, gap, S["bn_done"], TT)
                n = [0]

                def link(ins):
                    ins.then_inc(S["chain"], 1)
                    n[0] += 1
                    dve.wait_ge(S["chain"], n[0])
                link(dve.tensor_scalar(ms[:], var[:], 1.0 / D, None, ALU.mult))
                dve.tensor_scalar(var[:], var[:], 1.0 / D, LN_EPS, ALU.mult, ALU.add).then_inc(S["eps_done"], 1)
                dve.wait_ge(S["root_done"], 1)
                link(dve.tensor_tensor(ms[:], ms[:], a[:], ALU.mult))
                link(dve.tensor_tensor(ms[:], ms[:], a[:], ALU.mult))
                dve.tensor_scalar(ms[:], ms[:], RMS_EPS, None, ALU.add).then_inc(S["eps_done"], 1)
                dve.tensor_scalar(opa[:], a[:], 1.0, None, ALU.add)
                link(dve.scalar_tensor_tensor(nma[:], mean[:], -1.0, a[:], ALU.mult, ALU.mult))
                dve.wait_ge(S["root_done"], 2)
                dve.tensor_tensor(ar[:], a[:], r[:], ALU.mult).then_inc(S["eps_done"], 1)
                dve.wait_ge(S["eps_done"], 3)

                def tile(t, u, stored):
                    if stored is not None:
                        dve.wait_ge(xn_stored[u], 16 * stored)
                        dve.wait_ge(S["turned"], t - 1)
                    row = h2[:, bass.ds(t, 1), :].rearrange("p a d -> p (a d)")
                    dve.tensor_scalar(xr[u][:], row, mean[:, bass.ds(t, 1)], ar[:, bass.ds(t, 1)],
                                      ALU.subtract, ALU.mult).then_inc(S["xn_ready"], 1)
                    dve.tensor_scalar(row, row, opa[:, bass.ds(t, 1)], nma[:, bass.ds(t, 1)], ALU.mult,
                                      ALU.add).then_inc(S["h2_in_base"], 1)
                for u in range(2):
                    tile(u, u, None)
                with dve.Fori(1, TT // 2) as i:
                    for u in range(2):
                        tile(2 * i + u, u, i)
                tile(TT - 1, 0, TT // 2)

                dve.wait_ge(S["scored"], TT)
                dve.wait_ge(S["consts_b"], 1)
                per = [P, TT, EXPERTS, EXPERTS]
                other, own = score[:].unsqueeze(2).to_broadcast(per), score[:].unsqueeze(3).to_broadcast(per)
                dve.tensor_tensor(above[:], other, own, ALU.is_gt)
                link(dve.tensor_tensor(equal[:], other, own, ALU.is_equal))
                link(dve.tensor_tensor(equal[:], equal[:], lower[:].unsqueeze(1).to_broadcast(per), ALU.mult))
                link(dve.tensor_tensor(above[:], above[:], equal[:], ALU.add))
                link(dve.tensor_reduce(rank[:], above[:], AX, ALU.add))
                link(dve.tensor_scalar(sel[:], rank[:], float(TOP), None, ALU.is_lt))
                dve.tensor_scalar(pick[:], sel[:], 1.0, None, ALU.mult).then_inc(S["sel_ready"], 1)
                link(dve.tensor_reduce(total[:], score[:], AX, ALU.add))
                link(dve.reciprocal(inv_total[:], total[:]))
                link(dve.tensor_tensor(gate[:], score[:], sel[:], ALU.mult))
                per = [P, TT, EXPERTS]
                link(dve.tensor_tensor(gate[:], gate[:], inv_total[:].unsqueeze(2).to_broadcast(per), ALU.mult))
                dve.wait_ge(S["counted"], 1)
                link(dve.tensor_copy(pos[:].rearrange("p t e -> p (t e)"), ps[4][:, 0:TT * EXPERTS]))
                dve.tensor_copy(cnt[:].rearrange("p t e -> p (t e)"), ps[5][:, 0:TT * EXPERTS])
                link(dve.tensor_copy(run_a[:].rearrange("p t e -> p (t e)"), ps[5][:, 0:TT * EXPERTS]))
                x, y, d = run_a, run_b, 1
                while d < TT:
                    dve.tensor_copy(y[:, 0:d], x[:, 0:d])
                    link(dve.tensor_tensor(y[:, d:], x[:, d:], x[:, 0:TT - d], ALU.add))
                    x, y, d = y, x, 2 * d
                link(dve.tensor_scalar(padded_i[:], x[:, TT - 1], float(TILE - 1), None, ALU.add))
                link(dve.tensor_scalar(padded_i[:], padded_i[:], -TILE, None, ALU.bitwise_and))
                link(dve.tensor_copy(padded[:], padded_i[:]))
                link(dve.tensor_copy(base_a[:], padded[:]))
                xb, yb, d = base_a, base_b, 1
                while d < EXPERTS:
                    dve.tensor_copy(yb[:, 0:d], xb[:, 0:d])
                    link(dve.tensor_tensor(yb[:, d:], xb[:, d:], xb[:, 0:EXPERTS - d], ALU.add))
                    xb, yb, d = yb, xb, 2 * d
                link(dve.tensor_tensor(yb[:], xb[:], padded[:], ALU.subtract))
                dve.tensor_tensor(pos[:], pos[:], x[:], ALU.add)
                per7 = [P, NT, EXPERTS - 1]
                link(dve.tensor_tensor(passed[:], yb[:, 1:].unsqueeze(1).to_broadcast(per7),
                                       start[:].unsqueeze(2).to_broadcast(per7), ALU.is_le))
                link(dve.tensor_reduce(tile_e[:], passed[:], AX, ALU.add))
                link(dve.tensor_copy(T["tile_expert"][:], tile_e[:]))
                link(dve.tensor_tensor(pos[:], pos[:], cnt[:], ALU.subtract))
                link(dve.tensor_tensor(slot[:], pos[:], yb[:].unsqueeze(1).to_broadcast(per), ALU.add))
                far = float(4 * NT * TILE)
                for n_slot, sign in ((0, 1.0), (1, -1.0)):
                    link(dve.tensor_scalar(pick[:], sel[:], -sign * far, sign * far, ALU.mult, ALU.add))
                    link(dve.tensor_tensor(pick[:], pick[:], slot[:], ALU.add))
                    link(dve.tensor_reduce(slot_f[:, n_slot], pick[:], AX, ALU.min if n_slot == 0 else ALU.max))
                    link(dve.tensor_tensor(pick[:], pick[:], slot_f[:, n_slot].unsqueeze(2).to_broadcast(per), ALU.is_equal))
                    link(dve.tensor_tensor(pick[:], pick[:], gate[:], ALU.mult))
                    link(dve.tensor_reduce(T["gate"][:, n_slot], pick[:], AX, ALU.add))
                link(dve.tensor_copy(T["slot"][:], slot_f[:]))


class Weights:

    PARTS = 4

    def __init__(self, nc, ctx, A, T, which, w1, w2, count):
        sb = lambda n, s, d=F32: ctx.enter_context(nc.sbuf_tensor(n + which, s, d))
        self.A, self.which, self.w1, self.w2, self.count = A, which, w1, w2, count
        self.scale, self.b1 = T["scale" + which], T["b1" + which]
        self.raw = [sb(f"raw{i}", [P, HID]) for i in range(self.PARTS)]
        self.top = sb("top", [P, self.PARTS * count])
        self.gain, self.gains = sb("gain", [P, KD]), sb("gains", [P, KD])
        self.pair, self.big, self.big_all, self.power = (sb(n, [P, c]) for n, c in (("pair", KD), ("big", 3), ("big_all", 3), ("power", 3)))
        self.raw_in = [ctx.enter_context(nc.semaphore(f"raw_in{i}{which}")) for i in range(self.PARTS)]
        self.S = {n: ctx.enter_context(nc.semaphore(n + which)) for n in
                  "gain_in topped chain bigs reduced scaled hi_done lo_done".split()}

    def load_gain(self, nc, sp):
        with nc.allow_non_contiguous_dma(reason="256 gains onto partitions"):
            sp.dma_start(self.gain[:], self.A["g" + self.which].rearrange("(k p) -> p k", p=P)).then_inc(self.S["gain_in"], 16)

    def of(self, tensor, e):
        return tensor[e] if isinstance(e, int) else tensor[bass.ds(e, 1)].rearrange("a b c -> (a b) c")

    def load(self, sp, e, second):
        for part in range(self.PARTS):
            before = self.count if second else 0
            if second:
                if isinstance(e, int) and e == 0:
                    sp.wait_ge(self.S["topped"], self.PARTS * self.count)
                else:
                    sp.wait_ge(self.S["lo_done"], self.PARTS * (e - 1) + part + 1)
            elif reached(e, 1):
                sp.wait_ge(self.S["topped"], self.PARTS * (e - 1) + part + 1)
            o = self.raw[part][:]
            if part < KD:
                src = self.of(self.A["W1" + self.which], e)[part * P:(part + 1) * P, :]
            else:
                o = o.rearrange("p (j d) -> p j d", j=HJ // 2)
                half = (part - KD) * (HJ // 2)
                src = self.of(self.A["W2" + self.which], e).rearrange("(j p) d -> p j d", p=P)[:, half:half + HJ // 2, :]
            sp.dma_start(o, src).then_inc(self.raw_in[part], 16)

    def largest(self, dve, e, part):
        dve.wait_ge(self.raw_in[part], 16 * (e + 1))
        o = self.top[:, bass.ds(part * self.count + e, 1)]
        dve.tensor_reduce(o, self.raw[part][:], AX, ALU.max, apply_absolute_value=True).then_inc(self.S["topped"], 1)

    def reduce(self, g):
        g.wait_ge(self.S["bigs"], 1)
        g.partition_all_reduce(self.big_all[:], self.big[:], P, bass.bass_isa.ReduceOp.max).then_inc(self.S["reduced"], 1)

    def find_scales(self, dve):
        S, top, big, big_all, power, scale, count = self.S, self.top, self.big, self.big_all, self.power, self.scale, self.count
        n_link = [0]

        def link(ins):
            ins.then_inc(S["chain"], 1)
            n_link[0] += 1
            dve.wait_ge(S["chain"], n_link[0])
        dve.wait_ge(S["gain_in"], 16)
        dve.wait_ge(S["topped"], self.PARTS * count)
        dve.tensor_reduce(self.pair[:], top[:, 0:KD * count].rearrange("p (k e) -> p k e", k=KD), AX, ALU.max)
        dve.tensor_reduce(big[:, 1:2], top[:, KD * count:], AX, ALU.max)
        link(dve.tensor_reduce(big[:, 2:3], self.b1[:], AX, ALU.max, apply_absolute_value=True))
        link(dve.tensor_tensor(self.pair[:], self.pair[:], self.gain[:], ALU.mult))
        dve.tensor_reduce(big[:, 0:1], self.pair[:], AX, ALU.max, apply_absolute_value=True).then_inc(S["bigs"], 1)
        dve.wait_ge(S["reduced"], 1)
        link(dve.scalar_tensor_tensor(big_all[:, 2:3], big_all[:, 0:1], float(D), big_all[:, 2:3], ALU.mult, ALU.add))
        link(dve.tensor_scalar(big_all[:], big_all[:], 1e-30, None, ALU.max))
        link(dve.tensor_scalar(power[:].bitcast(I32), big_all[:].bitcast(I32), 0x7F800000, None, ALU.bitwise_and))
        link(dve.reciprocal(big_all[:], power[:]))
        dve.tensor_scalar(scale[:, 0:1], big_all[:, 0:1], 2.0 ** 13, None, ALU.mult)
        dve.tensor_scalar(scale[:, 1:2], power[:, 0:1], 2.0 ** -13 / X_SCALE, None, ALU.mult)
        dve.tensor_scalar(scale[:, 2:3], big_all[:, 2:3], 2.0 ** 14, None, ALU.mult)
        dve.tensor_scalar(scale[:, 3:4], big_all[:, 1:2], 2.0 ** 13, None, ALU.mult)
        link(dve.scalar_tensor_tensor(scale[:, 4:5], power[:, 1:2], 2.0 ** -27, power[:, 2:3], ALU.mult, ALU.mult))
        dve.tensor_scalar(self.gains[:], self.gain[:], scale[:, 0:1], None, ALU.mult).then_inc(S["scaled"], 1)
        dve.wait_ge(S["scaled"], 1)

    def halves(self, e, part):
        if part < KD:
            to = lambda n: (self.w1[:, e, n, part, :] if isinstance(e, int) else
                            self.w1[:, bass.ds(e, 1), n, part, :].rearrange("p a c -> p (a c)"))
            return self.raw[part][:], self.gains[:, part:part + 1], to
        rows = slice((part - KD) * (HJ // 2), (part - KD + 1) * (HJ // 2))
        to = lambda n: (self.w2[:, e, n, rows, :].rearrange("p j d -> p (j d)") if isinstance(e, int) else
                        self.w2[:, bass.ds(e, 1), n, rows, :].rearrange("p a j d -> p (a j d)"))
        return self.raw[part][:], self.scale[:, 3:4], to

    def high(self, act, e, part):
        if isinstance(e, int) and e == 0 and part == 0:
            act.wait_ge(self.S["scaled"], 1)
        act.wait_ge(self.raw_in[part], 16 * (self.count + e + 1))
        src, factor, to = self.halves(e, part)
        act.activation(to(0), src, ACT.Copy, scale=factor).then_inc(self.S["hi_done"], 1)

    def low(self, dve, e, part):
        dve.wait_ge(self.S["hi_done"], self.PARTS * e + part + 1)
        src, factor, to = self.halves(e, part)
        dve.scalar_tensor_tensor(to(1), src, factor, to(0), ALU.mult, ALU.subtract).then_inc(self.S["lo_done"], 1)


def shared_weights(nc, A, T, w1, w2):
    with ExitStack() as ctx:
        W = Weights(nc, ctx, A, T, "_s", w1, w2, SHARED)
        SETS = (("_s", SHARED), ("_r", EXPERTS))
        rows = {w: ctx.enter_context(nc.sbuf_tensor("b1_rows" + w, [c * HJ, P], F32)) for w, c in SETS}
        ps = {w: ctx.enter_context(nc.psum_tensor("b1_ps" + w, [P, c * HJ], F32)) for w, c in SETS}
        b1_in, b1_turned, b1_ready = (ctx.enter_context(nc.semaphore(n)) for n in ("b1_in", "b1_turned", "b1_ready"))
        EP = [(e, part) for e in range(SHARED) for part in range(W.PARTS)]
        with nc.Block() as block:
            @block.sync
            def _(sp):
                W.load_gain(nc, sp)
                for w, _ in SETS:
                    sp.dma_start(rows[w][:], A["b1" + w].rearrange("e (j p) -> (e j) p", p=P)).then_inc(b1_in, 16)
                for second in (False, True):
                    for e in range(SHARED):
                        W.load(sp, e, second)

            @block.tensor
            def _(pe):
                pe.wait_ge(b1_in, 32)
                for w, c in SETS:
                    pe.transpose(ps[w][:], rows[w][:], T["ident"][0:c * HJ, 0:c * HJ]).then_inc(b1_turned, 1)

            @block.gpsimd
            def _(g):
                W.reduce(g)

            @block.scalar
            def _(act):
                for e, part in EP:
                    W.high(act, e, part)

            @block.vector
            def _(dve):
                dve.wait_ge(b1_turned, 2)
                for w, _ in SETS:
                    dve.tensor_copy(T["b1" + w][:], ps[w][:]).then_inc(b1_ready, 1)
                dve.wait_ge(b1_ready, 2)
                for e, part in EP:
                    W.largest(dve, e, part)
                W.find_scales(dve)
                for e, part in EP:
                    W.low(dve, e, part)
                dve.wait_ge(W.S["lo_done"], len(EP))


def ffn(nc, A, T, which, w1, w2, rounds, units, routed, routed_w=None):
    HI, LO = 0, 1
    src = T["xg"] if routed else T["xn"]
    with ExitStack() as ctx:
        sb = lambda n, s, d=F32: ctx.enter_context(nc.sbuf_tensor(n + which, s, d))
        sem = lambda n: ctx.enter_context(nc.semaphore(n + which))
        rows = sb("rows", [P, BLK, D])
        xh, xl = sb("xh", [P, KD, TILE], F16), sb("xl", [P, KD, TILE], F16)
        hf = [sb(f"hf{i}", [P, 2, TILE]) for i in range(2)]
        hh = [sb(f"hh{i}", [P, HJ, TILE], F16) for i in range(2)]
        hl = [sb(f"hl{i}", [P, HJ, TILE], F16) for i in range(2)]
        out = sb("out", [P, BLK, D])
        base = out
        b2 = sb("b2bc", [P, EXPERTS, D]) if routed else None
        pair = [ctx.enter_context(nc.psum_tensor(f"f_ps{i}{which}", [P, 2, TILE], F32)) for i in range(4)]
        y_ps = ctx.enter_context(nc.psum_tensor("f_y" + which, [P, BLK, D], F32))
        t_ps = ctx.enter_context(nc.psum_tensor("f_t" + which, [P, KD, TILE], F32))
        S = {n: sem(n) for n in "row_in added_in x_turned xh_ready xl_ready h_done gelu_done h_ready y_done y_ready y_stored staged".split()}
        scattered = None if routed else [sem(f"scattered{i}") for i in range(2)]
        scale, b1 = T["scale" + which], T["b1" + which]
        TILES = rounds * units if routed else rounds
        UNITS = rounds * units

        R = Weights(nc, ctx, A, T, "_r", *routed_w, EXPERTS) if routed_w else None
        FIND, SPLIT, LEFT = 2, 2 + EXPERTS, 2 + 2 * EXPERTS

        def run(eng, unit, tail, find=None, between=None, split=None):
            def one(i, extra, e):
                for u in range(units):
                    unit(units * i + u, u, i)
                    if extra:
                        extra(e, u)
            for i in range(2):
                one(i, None, 0)
            if R is None:
                with eng.Fori(2, rounds) as i:
                    one(i, None, 0)
            else:
                one(FIND, find, 0)
                with eng.Fori(FIND + 1, SPLIT) as i:
                    one(i, find, i - FIND)
                if between:
                    between()
                one(SPLIT, split, 0)
                with eng.Fori(SPLIT + 1, LEFT) as i:
                    one(i, split, i - SPLIT)
                with eng.Fori(LEFT, rounds) as i:
                    one(i, None, 0)
            tail()

        def tile_of(n, i):
            return n if routed else i

        def turns(u):
            return routed or u == units - 1

        with nc.Block() as block:
            @block.sync
            def _(sp):
                if routed:
                    sp.dma_start(b2[:].rearrange("p e d -> p (e d)"), A["b2" + which].rearrange("e d -> (e d)").partition_broadcast(P)).then_inc(S["added_in"], 16)

                def load(t):
                    sp.dma_start(rows[:], src[bass.ds(t * TILE, TILE), :].rearrange("(b p) d -> p b d", p=P)).then_inc(S["row_in"], 16)
                load(0)
                if not routed:
                    sp.dma_start(base[:], T["base"][0:TILE, :].rearrange("(b p) d -> p b d", p=P)).then_inc(S["added_in"], 16)

                def store(t):
                    sp.wait_ge(S["y_ready"], t + 1)
                    dst = T["y"] if routed else T["part"]
                    sp.dma_start(dst[bass.ds(t * TILE, TILE), :].rearrange("(b p) d -> p b d", p=P), out[:]).then_inc(S["y_stored"], 16)
                sp.wait_ge(S["x_turned"], 1)
                load(1)

                def tile(t):
                    sp.wait_ge(S["x_turned"], t + 1)
                    load(t + 1)
                    store(t - 1)
                    if not routed:
                        sp.wait_ge(S["y_stored"], 16 * t)
                        sp.dma_start(base[:], T["base"][bass.ds(t * TILE, TILE), :].rearrange("(b p) d -> p b d", p=P)).then_inc(S["added_in"], 16)
                if R is None:
                    with sp.Fori(1, TILES) as t:
                        tile(t)
                else:
                    R.load_gain(nc, sp)
                    tile(1)
                    for second, begin in ((False, FIND), (True, SPLIT)):
                        R.load(sp, 0, second)
                        tile(begin)
                        with sp.Fori(begin + 1, begin + EXPERTS) as t:
                            R.load(sp, t - begin, second)
                            tile(t)
                    with sp.Fori(LEFT, TILES) as t:
                        tile(t)
                store(TILES - 1)
                sp.wait_ge(S["y_stored"], 16 * TILES)
                sp.wait_ge(S["row_in"], 16 * (TILES + 1))
                if not routed:
                    sp.wait_ge(S["added_in"], 16 * TILES)

            @block.tensor
            def _(pe):
                def turn(t):
                    pe.wait_ge(S["row_in"], 16 * (t + 1))
                    for k in range(KD):
                        for b in range(BLK):
                            mm = pe.transpose(t_ps[:, k, b * P:(b + 1) * P], rows[:, b, k * P:(k + 1) * P], T["ident"][:])
                    mm.then_inc(S["x_turned"], 1)

                def up(n, u, i):
                    e = expert(n) if routed else u
                    pe.wait_ge(S["xl_ready"], tile_of(n, i) + 1)
                    for p in range(4):
                        if reached(n, 1):
                            pe.wait_ge(S["gelu_done"], 4 * n + p - 3)
                        for j2 in range(2):
                            o = pair[p][:, j2, :]
                            col = slice((2 * p + j2) * P, (2 * p + j2 + 1) * P)
                            for k in range(KD):
                                pe.matmul(o, w1_at(e, HI, k, col), xh[:, k, :], start=k == 0, stop=False)
                                pe.matmul(o, w1_at(e, HI, k, col), xl[:, k, :], start=False, stop=False)
                                mm = pe.matmul(o, w1_at(e, LO, k, col), xh[:, k, :], start=False, stop=k == KD - 1)
                        mm.then_inc(S["h_done"], 1)

                def down(n, u, tile):
                    e = expert(n) if routed else u
                    first, last = routed or u == 0, routed or u == units - 1
                    pe.wait_ge(S["h_ready"], 4 * n + 4)
                    if first and reached(tile, 1):
                        pe.wait_ge(S["y_ready"], tile)
                    q = u % 2
                    for j in range(HJ):
                        for b in range(BLK):
                            o, col = y_ps[:, b, :], slice(b * P, (b + 1) * P)
                            pe.matmul(o, hh[q][:, j, col], w2_at(e, HI, j), start=first and j == 0 and b == 0, stop=False)
                            pe.matmul(o, hh[q][:, j, col], w2_at(e, LO, j), start=False, stop=False)
                            mm = pe.matmul(o, hl[q][:, j, col], w2_at(e, HI, j), start=False, stop=last and j == HJ - 1 and b == BLK - 1)
                    if last:
                        mm.then_inc(S["y_done"], 1)

                def w1_at(e, part, k, col):
                    if routed:
                        return w1[:, bass.ds(e, 1), part, k, col].rearrange("p a c -> p (a c)")
                    return w1[:, e, part, k, col]

                def w2_at(e, part, j):
                    if routed:
                        return w2[:, bass.ds(e, 1), part, j, :].rearrange("p a c -> p (a c)")
                    return w2[:, e, part, j, :]

                def expert(n):
                    return pe.value_load(T["tile_expert"][0:1, bass.ds(n, 1)], min_val=0, max_val=EXPERTS - 1)

                def unit(n, u, i):
                    up(n, u, i)
                    if turns(u):
                        turn(tile_of(n, i) + 1)
                    if reached(n, 1):
                        pu = (u - 1) % units
                        down(n - 1, pu, tile_of(n - 1, i if u else i - 1))
                turn(0)
                run(pe, unit, lambda: down(UNITS - 1, units - 1, TILES - 1))

            @block.scalar
            def _(act):
                def split(t):
                    act.wait_ge(S["x_turned"], t + 1)
                    act.activation(xh[:].rearrange("p k c -> p (k c)"), t_ps[:].rearrange("p k c -> p (k c)"), ACT.Copy, scale=X_SCALE).then_inc(S["xh_ready"], 1)

                def unit(n, u, i):
                    if routed:
                        e = act.value_load(T["tile_expert"][0:1, bass.ds(n, 1)], min_val=0, max_val=EXPERTS - 1)
                    for p in range(4):
                        act.wait_ge(S["h_done"], 4 * n + p + 1)
                        if reached(n, 1) or p >= 2:
                            act.wait_ge(S["h_ready"], 4 * n + p - 1)
                        for j2 in range(2):
                            j = 2 * p + j2
                            bias = b1[:, bass.ds(e * HJ + j, 1)] if routed else b1[:, u * HJ + j:u * HJ + j + 1]
                            last = act.activation(hf[p % 2][:, j2, :], pair[p][:, j2, :], ACT.Gelu, bias=bias, scale=scale[:, 1:2])
                        last.then_inc(S["gelu_done"], 1)
                    if turns(u):
                        split(tile_of(n, i) + 1)
                split(0)
                per = Weights.PARTS // units
                run(act, unit, lambda: None,
                    split=lambda e, u: [R.high(act, e, part) for part in range(u * per, (u + 1) * per)])

            @block.vector
            def _(dve):
                def split(t):
                    dve.wait_ge(S["xh_ready"], t + 1)
                    dve.scalar_tensor_tensor(xl[:].rearrange("p k c -> p (k c)"), t_ps[:].rearrange("p k c -> p (k c)"), X_SCALE,
                                             xh[:].rearrange("p k c -> p (k c)"), ALU.mult, ALU.subtract).then_inc(S["xl_ready"], 1)

                def finish(n, tile):
                    dve.wait_ge(S["y_done"], tile + 1)
                    if reached(tile, 1):
                        dve.wait_ge(S["y_stored"], 16 * tile)
                    if routed:
                        e = dve.value_load(T["tile_expert"][0:1, bass.ds(n, 1)], min_val=0, max_val=EXPERTS - 1)
                        for b in range(BLK):
                            last = dve.scalar_tensor_tensor(out[:, b, :], y_ps[:, b, :], scale[:, 4:5],
                                                            b2[:, bass.ds(e, 1), :].rearrange("p a d -> p (a d)"), ALU.mult, ALU.add)
                    else:
                        dve.wait_ge(S["added_in"], 16 * (tile + 1))
                        last = dve.scalar_tensor_tensor(out[:], y_ps[:], scale[:, 4:5], base[:], ALU.mult, ALU.add)
                    last.then_inc(S["y_ready"], 1)

                def unit(n, u, i):
                    q = u % 2
                    for p in range(4):
                        dve.wait_ge(S["gelu_done"], 4 * n + p + 1)
                        o = slice(2 * p, 2 * p + 2)
                        dve.tensor_scalar(hh[q][:, o, :], hf[p % 2][:], scale[:, 2:3], None, ALU.mult).then_inc(S["staged"], 1)
                        dve.wait_ge(S["staged"], 4 * n + p + 1)
                        dve.scalar_tensor_tensor(hl[q][:, o, :], hf[p % 2][:], scale[:, 2:3], hh[q][:, o, :],
                                                 ALU.mult, ALU.subtract).then_inc(S["h_ready"], 1)
                    if turns(u):
                        split(tile_of(n, i) + 1)
                    pu = (u - 1) % units
                    if reached(n, 1) and (routed or pu == units - 1):
                        finish(n - 1, tile_of(n - 1, i if u else i - 1))
                if routed:
                    dve.wait_ge(S["added_in"], 16)
                split(0)
                per = Weights.PARTS // units
                parts = lambda f: lambda e, u: [f(dve, e, part) for part in range(u * per, (u + 1) * per)]
                if R is None:
                    run(dve, unit, lambda: finish(UNITS - 1, TILES - 1))
                else:
                    run(dve, unit, lambda: finish(UNITS - 1, TILES - 1), parts(R.largest), lambda: R.find_scales(dve), parts(R.low))
                    dve.wait_ge(R.S["lo_done"], R.PARTS * EXPERTS)

            if not routed:
                @block.gpsimd
                def _(g):
                    scatter(g, nc, T, scattered, ctx)
                    R.reduce(g)


def scatter(g, nc, T, scattered, ctx):
    xr = [ctx.enter_context(nc.sbuf_tensor(f"sc_x{i}", [P, D], F32)) for i in range(2)]
    xr_in = [ctx.enter_context(nc.semaphore(f"sc_in{i}")) for i in range(2)]
    for t in range(TT):
        q = t % 2
        if t >= 2:
            g.wait_ge(scattered[q], 32 * (t // 2))
        g.dma_start(xr[q][:], T["xn"][t * P:(t + 1) * P, :]).then_inc(xr_in[q], 16)
        if t >= 1:
            send(g, T, xr, xr_in, scattered, t - 1)
    send(g, T, xr, xr_in, scattered, TT - 1)
    g.wait_ge(scattered[0], 32 * (TT // 2 + 1))
    g.wait_ge(scattered[1], 32 * (TT // 2))


def send(g, T, xr, xr_in, scattered, t):
    q = t % 2
    g.wait_ge(xr_in[q], 16 * (t // 2 + 1))
    for which in range(2):
        g.indirect_dma_start(T["xg"][:, :], bass.IndirectOffsetOnAxis(ap=T["slot"][:, which, t:t + 1], axis=0),
                             xr[q][:], None, bounds_check=NT * TILE - 1).then_inc(scattered[q], 16)


def combine(nc, T, out):
    with ExitStack() as ctx:
        RING = 4
        sb = lambda n, s, d=F32: ctx.enter_context(nc.sbuf_tensor(n, s, d))
        sem = lambda n: ctx.enter_context(nc.semaphore(n))
        part = [sb(f"c_part{i}", [P, D]) for i in range(RING)]
        ya = [sb(f"c_ya{i}", [P, D]) for i in range(RING)]
        yb = [sb(f"c_yb{i}", [P, D]) for i in range(RING)]
        part_in = [sem(f"c_part_in{i}") for i in range(RING)]
        y_in = [sem(f"c_y_in{i}") for i in range(RING)]
        stored = [sem(f"c_stored{i}") for i in range(RING)]
        half_done, done = sem("c_half_done"), sem("c_done")
        with nc.Block() as block:
            @block.gpsimd
            def _(g):
                for t in range(TT):
                    q = t % RING
                    if t >= RING:
                        g.wait_ge(y_in[q], 32 * (t // RING))
                        g.wait_ge(done, t - RING + 1)
                    for which, y in ((0, ya), (1, yb)):
                        g.indirect_dma_start(y[q][:], None, T["y"][:, :], bass.IndirectOffsetOnAxis(ap=T["slot"][:, which, t:t + 1], axis=0),
                                             bounds_check=NT * TILE - 1).then_inc(y_in[q], 16)

            @block.sync
            def _(sp):
                for t in range(TT + 2):
                    if t < TT:
                        q = t % RING
                        if t >= RING:
                            sp.wait_ge(stored[q], 16 * (t // RING))
                        sp.dma_start(part[q][:], T["part"][t * P:(t + 1) * P, :]).then_inc(part_in[q], 16)
                    if t >= 2:
                        d = t - 2
                        sp.wait_ge(done, d + 1)
                        sp.dma_start(out[d * P:(d + 1) * P, :], part[d % RING][:]).then_inc(stored[d % RING], 16)
                for q in range(RING):
                    sp.wait_ge(stored[q], 16 * len(range(q, TT, RING)))

            @block.vector
            def _(dve):
                for t in range(TT):
                    q = t % RING
                    dve.wait_ge(part_in[q], 16 * (t // RING + 1))
                    dve.wait_ge(y_in[q], 32 * (t // RING + 1))
                    dve.scalar_tensor_tensor(part[q][:], ya[q][:], T["gate"][:, 0, t:t + 1], part[q][:], ALU.mult, ALU.add).then_inc(half_done, 1)
                    dve.wait_ge(half_done, t + 1)
                    dve.scalar_tensor_tensor(part[q][:], yb[q][:], T["gate"][:, 1, t:t + 1], part[q][:], ALU.mult, ALU.add).then_inc(done, 1)


def early_fusion_block(nc, x, txt, tok_W, Wq, bq, Wk, bk, Wv, bv, Wo, bo, g_shared, W1_s, b1_s, W2_s, b2_s,
                       g_routed, W1_r, b1_r, W2_r, b2_r, centroids, out):
    A = {"Wq": Wq, "Wk": Wk, "Wv": Wv, "Wo": Wo, "bq": bq, "bk": bk, "bv": bv, "bo": bo, "centroids": centroids,
         "g_s": g_shared, "W1_s": W1_s, "b1_s": b1_s, "W2_s": W2_s, "b2_s": b2_s,
         "g_r": g_routed, "W1_r": W1_r, "b1_r": b1_r, "W2_r": W2_r, "b2_r": b2_r}
    with ExitStack() as ctx:
        sb = lambda n, s, d=F32: ctx.enter_context(nc.sbuf_tensor(n, s, d))
        rows = lambda n, count: nc.dram_tensor(n, [count, D], F32, kind="Internal").ap()
        T = {
            "ident": sb("ident", [P, P]),
            "slot": sb("slot", [P, TOP, TT], I32), "gate": sb("gate", [P, TOP, TT]),
            "tile_expert": sb("tile_expert", [P, NT], I32),
            "scale_s": sb("scale_s", [P, 5]), "scale_r": sb("scale_r", [P, 5]),
            "b1_s": sb("b1T_s", [P, SHARED * HJ]), "b1_r": sb("b1T_r", [P, EXPERTS * HJ]),
            "patch_h": rows("patch_h", BATCH * NPATCH), "h2": rows("h2_rows", TOKENS),
            "xn": rows("xn_rows", (GROUPS + 1) * TILE), "base": rows("base_rows", (GROUPS + 1) * TILE),
            "part": rows("part_rows", GROUPS * TILE),
            "xg": rows("slot_rows", (NT + 1) * TILE), "y": rows("y_rows", NT * TILE),
        }
        patches = nc.dram_tensor("patches", [BATCH * CHANNELS, IMAGE * IMAGE], F32, kind="Internal").ap()
        ident_done = ctx.enter_context(nc.semaphore("ident_done"))
        with nc.Block() as block:
            @block.gpsimd
            def _(g):
                g.memset(T["ident"][:], 0.0).then_inc(ident_done, 1)
                g.wait_ge(ident_done, 1)
                g.affine_select(out=T["ident"][:], in_=T["ident"][:], compare_op=ALU.not_equal, fill=1.0,
                                base=0, pattern=[[-1, P]], channel_multiplier=1).then_inc(ident_done, 1)
                g.wait_ge(ident_done, 2)
        patch_embed(nc, x, tok_W, patches, T)
        attention(nc, txt, A, T)
        router(nc, A, T)
        w1s, w2s = sb("w1s", [P, SHARED, 2, KD, HID], F16), sb("w2s", [P, SHARED, 2, HJ, D], F16)
        w1r, w2r = sb("w1r", [P, EXPERTS, 2, KD, HID], F16), sb("w2r", [P, EXPERTS, 2, HJ, D], F16)
        shared_weights(nc, A, T, w1s, w2s)
        ffn(nc, A, T, "_s", w1s, w2s, GROUPS, SHARED, False, (w1r, w2r))
        ffn(nc, A, T, "_r", w1r, w2r, NT // 2, 2, True)
        combine(nc, T, out)


_INS = ['x', 'txt', 'L0_tok_W', 'L0_attn_Wq', 'L0_attn_bq', 'L0_attn_Wk', 'L0_attn_bk', 'L0_attn_Wv', 'L0_attn_bv',
        'L0_attn_Wo', 'L0_attn_bo', 'L0_ffn_g_shared', 'L0_ffn_W1_s', 'L0_ffn_b1_s', 'L0_ffn_W2_s', 'L0_ffn_b2_s',
        'L0_ffn_g_routed', 'L0_ffn_W1_r', 'L0_ffn_b1_r', 'L0_ffn_W2_r', 'L0_ffn_b2_r', 'L0_ffn_centroids']


def kernel(**inputs):
    import numpy as _np
    import concourse.bacc as _bacc
    from concourse import mybir as _mybir
    from concourse.bass_utils import run_bass_kernel_spmd as _run

    nc = _bacc.Bacc("TRN2", target_bir_lowering=False, num_devices=1)
    arrays, args = {}, []
    for name in _INS:
        a = _np.ascontiguousarray(inputs[name])
        arrays[f"in_{name}_dram"] = a
        args.append(nc.dram_tensor(f"in_{name}_dram", a.shape, _mybir.dt.from_np(a.dtype), kind="ExternalInput").ap())
    args.append(nc.dram_tensor("out_0_dram", (TOKENS, D), _mybir.dt.float32, kind="ExternalOutput").ap())
    early_fusion_block(nc, *args)
    r = _run(nc, [arrays], core_ids=[0])
    return _np.asarray(r.results[0]["out_0_dram"]).reshape(BATCH, SEQ, D)
```

```python
import concourse.bass as bass
from concourse import mybir
from contextlib import ExitStack

F32 = mybir.dt.float32
F16 = mybir.dt.float16
BF16 = mybir.dt.bfloat16
I32 = mybir.dt.int32
ACT = mybir.ActivationFunctionType
ALU = mybir.AluOpType
AX = mybir.AxisListType.X

P = 128
BATCH, CHANNELS, IMAGE, PATCH = 32, 3, 96, 16
GRID = IMAGE // PATCH
NPATCH = GRID * GRID
FLAT = CHANNELS * PATCH * PATCH
TEXT = 128
SEQ = NPATCH + TEXT
D = 256
KD = D // P
HEADS, HD = 16, 16
HG = P // HD
TOKENS = BATCH * SEQ
TT = TOKENS // P
LN_EPS = 1e-5
MASK = -1.0e30
XA_SCALE, QKV_SCALE, WO_SCALE, E_SCALE = 2.0 ** 5, 2.0 ** 14, 2.0 ** 13, 2.0 ** 14


def reached(value, n):
    return not isinstance(value, int) or value >= n


def attention_inputs(nc, ctx, T):
    rows = BATCH + 2
    for name, shape in (("h_text", [P, rows, D]), ("ln_stats", [P, 2, rows, 6]), ("attn_w_in", [P, 4, KD, D]),
                        ("attn_b", [P, 3, KD]), ("bo", [P, D])):
        T[name] = ctx.enter_context(nc.sbuf_tensor(name, shape, F32))


def patch_embed(nc, x, W, patches, txt, A, T):
    NT = BATCH * NPATCH // P
    PER = 3
    with ExitStack() as ctx:
        sb = lambda n, s, d=F32: ctx.enter_context(nc.sbuf_tensor(n, s, d))
        sem = lambda n: ctx.enter_context(nc.semaphore(n))
        planes = sb("planes", [BATCH * CHANNELS, IMAGE * IMAGE])
        ordered = sb("ordered", [BATCH * CHANNELS, IMAGE * IMAGE])
        w_sb = sb("tok_w", [P, FLAT // P, D])
        rows = sb("patch_rows", [P, NT, FLAT])
        rowsT = sb("patch_rows_T", [P, PER, FLAT])
        h_out = sb("patch_h_rows", [P, NT, D])
        ps = [ctx.enter_context(nc.psum_tensor(f"pe_ps{i}", [P, 512], F32)) for i in range(8)]
        text, stats, w_in, b_in, bo = (T[n] for n in ("h_text", "ln_stats", "attn_w_in", "attn_b", "bo"))
        text_in, later_in, text_bn = sem("text_in"), sem("later_in"), sem("text_bn")
        plane_in = [sem(f"plane_in{i}") for i in range(GRID)]
        tok_w_in = sem("tok_w_in")
        row_in, patches_out = [[sem(f"{n}{i}") for i in range(2)] for n in ("row_in", "patches_out")]
        HALF_PLANES, EARLY = BATCH * CHANNELS // 2, BATCH * NPATCH // 2 // P
        reordered_v, reordered_a = sem("reordered_v"), sem("reordered_a")
        t_done, t_copied, mm_done, h_copied, h_stored = (
            sem("t_done"), sem("t_copied"), sem("mm_done"), sem("h_copied"), sem("h_stored"))
        x_v = x.rearrange("b c h w -> (b c) (h w)")
        BAND = PATCH * IMAGE
        src = planes[:].rearrange("p (y i x j) -> p y i j x", y=GRID, i=PATCH, x=GRID)
        dst = ordered[:].rearrange("p (i j y x) -> p y i j x", i=PATCH, j=PATCH, y=GRID)
        with nc.Block() as block:
            @block.sync
            def _(sp):
                for y in range(GRID):
                    sp.dma_start(planes[:, y * BAND:(y + 1) * BAND],
                                 x_v[:, y * BAND:(y + 1) * BAND]).then_inc(plane_in[y], 16)
                sp.dma_start(w_sb[:], W.rearrange("(k p) d -> p k d", p=P)).then_inc(tok_w_in, 16)
                sp.wait_ge(reordered_v, GRID // 2)
                sp.wait_ge(reordered_a, GRID // 2)
                for n in range(2):
                    own = slice(n * HALF_PLANES, (n + 1) * HALF_PLANES)
                    sp.dma_start(patches[own], ordered[own]).then_inc(patches_out[n], 16)
                as_rows = patches.rearrange("a b -> (a b)").rearrange("(t p f) -> p t f", p=P, f=FLAT)
                for n, tiles in enumerate((slice(0, EARLY), slice(EARLY, NT))):
                    sp.wait_ge(patches_out[n], 16)
                    sp.dma_start(rows[:, tiles], as_rows[:, tiles]).then_inc(row_in[n], 16)
                sp.dma_start(text[:, 0:BATCH], txt.rearrange("b p d -> p b d")).then_inc(text_in, 16)
                for n, name in enumerate(("Wq", "Wk", "Wv", "Wo")):
                    sp.dma_start(w_in[:, n], A[name].rearrange("(m p) c -> p m c", p=P)).then_inc(later_in, 16)
                with nc.allow_non_contiguous_dma(reason="256 biases onto partitions"):
                    for n, name in enumerate(("bq", "bk", "bv")):
                        sp.dma_start(b_in[:, n], A[name].rearrange("(m p) -> p m", p=P)).then_inc(later_in, 16)
                sp.dma_start(bo[:], A["bo"].partition_broadcast(P)).then_inc(later_in, 16)
                sp.wait_ge(h_copied, NT)
                sp.dma_start(T["patch_h"].rearrange("(t p) d -> p t d", p=P), h_out[:]).then_inc(h_stored, 16)
                sp.wait_ge(h_stored, 16)
                sp.wait_ge(later_in, 16 * 8)

            @block.gpsimd
            def _(g):
                g.memset(text[:, BATCH:], 0.0)
                g.memset(stats[:], 1.0).then_inc(text_bn, 1)

            @block.vector
            def _(dve):
                for n, y in enumerate(range(0, GRID, 2)):
                    dve.wait_ge(plane_in[y], 16)
                    dve.tensor_copy(dst[:, y], src[:, y]).then_inc(reordered_v, 1)
                with dve.Fori(0, NT // PER) as r:
                    for u in range(PER):
                        dve.wait_ge(t_done, r * PER + u + 1)
                        dve.tensor_copy(rowsT[:, u, 0:512], ps[2 * u][:, :])
                        dve.tensor_copy(rowsT[:, u, 512:FLAT], ps[2 * u + 1][:, 0:FLAT - 512]).then_inc(t_copied, 1)

                dve.wait_ge(text_bn, 1)
                dve.wait_ge(text_in, 16)
                row_statistics(dve, stats[:, 0], text, text_bn)
                dve.wait_ge(text_bn, 1 + text.shape[1])

            @block.scalar
            def _(act):
                for n, y in enumerate(range(1, GRID, 2)):
                    act.wait_ge(plane_in[y], 16)
                    act.activation(dst[:, y], src[:, y], ACT.Copy).then_inc(reordered_a, 1)
                with act.Fori(0, NT // PER) as r:
                    for u in range(PER):
                        act.wait_ge(mm_done, r * PER + u + 1)
                        act.activation(h_out[:, bass.ds(r * PER + u, 1), :].rearrange("p a d -> p (a d)"),
                                       ps[6 + u % 2][:, 0:D], ACT.Copy).then_inc(h_copied, 1)

            @block.tensor
            def _(pe):
                pe.wait_ge(row_in[0], 16)
                pe.wait_ge(tok_w_in, 16)
                for r in range(NT // PER):
                    for u in range(PER):
                        if r * PER + u == EARLY:
                            pe.wait_ge(row_in[1], 16)
                        for k in range(FLAT // P):
                            o = ps[2 * u + k // 4][:, (k % 4) * P:(k % 4 + 1) * P]
                            if k == 0 and r:
                                pe.wait_ge(t_copied, (r - 1) * PER + u + 1)
                            mm = pe.transpose(o, rows[:, r * PER + u, k * P:(k + 1) * P], T["ident"][:])
                        mm.then_inc(t_done, 1)
                    for u in range(PER):
                        n = r * PER + u
                        pe.wait_ge(t_copied, n + 1)
                        if n >= 2:
                            pe.wait_ge(h_copied, n if u == 0 else n - 1)
                        for k in range(FLAT // P):
                            mm = pe.matmul(ps[6 + u % 2][:, 0:D], rowsT[:, u, k * P:(k + 1) * P], w_sb[:, k, :],
                                           start=k == 0, stop=k == FLAT // P - 1)
                        mm.then_inc(mm_done, 1)


def moments_of(dve, stats, mean, squares, gap, sem, count):
    dve.tensor_tensor(gap[:], stats[:, :, 1], stats[:, :, 4], ALU.subtract)
    dve.tensor_tensor(mean[:], stats[:, :, 1], stats[:, :, 4], ALU.add)
    dve.tensor_tensor(squares[:], stats[:, :, 2], stats[:, :, 5], ALU.add).then_inc(sem, 1)
    dve.wait_ge(sem, count + 1)
    dve.tensor_tensor(gap[:], gap[:], gap[:], ALU.mult)
    dve.tensor_scalar(mean[:], mean[:], 0.5, None, ALU.mult).then_inc(sem, 1)
    dve.wait_ge(sem, count + 2)
    dve.scalar_tensor_tensor(squares[:], gap[:], D / 4, squares[:], ALU.mult, ALU.add).then_inc(sem, 1)
    dve.wait_ge(sem, count + 3)


def row_statistics(dve, stats, rows, sem):
    def one(i):
        row = lambda t: t[:, bass.ds(i, 1), :].rearrange("p a d -> p (a d)")
        dve.bn_stats(row(stats), row(rows)).then_inc(sem, 1)
    count = rows.shape[1]
    with dve.Fori(0, count // 4) as i:
        for u in range(4):
            one(4 * i + u)
    for i in range(count // 4 * 4, count):
        one(i)


def attention(nc, A, T, w1s, w2s):
    STEPS = 2 * BATCH
    GD = HG * HD
    PAIRS = HG // 2
    HALF = P // 2
    VW = HD + 1
    HI, LO = 0, 1
    with ExitStack() as ctx:
        sb = lambda n, s, d=F32: ctx.enter_context(nc.sbuf_tensor(n, s, d))
        sem = lambda n: ctx.enter_context(nc.semaphore(n))
        NB = BATCH + 2
        h_text, stats, w_in, b_in, bo = (T[n] for n in ("h_text", "ln_stats", "attn_w_in", "attn_b", "bo"))
        assert h_text.shape[1] == NB
        h_patch = sb("h_patch", [NPATCH, NB, D])
        mean = sb("ln_mean", [P, 2 * NB])
        mean_gap = sb("ln_mean_gap", [P, 2 * NB])
        rstd = sb("ln_rstd", [P, 2 * NB])
        expo = sb("ln_expo", [P, 2 * NB])
        w = sb("attn_w", [P, 4, 2, KD, D], F16)
        big, big_all = sb("attn_big", [P, 7]), sb("attn_big_all", [P, 7])
        power, inv_power = sb("attn_power", [P, 4]), sb("attn_inv_power", [P, 4])
        w_scale, b_scale, back = sb("attn_w_scale", [P, 4]), sb("attn_b_scale", [P, 3]), sb("attn_back", [P, 2])
        head_of = sb("head_of", [P, HG], F16)
        one = sb("attn_one", [P, 2 * KD], F16)
        causal = sb("causal", [P, 4, TEXT], BF16)
        causal_p = sb("causal_p", [P, HG, NPATCH], BF16)
        identb = sb("identb", [P, P], BF16)
        xn = sb("xn", [P, D])
        xn_p = sb("xn_p", [NPATCH, D])
        x = [sb(f"xT{i}", [P, 2, KD, SEQ + 2 * HALF], F16) for i in range(2)]
        qk = [sb(f"qk{i}", [P, 2, 2, SEQ], F16) for i in range(2)]
        kbd = [sb(f"kbd{i}", [P, 2, HG, SEQ], F16) for i in range(2)]
        v_t = [sb(f"v_t{i}", [P, 2, HEADS, VW], F16) for i in range(2)]
        v_p = [sb(f"v_p{i}", [P, 2, HEADS // 2, 2, VW], F16) for i in range(2)]
        e_tt = [sb(f"e_tt{i}", [P, HG, TEXT]) for i in range(2)]
        e_p = [sb(f"e_p{i}", [P, 2, HG, HALF]) for i in range(2)]
        top_t, top = sb("top_t", [P, HG]), sb("top", [P, 2, HG])
        eT_tt = sb("eT_tt", [P, 2, HG, P], F16)
        eT_tp = sb("eT_tp", [P, 2, PAIRS, P], F16)
        eT_pp = sb("eT_pp", [P, 2, PAIRS, NPATCH], F16)
        inv, inv_p = sb("inv", [P, HG]), sb("inv_p", [NPATCH, HG])
        o, o_p = sb("attn_o", [P, D]), sb("attn_o_p", [NPATCH, D])
        oT = sb("attn_oT", [P, 2, KD, SEQ], F16)
        hb = [sb(f"hb{i}", [P, D]) for i in range(2)]
        hb_p = [sb(f"hb_p{i}", [NPATCH, D]) for i in range(2)]
        h2 = [sb(f"h2_{i}", [P, D]) for i in range(2)]
        h2_p = [sb(f"h2_p{i}", [NPATCH, D]) for i in range(2)]
        sc = ctx.enter_context(nc.psum_tensor("at_scores", [P, HG, TEXT], F32))
        sc_p = ctx.enter_context(nc.psum_tensor("at_scores_p", [P, 2, 512], F32))
        turn = [ctx.enter_context(nc.psum_tensor(f"at_turn{i}", [P, 512], F32)) for i in range(2)]
        x_ps, v_ps = (ctx.enter_context(nc.psum_tensor(n, [P, 512], F32)) for n in ("at_x", "at_v"))
        w_ps = [sc_p[:, 0], sc_p[:, 1], turn[0][:], turn[1][:]]

        ZROWS = T["xg"].shape[0] // (BATCH // 2)
        assert ZROWS * (BATCH // 2) == T["xg"].shape[0] and ZROWS * D % P == 0
        zeros = sb("attn_zeros", [P, ZROWS * D // P])
        names = ("rows_in gap_zeroed centred zeroed rest_zeroed shared_in w_turned w_high w_low bn_done eps_done consts_done "
                 "bigs reduced chain xn_ready xt_done x_hi x_lo x_doubled qk_done qk_hi qk_lo kbd_ready v_done v_hi v_lo "
                 "s_done maxed shifted exp_done t_done t_hi t_lo o_done inverted o_ready ot_done ot_hi ot_lo wo_done "
                 "hb_ready h2_ready").split()
        S = {n: sem(n) for n in names}
        h2_stored = [sem(f"h2_stored{i}") for i in range(2)]

        with nc.Block() as block:
            @block.sync
            def _(sp):
                sp.dma_start(h_patch[:, 0:BATCH], T["patch_h"].rearrange("(b p) d -> p b d", p=NPATCH)).then_inc(S["rows_in"], 16)

            @block.gpsimd
            def _(g):
                g.memset(h_patch[:, BATCH:], 0.0).then_inc(S["gap_zeroed"], 1)
                g.memset(expo[:], -0.5).then_inc(S["gap_zeroed"], 1)
                g.wait_ge(S["bigs"], 1)
                g.partition_all_reduce(big_all[:], big[:], P, bass.bass_isa.ReduceOp.max).then_inc(S["reduced"], 1)

                def root(n):
                    own = slice(n * NB, (n + 1) * NB)
                    g.wait_ge(S["eps_done"], n + 1)
                    g.tensor_tensor(rstd[:, own], rstd[:, own], expo[:, own], ALU.pow)
                g.wait_ge(S["gap_zeroed"], 2)
                root(0)
                g.memset(zeros[:], 0.0)
                g.memset(causal[:], 0.0)
                g.memset(causal_p[:], 0.0)
                g.memset(head_of[:], 1.0)
                g.memset(one[:], 1.0)
                g.memset(identb[:], 0.0)
                for i in range(2):
                    g.memset(x[i][:], 0.0)
                    g.memset(e_p[i][:], 0.0)
                    g.memset(v_t[i][:, LO], 0.0)
                    g.memset(v_t[i][:, HI], 1.0)
                    last = g.memset(v_p[i][:], 0.0)
                last.then_inc(S["consts_done"], 1)
                g.wait_ge(S["consts_done"], 1)
                g.affine_select(out=causal[:], in_=causal[:], compare_op=ALU.is_ge, fill=MASK,
                                base=0, pattern=[[0, 4], [-1, TEXT]], channel_multiplier=1)
                g.affine_select(out=causal_p[:], in_=causal_p[:], compare_op=ALU.is_ge, fill=MASK,
                                base=0, pattern=[[0, HG], [-1, NPATCH]], channel_multiplier=1)
                g.affine_select(out=identb[:], in_=identb[:], compare_op=ALU.not_equal, fill=1.0,
                                base=0, pattern=[[-1, P]], channel_multiplier=1)
                g.affine_select(out=head_of[:], in_=head_of[:], compare_op=ALU.is_ge, fill=0.0,
                                base=0, pattern=[[-HD, HG]], channel_multiplier=1).then_inc(S["consts_done"], 1)
                g.wait_ge(S["consts_done"], 2)
                g.affine_select(out=head_of[:], in_=head_of[:], compare_op=ALU.is_ge, fill=0.0,
                                base=HD - 1, pattern=[[HD, HG]], channel_multiplier=-1).then_inc(S["consts_done"], 1)
                root(1)

            @block.vector
            def _(dve):
                n_link = [0]

                def link(ins):
                    ins.then_inc(S["chain"], 1)
                    n_link[0] += 1
                    dve.wait_ge(S["chain"], n_link[0])
                def moments(n, count):
                    own = slice(n * NB, (n + 1) * NB)
                    moments_of(dve, stats[:, n], mean[:, own], rstd[:, own], mean_gap[:, own], S["bn_done"], count)
                    dve.tensor_scalar(rstd[:, own], rstd[:, own], 1.0 / D, LN_EPS, ALU.mult, ALU.add).then_inc(S["eps_done"], 1)
                dve.tensor_reduce(big[:, 0:4], w_in[:].rearrange("p n k d -> p n (k d)"), AX, ALU.max, apply_absolute_value=True)
                dve.tensor_reduce(big[:, 4:7], b_in[:], AX, ALU.max, apply_absolute_value=True).then_inc(S["bigs"], 1)
                moments(0, 0)
                dve.wait_ge(S["reduced"], 1)
                link(dve.scalar_tensor_tensor(big_all[:, 0:3], big_all[:, 0:3], float(D), big_all[:, 4:7], ALU.mult, ALU.add))
                dve.tensor_scalar(big_all[:, 0:2], big_all[:, 0:2], 1e-5, None, ALU.max)
                link(dve.tensor_scalar(big_all[:, 2:4], big_all[:, 2:4], 1e-15, None, ALU.max))
                link(dve.tensor_scalar(power[:].bitcast(I32), big_all[:, 0:4].bitcast(I32), 0x7F800000, None, ALU.bitwise_and))
                link(dve.reciprocal(inv_power[:], power[:]))
                dve.tensor_scalar(w_scale[:, 0:3], inv_power[:, 0:3], QKV_SCALE / XA_SCALE, None, ALU.mult)
                dve.tensor_scalar(w_scale[:, 3:4], inv_power[:, 3:4], WO_SCALE, None, ALU.mult)
                dve.tensor_scalar(b_scale[:], inv_power[:, 0:3], QKV_SCALE, None, ALU.mult)
                dve.scalar_tensor_tensor(back[:, 0:1], power[:, 0:1], HD ** -0.5 / QKV_SCALE ** 2, power[:, 1:2], ALU.mult, ALU.mult)
                link(dve.scalar_tensor_tensor(back[:, 1:2], power[:, 2:3], 1 / (QKV_SCALE * WO_SCALE), power[:, 3:4], ALU.mult, ALU.mult))
                link(dve.tensor_tensor(b_in[:], b_in[:], b_scale[:].unsqueeze(2).to_broadcast([P, 3, KD]), ALU.mult))
                dve.wait_ge(S["rows_in"], 16)
                dve.wait_ge(S["gap_zeroed"], 1)
                row_statistics(dve, stats[0:NPATCH, 1], h_patch, S["bn_done"])
                dve.wait_ge(S["bn_done"], 3 + NB)
                moments(1, 3 + NB)
                dve.wait_ge(S["consts_done"], 1)
                for i in range(2):
                    for n in range(2):
                        dve.memset(v_p[i][n * HALF:(n + 1) * HALF, HI, :, n, HD:VW], 1.0)
                for n in range(4):
                    dve.wait_ge(S["w_high"], n + 1)
                    flat = lambda part: w[:, n, part].rearrange("p k d -> p (k d)")
                    dve.scalar_tensor_tensor(flat(LO), w_ps[n], w_scale[:, n:n + 1], flat(HI), ALU.mult, ALU.subtract).then_inc(S["w_low"], 1)

            @block.scalar
            def _(act):
                act.wait_ge(S["chain"], 6)
                for n in range(4):
                    act.wait_ge(S["w_turned"], n + 1)
                    act.activation(w[:, n, HI].rearrange("p k d -> p (k d)"), w_ps[n], ACT.Copy, scale=w_scale[:, n:n + 1]).then_inc(S["w_high"], 1)

            @block.tensor
            def _(pe):
                for n in range(4):
                    for k in range(KD):
                        for m in range(KD):
                            mm = pe.transpose(w_ps[n][:, k * D + m * P:k * D + (m + 1) * P],
                                              w_in[:, n, m, k * P:(k + 1) * P], T["ident"][:])
                    mm.then_inc(S["w_turned"], 1)

        WQ, WK, WV, WO = range(4)
        PASSES = ((HI, HI), (HI, LO), (LO, HI))
        PAT, TXT = slice(0, NPATCH), slice(NPATCH, SEQ)
        ROUNDS = 4
        QUADS = (slice(0, 4), slice(4, 8))

        def run(eng, step, tail):
            for i in range(2):
                for u in range(4):
                    step(4 * i + u, 2 * i + u // 2, u, i)
            with eng.Fori(2, STEPS // 4) as i:
                for u in range(4):
                    step(4 * i + u, 2 * i + u // 2, u, i)
            for u in range(3):
                tail(STEPS + u, BATCH + u // 2, u)

        def exponents(q):
            return (e_tt[q][:].rearrange("p h k -> p (h k)"), e_p[q][:].rearrange("p r h k -> p (r h) k")[:, :, 0:NPATCH])

        def turned(part, n):
            if n < 2:
                return eT_tt[:, part, 4 * n:4 * n + 4, :].rearrange("p h q -> p (h q)"), turn[n][:]
            if n == 2:
                return eT_tp[:, part].rearrange("p j q -> p (j q)"), turn[0][:]
            return eT_pp[:, part].rearrange("p j q -> p (j q)"), turn[1][:, 0:PAIRS * NPATCH]

        def values_of(part, par):
            both = [(v_t[par][:, part, :, 0:HD], v_ps[:, 0:D].rearrange("p (h c) -> p h c", h=HEADS))]
            for n in range(2):
                rows = slice(n * HALF, (n + 1) * HALF)
                src = v_ps[rows, D:2 * D].rearrange("p (j h c) -> p j h c", h=2, c=HD)
                both.append((v_p[par][rows, part, :, n, 0:HD], src[:, :, n, :]))
            return both

        with nc.Block() as block:
            @block.tensor
            def _(pe):
                def product(out, left, right, first=True, last=True):
                    for n, (a, c) in enumerate(PASSES):
                        mm = pe.matmul(out, left(a), right(c), start=first and n == 0, stop=last and n == 2)
                    return mm

                def turn_xn(b):
                    pe.wait_ge(S["xn_ready"], b + 1)
                    for k in range(KD):
                        pe.transpose(x_ps[:, k * SEQ + NPATCH:(k + 1) * SEQ], xn[:, k * P:(k + 1) * P], T["ident"][:])
                        mm = pe.transpose(x_ps[:, k * SEQ:k * SEQ + NPATCH], xn_p[:, k * P:(k + 1) * P],
                                          T["ident"][0:NPATCH, 0:NPATCH])
                    mm.then_inc(S["xt_done"], 1)

                def queries_keys(par, g):
                    cols = slice(g * GD, (g + 1) * GD)
                    for n, of in enumerate((WQ, WK)):
                        for k in range(KD):
                            mm = product(x_ps[:, n * SEQ:(n + 1) * SEQ], lambda a: w[:, of, a, k, cols],
                                         lambda c: x[par][:, c, k, 0:SEQ], k == 0, k == KD - 1)
                    mm.then_inc(S["qk_done"], 1)

                def values(par):
                    for n, rows in enumerate((TXT, slice(SEQ, SEQ + 2 * HALF))):
                        for k in range(KD):
                            mm = product(v_ps[:, n * D:(n + 1) * D], lambda a: x[par][:, a, k, rows],
                                         lambda c: w[:, WV, c, k, :], k == 0, k == KD - 1)
                    mm.then_inc(S["v_done"], 1)

                def turn_text(q, projected):
                    for n in range(2):
                        if n == 1 and projected is not None:
                            pe.wait_ge(S["h2_ready"], projected)
                        for h in range(4):
                            mm = pe.transpose(turn[n][:, h * TEXT:(h + 1) * TEXT], e_tt[q][:, 4 * n + h, :], T["ident"][:])
                        mm.then_inc(S["t_done"], 1)

                def turn_patches(q):
                    for j in range(PAIRS):
                        mm = pe.transpose(turn[0][:, j * TEXT:(j + 1) * TEXT],
                                          e_p[q][:, 0, 2 * j:2 * j + 2, :].rearrange("p h k -> p (h k)"), T["ident"][:])
                    mm.then_inc(S["t_done"], 1)
                    for j in range(PAIRS):
                        mm = pe.transpose(turn[1][:, j * NPATCH:(j + 1) * NPATCH],
                                          e_p[q][0:NPATCH, 1, 2 * j:2 * j + 2, :].rearrange("p h k -> p (h k)"),
                                          T["ident"][0:NPATCH, 0:NPATCH])
                    mm.then_inc(S["t_done"], 1)

                def attend_text(par, g):
                    for h in range(HG):
                        product(v_ps[:, h * VW:(h + 1) * VW], lambda p: eT_tt[:, p, h, :],
                                lambda c: v_t[par][:, c, g * HG + h, :], h == 0, False)

                def attend_patches(par, g):
                    for rows, turned, at in ((slice(0, NPATCH), eT_pp, HG * VW), (slice(0, P), eT_tp, 0)):
                        for j in range(PAIRS):
                            pair = v_ps[rows, at + 2 * j * VW:at + 2 * (j + 1) * VW]
                            mm = product(pair, lambda p: turned[:, p, j, :],
                                         lambda c: v_p[par][:, c, g * PAIRS + j].rearrange("p h c -> p (h c)"),
                                         False, at == 0 and j == PAIRS - 1)
                    mm.then_inc(S["o_done"], 1)

                def turn_o():
                    for k in range(KD):
                        pe.transpose(v_ps[:, k * SEQ + NPATCH:(k + 1) * SEQ], o[:, k * P:(k + 1) * P], T["ident"][:])
                        mm = pe.transpose(v_ps[:, k * SEQ:k * SEQ + NPATCH], o_p[:, k * P:(k + 1) * P],
                                          T["ident"][0:NPATCH, 0:NPATCH])
                    mm.then_inc(S["ot_done"], 1)

                def out_project():
                    for rows, out in ((TXT, turn[1][:, 0:D]), (PAT, turn[1][0:NPATCH, D:2 * D])):
                        for k in range(KD):
                            mm = product(out, lambda a: oT[:, a, k, rows], lambda c: w[:, WO, c, k, :], k == 0, k == KD - 1)
                    mm.then_inc(S["wo_done"], 1)

                def patch_scores(s, q):
                    pe.wait_ge(S["kbd_ready"], s + 1)
                    if reached(s, 1):
                        pe.wait_ge(S["shifted"], s)
                    out = [sc_p[:, n, 0:HG * NPATCH] for n in range(2)]
                    product(out[0], lambda a: qk[q][:, 0, a, TXT], lambda c: kbd[q][:, c, :, PAT])
                    pe.matmul(out[1], identb[:], causal_p[:].rearrange("p h k -> p (h k)"), start=True, stop=False)
                    product(out[1], lambda a: qk[q][:, 0, a, 0:P], lambda c: kbd[q][:, c, :, PAT], False).then_inc(S["s_done"], 1)

                def text_scores(q):
                    for heads in QUADS:
                        pe.matmul(sc[:, heads, :], identb[:], causal[:], start=True, stop=False)
                        product(sc[:, heads, :], lambda a: qk[q][:, 0, a, TXT], lambda c: kbd[q][:, c, heads, TXT], False).then_inc(S["s_done"], 1)

                def step(s, b, u, i, live=True):
                    g, a, q = u % 2, s - 2, u % 2
                    lagged = reached(s, 2) and not (isinstance(s, int) and s >= STEPS + 2)
                    if lagged:
                        pe.wait_ge(S["exp_done"], a + 1)
                        turn_text(q, b - 1 if g == 1 and reached(b, 2) else None)
                    if reached(s, 3):
                        pe.wait_ge(S["o_ready"], s - 2)
                    if g == 0 and reached(b, 2):
                        turn_o()
                    if g == 1 and live:
                        pe.wait_ge(S["x_doubled"], b + 1)
                        values((u // 2) % 2)
                    if live:
                        pe.wait_ge(S["x_lo"], b + 1 + g)
                        pe.wait_ge(S["qk_lo"], s + 1)
                        queries_keys((u + 1) // 2 % 2, (u + 1) % 2)
                        patch_scores(s, q)
                    if lagged:
                        pe.wait_ge(S["t_lo"], ROUNDS * a + 2)
                        turn_patches(q)
                    if live:
                        text_scores(q)
                    if lagged:
                        pe.wait_ge(S["t_lo"], ROUNDS * a + 4)
                    if g == 0 and reached(b, 2):
                        pe.wait_ge(S["ot_lo"], b - 1)
                        out_project()
                    if lagged:
                        if g == 0:
                            pe.wait_ge(S["v_lo"], b)
                        elif live:
                            pe.wait_ge(S["v_lo"], b + 1)
                        attend_text((u // 2 + 1) % 2, g)
                        attend_patches((u // 2 + 1) % 2, g)
                    if g == 0 and live:
                        pe.wait_ge(S["qk_lo"], s + 2)
                        turn_xn(b + 1)

                turn_xn(0)
                pe.wait_ge(S["x_lo"], 1)
                queries_keys(0, 0)
                run(pe, step, lambda s, b, u: step(s, b, u, 0, False))

            @block.scalar
            def _(act):
                def turned_high(a, n):
                    act.wait_ge(S["t_done"], ROUNDS * a + n + 1)
                    to, src = turned(HI, n)
                    act.activation(to, src, ACT.Copy, scale=E_SCALE).then_inc(S["t_hi"], 1)

                def exponential(t):
                    return act.activation(t, t, ACT.Exp, scale=back[0:t.shape[0], 0:1])

                def x_high(b, par):
                    act.wait_ge(S["xt_done"], b + 1)
                    act.activation(x[par][:, HI, :, 0:SEQ], x_ps[:, 0:KD * SEQ].rearrange("p (k c) -> p k c", k=KD),
                                   ACT.Copy, scale=XA_SCALE).then_inc(S["x_hi"], 1)

                def qk_high(s, q):
                    act.wait_ge(S["qk_done"], s + 1)
                    for n in range(2):
                        last = act.activation(qk[q][:, n, HI, :], x_ps[:, n * SEQ:(n + 1) * SEQ], ACT.Identity, bias=b_in[:, n, q:q + 1])
                    last.then_inc(S["qk_hi"], 1)

                def step(s, b, u, i, live=True):
                    g, a = u % 2, s - 2
                    lagged = reached(s, 2) and not (isinstance(s, int) and s >= STEPS + 2)
                    if lagged:
                        turned_high(a, 0)
                        turned_high(a, 1)
                    if g == 0 and reached(b, 2):
                        act.wait_ge(S["ot_done"], b - 1)
                        for k in range(KD):
                            last = act.activation(oT[:, HI, k], v_ps[:, k * SEQ:(k + 1) * SEQ], ACT.Identity, bias=b_in[:, 2, k:k + 1])
                        last.then_inc(S["ot_hi"], 1)
                    if g == 1 and live:
                        act.wait_ge(S["v_done"], b + 1)
                        for to, src in values_of(HI, u // 2 % 2):
                            last = act.activation(to, src, ACT.Copy)
                        last.then_inc(S["v_hi"], 1)
                    if live:
                        qk_high(s + 1, (u + 1) % 2)
                    exp = reached(s, 1) and (live or u == 0)
                    if exp:
                        act.wait_ge(S["shifted"], s)
                        exponential(exponents((u + 1) % 2)[0])
                    if lagged:
                        turned_high(a, 2)
                        turned_high(a, 3)
                    if exp:
                        for t in exponents((u + 1) % 2)[1:]:
                            last = exponential(t)
                        last.then_inc(S["exp_done"], 1)
                    if g == 0 and live:
                        x_high(b + 1, (u // 2 + 1) % 2)

                x_high(0, 0)
                qk_high(0, 0)
                run(act, step, lambda s, b, u: step(s, b, u, 0, False))

            @block.gpsimd
            def _(g):
                def blocks(s, q):
                    g.wait_ge(S["qk_lo"], s + 1)
                    for part in (HI, LO):
                        last = g.tensor_tensor(kbd[q][:, part], qk[q][:, 1, part].unsqueeze(1).to_broadcast([P, HG, SEQ]),
                                               head_of[:].unsqueeze(2).to_broadcast([P, HG, SEQ]), ALU.mult)
                    last.then_inc(S["kbd_ready"], 1)

                def normed(b):
                    row = lambda t: t[:, bass.ds(b, 1), :].rearrange("p a d -> p (a d)")
                    sets = ((xn, h_text, b, P), (xn_p, h_patch, NB + b, NPATCH))
                    for out, src, col, n in sets:
                        last = g.tensor_tensor(out[:], row(src), mean[0:n, bass.ds(col, 1)].to_broadcast([n, D]), ALU.subtract)
                    last.then_inc(S["centred"], 1)
                    g.wait_ge(S["centred"], b + 1)
                    for out, _, col, n in sets:
                        last = g.tensor_tensor(out[:], out[:], rstd[0:n, bass.ds(col, 1)].to_broadcast([n, D]), ALU.mult)
                    last.then_inc(S["xn_ready"], 1)

                def doubled(b, par):
                    g.wait_ge(S["x_lo"], b + 1)
                    t = x[par][:].rearrange("p a k c -> p (a k) c")
                    per = [P, 2 * KD, 2, NPATCH]
                    g.tensor_tensor(t[:, :, SEQ:].rearrange("p a (n c) -> p a n c", n=2)[:, :, :, 0:NPATCH],
                                    t[:, :, PAT].unsqueeze(2).to_broadcast(per),
                                    one[:].unsqueeze(2).unsqueeze(3).to_broadcast(per), ALU.mult).then_inc(S["x_doubled"], 1)

                def step(s, b, u, i):
                    blocks(s + 1, (u + 1) % 2)
                    if u % 2 == 0:
                        doubled(b + 1, (u // 2 + 1) % 2)
                    else:
                        g.wait_ge(S["xt_done"], b + 2)
                        normed(b + 2)
                        if reached(b, 2):
                            g.wait_ge(S["h2_ready"], b - 1)
                        row = lambda t: t[:, bass.ds(b, 1), :].rearrange("p a d -> p (a d)")
                        g.tensor_tensor(hb[u // 2][:], row(h_text), bo[:], ALU.add)
                        g.tensor_tensor(hb_p[u // 2][:], row(h_patch), bo[0:NPATCH], ALU.add).then_inc(S["hb_ready"], 1)

                normed(0)
                doubled(0, 0)
                g.wait_ge(S["xt_done"], 1)
                normed(1)
                blocks(0, 0)
                run(g, step, lambda s, b, u: None)

            @block.vector
            def _(dve):
                def low(to, src, high, factor=None, bias=None):
                    if bias is not None:
                        return dve.scalar_tensor_tensor(to, src, bias, high, ALU.add, ALU.subtract)
                    return dve.scalar_tensor_tensor(to, src, factor, high, ALU.mult, ALU.subtract)

                def turned_low(a, n):
                    dve.wait_ge(S["t_hi"], ROUNDS * a + n + 1)
                    (to, src), (high, _) = turned(LO, n), turned(HI, n)
                    low(to, src, high, E_SCALE).then_inc(S["t_lo"], 1)

                def x_low(b, par):
                    dve.wait_ge(S["x_hi"], b + 1)
                    low(x[par][:, LO, :, 0:SEQ], x_ps[:, 0:KD * SEQ].rearrange("p (k c) -> p k c", k=KD),
                        x[par][:, HI, :, 0:SEQ], XA_SCALE).then_inc(S["x_lo"], 1)

                def qk_low(s, q):
                    dve.wait_ge(S["qk_hi"], s + 1)
                    for n in range(2):
                        last = low(qk[q][:, n, LO, :], x_ps[:, n * SEQ:(n + 1) * SEQ], qk[q][:, n, HI, :], bias=b_in[:, n, q:q + 1])
                    last.then_inc(S["qk_lo"], 1)

                by_patches = sc_p[:, :, 0:HG * NPATCH].rearrange("p r (h k) -> p r h k", h=HG)

                def largest_patches(s):
                    dve.wait_ge(S["s_done"], 3 * s + 1)
                    dve.tensor_reduce(top[:], by_patches, AX, ALU.max)

                def largest_text(s):
                    for n, heads in enumerate(QUADS):
                        dve.wait_ge(S["s_done"], 3 * s + 2 + n)
                        last = dve.tensor_reduce(top_t[:, heads], sc[:, heads, :], AX, ALU.max)
                    last.then_inc(S["maxed"], 1)
                    dve.wait_ge(S["maxed"], 2 * s + 1)
                    dve.tensor_tensor(top[:, 0], top[:, 0], top_t[:], ALU.max).then_inc(S["maxed"], 1)

                def shift(s, q):
                    dve.wait_ge(S["maxed"], 2 * s + 2)
                    dve.tensor_tensor(e_tt[q][:], sc[:], top[:, 0].unsqueeze(2).to_broadcast([P, HG, TEXT]), ALU.subtract)
                    dve.tensor_tensor(e_p[q][:, :, :, 0:NPATCH], by_patches, top[:].unsqueeze(3).to_broadcast([P, 2, HG, NPATCH]),
                                      ALU.subtract).then_inc(S["shifted"], 1)

                def divide(a, g):
                    dve.wait_ge(S["o_done"], a + 1)
                    sets = ((o, inv, v_ps[:, 0:HG * VW], P), (o_p, inv_p, v_ps[0:NPATCH, HG * VW:2 * HG * VW], NPATCH))
                    for _, r, src, n in sets:
                        last = dve.reciprocal(r[:], src.rearrange("p (h c) -> p h c", c=VW)[:, :, HD])
                    last.then_inc(S["inverted"], 1)
                    dve.wait_ge(S["inverted"], a + 1)
                    for out, r, src, n in sets:
                        last = dve.tensor_tensor(out[:, g * GD:(g + 1) * GD].rearrange("p (h c) -> p h c", h=HG),
                                                 src.rearrange("p (h c) -> p h c", c=VW)[:, :, 0:HD],
                                                 r[:].unsqueeze(2).to_broadcast([n, HG, HD]), ALU.mult)
                    last.then_inc(S["o_ready"], 1)

                def residual(b, par, old):
                    dve.wait_ge(S["wo_done"], b + 1)
                    dve.wait_ge(S["hb_ready"], b + 1)
                    if reached(old, 1):
                        dve.wait_ge(h2_stored[par], 32 * old)
                    dve.scalar_tensor_tensor(h2[par][:], turn[1][:, 0:D], back[:, 1:2], hb[par][:], ALU.mult, ALU.add)
                    dve.scalar_tensor_tensor(h2_p[par][:], turn[1][0:NPATCH, D:2 * D], back[0:NPATCH, 1:2], hb_p[par][:],
                                             ALU.mult, ALU.add).then_inc(S["h2_ready"], 1)

                def step(s, b, u, i, live=True):
                    g, a = u % 2, s - 2
                    lagged = reached(s, 2) and not (isinstance(s, int) and s >= STEPS + 2)
                    if reached(s, 1) and (live or u == 0):
                        shift(s - 1, (u + 1) % 2)
                    if lagged:
                        turned_low(a, 0)
                        turned_low(a, 1)
                    if g == 1 and live:
                        dve.wait_ge(S["v_hi"], b + 1)
                        for (to, src), (high, _) in zip(values_of(LO, u // 2 % 2), values_of(HI, u // 2 % 2)):
                            last = dve.tensor_tensor(to, src, high, ALU.subtract)
                        last.then_inc(S["v_lo"], 1)
                    if g == 0 and reached(b, 2):
                        dve.wait_ge(S["ot_hi"], b - 1)
                        for k in range(KD):
                            last = low(oT[:, LO, k], v_ps[:, k * SEQ:(k + 1) * SEQ], oT[:, HI, k], bias=b_in[:, 2, k:k + 1])
                        last.then_inc(S["ot_lo"], 1)
                    if live:
                        qk_low(s + 1, (u + 1) % 2)
                        largest_patches(s)
                    if lagged:
                        turned_low(a, 2)
                        turned_low(a, 3)
                    if live:
                        largest_text(s)
                    if g == 0 and reached(b, 2):
                        residual(b - 2, u // 2 % 2, i - 1)
                    if lagged:
                        divide(a, g)
                    if g == 0 and live:
                        x_low(b + 1, (u // 2 + 1) % 2)

                x_low(0, 0)
                qk_low(0, 0)
                run(dve, step, lambda s, b, u: step(s, b, u, BATCH // 2, False))

            @block.sync
            def _(sp):
                shared_and_zeros(sp, A, T, w1s, w2s, zeros, S["shared_in"], S["rest_zeroed"])
                with sp.Fori(0, BATCH // 2) as i:
                    sp.dma_start(T["xg"][bass.ds(i * ZROWS, ZROWS), :].rearrange("r d -> (r d)").rearrange("(p q) -> p q", p=P), zeros[:]).then_inc(S["zeroed"], 16)
                    for par in range(2):
                        b = 2 * i + par
                        sp.wait_ge(S["h2_ready"], b + 1)
                        sp.dma_start(T["h2"][bass.ds(b * SEQ + NPATCH, TEXT), :], h2[par][:]).then_inc(h2_stored[par], 16)
                        sp.dma_start(T["h2"][bass.ds(b * SEQ, NPATCH), :], h2_p[par][:]).then_inc(h2_stored[par], 16)
                for par in range(2):
                    sp.wait_ge(h2_stored[par], 16 * BATCH)
                sp.wait_ge(S["zeroed"], 16 * (BATCH // 2))
                sp.wait_ge(S["rest_zeroed"], 32)
                sp.wait_ge(S["shared_in"], 16 * 2 * SHARED)




def shared_and_zeros(sp, A, T, w1, w2, zeros, shared_in, rest_zeroed):
    for e in range(SHARED):
        sp.dma_start(w1[:, e].rearrange("p n k c -> p (n k c)").bitcast(F32).rearrange("p (k c) -> p k c", k=KD),
                     A["W1_s"][e].rearrange("(k p) c -> p k c", p=P)).then_inc(shared_in, 16)
        sp.dma_start(w2[:, e].rearrange("p n j d -> p (n j d)").bitcast(F32).rearrange("p (j d) -> p j d", j=HJ),
                     A["W2_s"][e].rearrange("(j p) d -> p j d", p=P)).then_inc(shared_in, 16)
    for name in ("xn", "base"):
        rest = T[name][TOKENS:, :]
        sp.dma_start(rest.rearrange("(p q) d -> p (q d)", p=P), zeros[:, 0:rest.shape[0] * D // P]).then_inc(rest_zeroed, 16)

EXPERTS, SHARED, TOP = 8, 2, 2
HID = 1024
HJ = HID // P
TILE = 256
BLK = TILE // P
NT = (TOP * TOKENS + EXPERTS * (TILE - 1)) // TILE
GROUPS = -(-TOKENS // TILE)
RMS_EPS = 1.1920929e-07
X_SCALE = 1024.0


def router(nc, A, T, w1s, w2s):
    with ExitStack() as ctx:
        sb = lambda n, s, d=F32: ctx.enter_context(nc.sbuf_tensor(n, s, d))
        h2 = sb("r_h2", [P, TT, D])
        stats = sb("r_stats", [P, TT, 6])
        mean, var, gap, ms = (sb(f"r_{n}", [P, TT]) for n in ("mean", "var", "gap", "ms"))
        a, r, inv_r, ar, opa, nma = (sb(f"r_{n}", [P, TT]) for n in ("a", "r", "inv_r", "ar", "opa", "nma"))
        minus_half = sb("r_minus_half", [P, TT])
        RING = 4
        xr = [sb(f"r_xn{i}", [P, D]) for i in range(RING)]
        xT = [sb(f"r_xT{i}", [P, KD, P]) for i in range(2)]
        cent = sb("r_cent", [P, KD, EXPERTS])
        b2s = sb("r_b2s", [P, SHARED, D])
        score = sb("r_score", [P, TT, EXPERTS])
        order_i, order = sb("r_order_i", [P, EXPERTS], I32), sb("r_order", [P, EXPERTS])
        one = [sb(f"r_one{n}", [P, TT, EXPERTS]) for n in range(TOP)]
        rest, sel, gate, pos, cnt, run_a, run_b, slot, pick = (
            sb(f"r_{n}", [P, TT, EXPERTS]) for n in ("rest", "sel", "gate", "pos", "cnt", "run_a", "run_b", "slot", "pick"))
        total, inv_total, most = (sb(f"r_{n}", [P, TT]) for n in ("total", "inv_total", "most"))
        slot_f = sb("r_slot_f", [P, 2, TT])
        before, ones = sb("r_before", [P, P]), sb("r_ones", [P, P])
        padded_i = sb("r_padded_i", [P, EXPERTS], I32)
        padded, base_a, base_b = (sb(f"r_{n}", [P, EXPERTS]) for n in ("padded", "base_a", "base_b"))
        start_i, start = sb("r_start_i", [P, NT], I32), sb("r_start", [P, NT])
        passed, tile_e = sb("r_passed", [P, NT, EXPERTS - 1]), sb("r_tile_e", [P, NT])
        ps = [ctx.enter_context(nc.psum_tensor(f"r_ps{i}", [P, 512], F32)) for i in range(6)]
        W = Weights(nc, ctx, A, T, "_s", w1s, w2s, SHARED, SHARED)
        SETS = (("_s", SHARED), ("_r", EXPERTS))
        b1_rows = {w: sb("b1_rows" + w, [c * HJ, P]) for w, c in SETS}
        b1_ps = {w: ctx.enter_context(nc.psum_tensor("b1_ps" + w, [P, c * HJ], F32)) for w, c in SETS}
        PARTS = [(e, part) for e in range(SHARED) for part in range(W.PARTS)]
        names = ("h2_in_base small_in consts bn_done eps_done root_done xn_ready turned xT_ready "
                 "logits_done scaled scored chain sel_ready counted base_ready base_stored consts_b "
                 "b1_in b1_turned b1_ready").split()
        CUT = TT // 2
        RUNS = ((0, CUT), (CUT, TT))
        h2_in = [ctx.enter_context(nc.semaphore(f"r_h2_in{i}")) for i in range(2)]
        S = {n: ctx.enter_context(nc.semaphore(n)) for n in names}
        xn_stored = [ctx.enter_context(nc.semaphore(f"xn_stored{i}")) for i in range(RING)]

        with nc.Block() as block:
            @block.sync
            def _(sp):
                for w, _ in SETS:
                    sp.dma_start(b1_rows[w][:], A["b1" + w].rearrange("e (j p) -> (e j) p", p=P)).then_inc(S["b1_in"], 16)
                W.load_gain(nc, sp)
                for n, (lo, hi) in enumerate(RUNS):
                    sp.dma_start(h2[:, lo:hi], T["h2"][lo * P:hi * P].rearrange("(t p) d -> p t d", p=P)).then_inc(h2_in[n], 16)
                sp.dma_start(cent[:], A["centroids"].rearrange("(k p) e -> p k e", p=P)).then_inc(S["small_in"], 16)
                sp.dma_start(b2s[:].rearrange("p s d -> p (s d)"), A["b2_s"].rearrange("s d -> (s d)").partition_broadcast(P)).then_inc(S["small_in"], 16)

                def store(t, u):
                    sp.wait_ge(S["xn_ready"], t + 1)
                    sp.dma_start(T["xn"][bass.ds(t * P, P), :], xr[u][:]).then_inc(xn_stored[u], 16)
                    sp.wait_ge(S["base_ready"], t + 1)
                    sp.dma_start(T["base"][bass.ds(t * P, P), :], h2[:, bass.ds(t, 1), :].rearrange("p a d -> p (a d)")).then_inc(S["base_stored"], 16)
                with sp.Fori(0, TT // RING) as i:
                    for u in range(RING):
                        store(RING * i + u, u)
                store(TT - 1, 0)
                sp.wait_ge(S["base_stored"], 16 * TT)
                for u in range(RING):
                    sp.wait_ge(xn_stored[u], 16 * len(range(u, TT, RING)))

            @block.gpsimd
            def _(g):
                g.memset(minus_half[:], -0.5)
                g.memset(before[:], 1.0)
                g.memset(ones[:], 1.0)
                g.iota(order_i[:], pattern=[[-1, EXPERTS]], base=EXPERTS, channel_multiplier=0)
                g.iota(start_i[:], pattern=[[TILE, NT]], base=0, channel_multiplier=0).then_inc(S["consts"], 1)
                g.wait_ge(S["consts"], 1)
                g.affine_select(out=before[:], in_=before[:], compare_op=ALU.is_gt, fill=0.0, base=0,
                                pattern=[[1, P]], channel_multiplier=-1)
                g.tensor_copy(order[:], order_i[:])
                g.tensor_copy(start[:], start_i[:]).then_inc(S["consts_b"], 1)
                W.reduce(g)
                g.wait_ge(S["eps_done"], 1)
                g.tensor_tensor(a[:], var[:], minus_half[:], ALU.pow).then_inc(S["root_done"], 1)
                g.wait_ge(S["eps_done"], 2)
                g.tensor_tensor(r[:], ms[:], minus_half[:], ALU.pow).then_inc(S["root_done"], 1)
                g.wait_ge(S["small_in"], 32)
                g.tensor_tensor(b2s[:, 0], b2s[:, 0], b2s[:, 1], ALU.add).then_inc(S["consts_b"], 1)
                g.wait_ge(S["consts_b"], 2)
                with g.Fori(0, TT) as t:
                    g.wait_ge(S["h2_in_base"], t + 1)
                    row = h2[:, bass.ds(t, 1), :].rearrange("p a d -> p (a d)")
                    g.tensor_tensor(row, row, b2s[:, 0], ALU.add).then_inc(S["base_ready"], 1)

            @block.tensor
            def _(pe):
                pe.wait_ge(S["b1_in"], 32)
                for w, c in SETS:
                    pe.transpose(b1_ps[w][:], b1_rows[w][:], T["ident"][0:c * HJ, 0:c * HJ]).then_inc(S["b1_turned"], 1)
                pe.wait_ge(S["small_in"], 32)

                def turn(t, v):
                    u = v % 2
                    pe.wait_ge(S["xn_ready"], t + 1)
                    if reached(t, 2):
                        pe.wait_ge(S["xT_ready"], t - 1)
                    for k in range(KD):
                        mm = pe.transpose(ps[u][:, k * P:(k + 1) * P], xr[v][:, k * P:(k + 1) * P], T["ident"][:])
                    mm.then_inc(S["turned"], 1)

                def logits(t, u):
                    pe.wait_ge(S["xT_ready"], t + 1)
                    if reached(t, 2):
                        pe.wait_ge(S["scaled"], t - 1)
                    for k in range(KD):
                        mm = pe.matmul(ps[2 + u][:, 0:EXPERTS], xT[u][:, k, :], cent[:, k, :], start=k == 0, stop=k == KD - 1)
                    mm.then_inc(S["logits_done"], 1)
                turn(0, 0)
                for t in range(1, RING):
                    turn(t, t)
                    logits(t - 1, (t - 1) % 2)
                with pe.Fori(1, TT // RING) as i:
                    for v in range(RING):
                        turn(RING * i + v, v)
                        logits(RING * i + v - 1, (v - 1) % 2)
                turn(TT - 1, 0)
                logits(TT - 2, 1)
                logits(TT - 1, 0)
                pe.wait_ge(S["sel_ready"], 1)
                pe.wait_ge(S["consts_b"], 1)
                flat = sel[:].rearrange("p t e -> p (t e)")
                pe.matmul(ps[4][:, 0:TT * EXPERTS], before[:], flat, start=True, stop=True)
                pe.matmul(ps[5][:, 0:TT * EXPERTS], ones[:], flat, start=True, stop=True).then_inc(S["counted"], 1)

            @block.scalar
            def _(act):
                for e in range(SHARED):
                    W.stage(act, e)
                    for part in range(W.PARTS):
                        W.high(act, e, part)

                act.wait_ge(S["root_done"], 3)

                def turned(t, u):
                    act.wait_ge(S["turned"], t + 1)
                    act.activation(xT[u][:].rearrange("p k c -> p (k c)"), ps[u][:, 0:D], ACT.Copy).then_inc(S["xT_ready"], 1)

                def scaled(t, u):
                    act.wait_ge(S["logits_done"], t + 1)
                    act.activation(rest[:, bass.ds(t, 1), :].rearrange("p a e -> p (a e)"), ps[2 + u][:, 0:EXPERTS],
                                   ACT.Copy, scale=inv_r[:, bass.ds(t, 1)]).then_inc(S["scaled"], 1)
                turned(0, 0)
                turned(1, 1)
                scaled(0, 0)
                with act.Fori(1, TT // 2) as i:
                    turned(2 * i, 0)
                    scaled(2 * i - 1, 1)
                    turned(2 * i + 1, 1)
                    scaled(2 * i, 0)
                turned(TT - 1, 0)
                scaled(TT - 2, 1)
                scaled(TT - 1, 0)
                act.wait_ge(S["scaled"], TT)
                act.activation(score[:], rest[:], ACT.Sigmoid).then_inc(S["scored"], 1)

            @block.vector
            def _(dve):
                dve.wait_ge(S["b1_turned"], 2)
                for w, _ in SETS:
                    dve.tensor_copy(T["b1" + w][:], b1_ps[w][:]).then_inc(S["b1_ready"], 1)
                dve.wait_ge(S["b1_ready"], 2)
                for e, part in PARTS:
                    W.largest(dve, e, part)
                W.find_largest(dve)
                W.find_scales(dve)
                for n, (lo, hi) in enumerate(RUNS):
                    dve.wait_ge(h2_in[n], 16)
                    each = 5
                    assert lo % each == 0 and (hi - lo - n) % each == 0
                    with dve.Fori(lo // each, (hi - n) // each) as i:
                        for u in range(each):
                            row = lambda x: x[:, bass.ds(each * i + u, 1), :].rearrange("p a d -> p (a d)")
                            dve.bn_stats(row(stats), row(h2)).then_inc(S["bn_done"], 1)
                dve.bn_stats(stats[:, TT - 1, :], h2[:, TT - 1, :]).then_inc(S["bn_done"], 1)
                dve.wait_ge(S["bn_done"], TT)
                moments_of(dve, stats[:], mean, var, gap, S["bn_done"], TT)
                links = [0]

                def link(ins):
                    ins.then_inc(S["chain"], 1)
                    links[0] += 1
                    dve.wait_ge(S["chain"], links[0])
                link(dve.tensor_scalar(ms[:], var[:], 1.0 / D, None, ALU.mult))
                dve.tensor_scalar(var[:], var[:], 1.0 / D, LN_EPS, ALU.mult, ALU.add).then_inc(S["eps_done"], 1)
                dve.wait_ge(S["root_done"], 1)
                link(dve.tensor_tensor(ms[:], ms[:], a[:], ALU.mult))
                link(dve.tensor_tensor(ms[:], ms[:], a[:], ALU.mult))
                dve.tensor_scalar(ms[:], ms[:], RMS_EPS, None, ALU.add).then_inc(S["eps_done"], 1)
                dve.tensor_scalar(opa[:], a[:], 1.0, None, ALU.add)
                link(dve.scalar_tensor_tensor(nma[:], mean[:], -1.0, a[:], ALU.mult, ALU.mult))
                dve.wait_ge(S["root_done"], 2)
                dve.tensor_tensor(inv_r[:], ms[:], r[:], ALU.mult).then_inc(S["root_done"], 1)
                link(dve.tensor_tensor(ar[:], a[:], r[:], ALU.mult))

                def tile(t, u, stored):
                    if stored is not None:
                        dve.wait_ge(xn_stored[u], 16 * stored)
                        dve.wait_ge(S["turned"], t - RING + 1)
                    row = h2[:, bass.ds(t, 1), :].rearrange("p a d -> p (a d)")
                    dve.tensor_scalar(xr[u][:], row, mean[:, bass.ds(t, 1)], ar[:, bass.ds(t, 1)],
                                      ALU.subtract, ALU.mult).then_inc(S["xn_ready"], 1)
                    dve.tensor_scalar(row, row, opa[:, bass.ds(t, 1)], nma[:, bass.ds(t, 1)], ALU.mult,
                                      ALU.add).then_inc(S["h2_in_base"], 1)
                for u in range(RING):
                    tile(u, u, None)
                cuts = [1 + n * (TT // RING - 1) // (len(PARTS) // 2) for n in range(len(PARTS) // 2 + 1)]
                for n in range(len(PARTS) // 2):
                    with dve.Fori(cuts[n], cuts[n + 1]) as i:
                        for u in range(RING):
                            tile(RING * i + u, u, i)
                    for e, part in PARTS[2 * n:2 * n + 2]:
                        W.low(dve, e, part)
                tile(TT - 1, 0, TT // RING)

                dve.wait_ge(S["scored"], 1)
                dve.wait_ge(S["consts_b"], 1)
                per = [P, TT, EXPERTS]
                wide = lambda x: x[:].unsqueeze(2).to_broadcast(per)
                left = score
                for n in range(TOP):
                    link(dve.tensor_reduce(most[:], left[:], AX, ALU.max))
                    link(dve.tensor_tensor(pick[:], left[:], wide(most), ALU.is_equal))
                    link(dve.tensor_tensor(pick[:], pick[:], order[:].unsqueeze(1).to_broadcast(per), ALU.mult))
                    link(dve.tensor_reduce(most[:], pick[:], AX, ALU.max))
                    link(dve.tensor_tensor(one[n][:], pick[:], wide(most), ALU.is_equal))
                    if n == 0:
                        link(dve.scalar_tensor_tensor(rest[:], one[0][:], -2.0, score[:], ALU.mult, ALU.add))
                        left = rest
                dve.tensor_tensor(sel[:], one[0][:], one[1][:], ALU.add).then_inc(S["sel_ready"], 1)
                dve.wait_ge(S["sel_ready"], 1)
                link(dve.tensor_reduce(total[:], score[:], AX, ALU.add))
                link(dve.reciprocal(inv_total[:], total[:]))
                link(dve.tensor_tensor(gate[:], score[:], wide(inv_total), ALU.mult))
                dve.wait_ge(S["counted"], 1)
                link(dve.tensor_copy(pos[:].rearrange("p t e -> p (t e)"), ps[4][:, 0:TT * EXPERTS]))
                dve.tensor_copy(cnt[:].rearrange("p t e -> p (t e)"), ps[5][:, 0:TT * EXPERTS])
                link(dve.tensor_copy(run_a[:].rearrange("p t e -> p (t e)"), ps[5][:, 0:TT * EXPERTS]))
                x, y, d = run_a, run_b, 1
                while d < TT:
                    dve.tensor_copy(y[:, 0:d], x[:, 0:d])
                    link(dve.tensor_tensor(y[:, d:], x[:, d:], x[:, 0:TT - d], ALU.add))
                    x, y, d = y, x, 2 * d
                link(dve.tensor_scalar(padded_i[:], x[:, TT - 1], float(TILE - 1), None, ALU.add))
                link(dve.tensor_scalar(padded_i[:], padded_i[:], -TILE, None, ALU.bitwise_and))
                link(dve.tensor_copy(padded[:], padded_i[:]))
                link(dve.tensor_copy(base_a[:], padded[:]))
                xb, yb, d = base_a, base_b, 1
                while d < EXPERTS:
                    dve.tensor_copy(yb[:, 0:d], xb[:, 0:d])
                    link(dve.tensor_tensor(yb[:, d:], xb[:, d:], xb[:, 0:EXPERTS - d], ALU.add))
                    xb, yb, d = yb, xb, 2 * d
                link(dve.tensor_tensor(yb[:], xb[:], padded[:], ALU.subtract))
                dve.tensor_tensor(pos[:], pos[:], x[:], ALU.add)
                per7 = [P, NT, EXPERTS - 1]
                link(dve.tensor_tensor(passed[:], yb[:, 1:].unsqueeze(1).to_broadcast(per7),
                                       start[:].unsqueeze(2).to_broadcast(per7), ALU.is_le))
                link(dve.tensor_reduce(tile_e[:], passed[:], AX, ALU.add))
                link(dve.tensor_copy(T["tile_expert"][:], tile_e[:]))
                link(dve.tensor_tensor(pos[:], pos[:], cnt[:], ALU.subtract))
                link(dve.tensor_tensor(slot[:], pos[:], yb[:].unsqueeze(1).to_broadcast(per), ALU.add))
                for n in range(TOP):
                    for src, out in ((slot, slot_f[:, n]), (gate, T["gate"][:, n])):
                        link(dve.tensor_tensor(pick[:], src[:], one[n][:], ALU.mult))
                        link(dve.tensor_reduce(out, pick[:], AX, ALU.add))
                link(dve.tensor_copy(T["slot"][:], slot_f[:]))
                dve.wait_ge(W.S["lo_done"], len(PARTS))


class Weights:

    PARTS = 4

    def __init__(self, nc, ctx, A, T, which, w1, w2, count, held=1):
        sb = lambda n, s, d=F32: ctx.enter_context(nc.sbuf_tensor(n + which, s, d))
        self.A, self.which, self.w1, self.w2, self.count = A, which, w1, w2, count
        self.scale, self.b1 = T["scale" + which], T["b1" + which]
        self.raw = [sb(f"raw{i}", [P, HID]) for i in range(held * self.PARTS)]
        self.top = sb("top", [P, self.PARTS * count])
        self.gain, self.gains = sb("gain", [P, KD]), sb("gains", [P, KD])
        self.pair, self.big, self.big_all, self.power = (sb(n, [P, c]) for n, c in (("pair", KD), ("big", 3), ("big_all", 3), ("power", 3)))
        self.held = held > 1
        self.links = 0
        self.raw_in = [] if self.held else [ctx.enter_context(nc.semaphore(f"raw_in{i}{which}")) for i in range(self.PARTS)]
        self.S = {n: ctx.enter_context(nc.semaphore(n + which)) for n in
                  "gain_in topped chain bigs reduced scaled staged hi_done lo_done".split()}

    def load_gain(self, nc, sp):
        with nc.allow_non_contiguous_dma(reason="256 gains onto partitions"):
            sp.dma_start(self.gain[:], self.A["g" + self.which].rearrange("(k p) -> p k", p=P)).then_inc(self.S["gain_in"], 16)

    def of(self, tensor, e):
        return tensor[e] if isinstance(e, int) else tensor[bass.ds(e, 1)].rearrange("a b c -> (a b) c")

    def load(self, sp, e, second):
        for part in range(self.PARTS):
            before = self.count if second else 0
            if second:
                if isinstance(e, int) and e == 0:
                    sp.wait_ge(self.S["topped"], self.PARTS * self.count)
                else:
                    sp.wait_ge(self.S["lo_done"], self.PARTS * (e - 1) + part + 1)
            elif reached(e, 1):
                sp.wait_ge(self.S["topped"], self.PARTS * (e - 1) + part + 1)
            o = self.raw[part][:]
            if part < KD:
                src = self.of(self.A["W1" + self.which], e)[part * P:(part + 1) * P, :]
            else:
                o = o.rearrange("p (j d) -> p j d", j=HJ // 2)
                half = (part - KD) * (HJ // 2)
                src = self.of(self.A["W2" + self.which], e).rearrange("(j p) d -> p j d", p=P)[:, half:half + HJ // 2, :]
            sp.dma_start(o, src).then_inc(self.raw_in[part], 16)

    def largest(self, dve, e, part):
        if self.held:
            src = whole(self.w1, self.w2, e, part)
        else:
            dve.wait_ge(self.raw_in[part], 16 * (e + 1))
            src = self.raw[part][:]
        o = self.top[:, bass.ds(part * self.count + e, 1)]
        dve.tensor_reduce(o, src, AX, ALU.max, apply_absolute_value=True).then_inc(self.S["topped"], 1)

    def reduce(self, g):
        g.wait_ge(self.S["bigs"], 1)
        g.partition_all_reduce(self.big_all[:], self.big[:], P, bass.bass_isa.ReduceOp.max).then_inc(self.S["reduced"], 1)

    def link(self, dve, ins):
        ins.then_inc(self.S["chain"], 1)
        self.links += 1
        dve.wait_ge(self.S["chain"], self.links)

    def find_largest(self, dve):
        S, top, big, count = self.S, self.top, self.big, self.count
        dve.wait_ge(S["gain_in"], 16)
        dve.wait_ge(S["topped"], self.PARTS * count)
        dve.tensor_reduce(self.pair[:], top[:, 0:KD * count].rearrange("p (k e) -> p k e", k=KD), AX, ALU.max)
        dve.tensor_reduce(big[:, 1:2], top[:, KD * count:], AX, ALU.max)
        self.link(dve, dve.tensor_reduce(big[:, 2:3], self.b1[:], AX, ALU.max, apply_absolute_value=True))
        self.link(dve, dve.tensor_tensor(self.pair[:], self.pair[:], self.gain[:], ALU.mult))
        dve.tensor_reduce(big[:, 0:1], self.pair[:], AX, ALU.max, apply_absolute_value=True).then_inc(S["bigs"], 1)

    def find_scales(self, dve):
        S, big_all, power, scale = self.S, self.big_all, self.power, self.scale
        link = lambda ins: self.link(dve, ins)
        dve.wait_ge(S["reduced"], 1)
        link(dve.scalar_tensor_tensor(big_all[:, 2:3], big_all[:, 0:1], float(D), big_all[:, 2:3], ALU.mult, ALU.add))
        link(dve.tensor_scalar(big_all[:], big_all[:], 1e-30, None, ALU.max))
        link(dve.tensor_scalar(power[:].bitcast(I32), big_all[:].bitcast(I32), 0x7F800000, None, ALU.bitwise_and))
        link(dve.reciprocal(big_all[:], power[:]))
        dve.tensor_scalar(scale[:, 0:1], big_all[:, 0:1], 2.0 ** 13, None, ALU.mult)
        dve.tensor_scalar(scale[:, 1:2], power[:, 0:1], 2.0 ** -13 / X_SCALE, None, ALU.mult)
        dve.tensor_scalar(scale[:, 2:3], big_all[:, 2:3], 2.0 ** 14, None, ALU.mult)
        dve.tensor_scalar(scale[:, 3:4], big_all[:, 1:2], 2.0 ** 13, None, ALU.mult)
        link(dve.scalar_tensor_tensor(scale[:, 4:5], power[:, 1:2], 2.0 ** -27, power[:, 2:3], ALU.mult, ALU.mult))
        dve.tensor_scalar(self.gains[:], self.gain[:], scale[:, 0:1], None, ALU.mult).then_inc(S["scaled"], 1)
        dve.wait_ge(S["scaled"], 1)

    def halves(self, e, part):
        if part < KD:
            to = lambda n: (self.w1[:, e, n, part, :] if isinstance(e, int) else
                            self.w1[:, bass.ds(e, 1), n, part, :].rearrange("p a c -> p (a c)"))
            return self.raw[part][:], self.gains[:, part:part + 1], to
        rows = slice((part - KD) * (HJ // 2), (part - KD + 1) * (HJ // 2))
        to = lambda n: (self.w2[:, e, n, rows, :].rearrange("p j d -> p (j d)") if isinstance(e, int) else
                        self.w2[:, bass.ds(e, 1), n, rows, :].rearrange("p a j d -> p (a j d)"))
        return self.raw[part][:], self.scale[:, 3:4], to

    def stage(self, act, e):
        if e == 0:
            act.wait_ge(self.S["scaled"], 1)
        for part in range(self.PARTS):
            _, factor, _ = self.halves(e, part)
            act.activation(self.raw[e * self.PARTS + part][:], whole(self.w1, self.w2, e, part), ACT.Copy, scale=factor).then_inc(self.S["staged"], 1)

    def high(self, act, e, part):
        src, factor, to = self.halves(e, part)
        if self.held:
            act.wait_ge(self.S["staged"], self.PARTS * (e + 1))
            act.activation(to(0), self.raw[e * self.PARTS + part][:], ACT.Copy).then_inc(self.S["hi_done"], 1)
            return
        if isinstance(e, int) and e == 0 and part == 0:
            act.wait_ge(self.S["scaled"], 1)
        act.wait_ge(self.raw_in[part], 16 * (self.count + e + 1))
        act.activation(to(0), src, ACT.Copy, scale=factor).then_inc(self.S["hi_done"], 1)

    def low(self, dve, e, part):
        dve.wait_ge(self.S["hi_done"], self.PARTS * e + part + 1)
        src, factor, to = self.halves(e, part)
        if self.held:
            dve.tensor_tensor(to(1), self.raw[e * self.PARTS + part][:], to(0), ALU.subtract).then_inc(self.S["lo_done"], 1)
            return
        dve.scalar_tensor_tensor(to(1), src, factor, to(0), ALU.mult, ALU.subtract).then_inc(self.S["lo_done"], 1)


def whole(w1, w2, e, part):
    w = (w1, w2)[part // KD][:, e].rearrange("p n k c -> p (n k c)").bitcast(F32)
    return w[:, part % KD * HID:(part % KD + 1) * HID]


def ffn(nc, A, T, which, w1, w2, rounds, units, routed, routed_w=None):
    HI, LO = 0, 1
    src = T["xg"] if routed else T["xn"]
    with ExitStack() as ctx:
        sb = lambda n, s, d=F32: ctx.enter_context(nc.sbuf_tensor(n + which, s, d))
        sem = lambda n: ctx.enter_context(nc.semaphore(n + which))
        rows = sb("rows", [P, BLK, D])
        xh, xl = sb("xh", [P, KD, TILE], F16), sb("xl", [P, KD, TILE], F16)
        hf = [sb(f"hf{i}", [P, 2, TILE]) for i in range(2)]
        hh = [sb(f"hh{i}", [P, HJ, TILE], F16) for i in range(2)]
        hl = [sb(f"hl{i}", [P, HJ, TILE], F16) for i in range(2)]
        out = sb("out", [P, BLK, D])
        base = out
        b2 = sb("b2bc", [P, EXPERTS, D]) if routed else None
        pair = [ctx.enter_context(nc.psum_tensor(f"f_ps{i}{which}", [P, 2, TILE], F32)) for i in range(4)]
        y_ps = ctx.enter_context(nc.psum_tensor("f_y" + which, [P, BLK, D], F32))
        t_ps = ctx.enter_context(nc.psum_tensor("f_t" + which, [P, KD, TILE], F32))
        S = {n: sem(n) for n in "row_in added_in x_turned xh_ready xl_ready h_done gelu_done h_ready y_done y_ready y_stored staged".split()}
        scattered = None if routed else [sem(f"scattered{i}") for i in range(2)]
        scale, b1 = T["scale" + which], T["b1" + which]
        TILES = rounds * units if routed else rounds
        UNITS = rounds * units

        R = Weights(nc, ctx, A, T, "_r", *routed_w, EXPERTS) if routed_w else None
        FIND, SPLIT, LEFT = 2, 3 + EXPERTS, 3 + 2 * EXPERTS

        def run(eng, unit, tail, find=None, between=None, split=None):
            def one(i, extra, e):
                for u in range(units):
                    unit(units * i + u, u, i)
                    if extra:
                        extra(e, u)
            for i in range(2):
                one(i, None, 0)
            if R is None:
                with eng.Fori(2, rounds) as i:
                    one(i, None, 0)
            else:
                one(FIND, find, 0)
                with eng.Fori(FIND + 1, SPLIT - 1) as i:
                    one(i, find, i - FIND)
                if between:
                    between[0]()
                one(SPLIT - 1, None, 0)
                if between:
                    between[1]()
                one(SPLIT, split, 0)
                with eng.Fori(SPLIT + 1, LEFT) as i:
                    one(i, split, i - SPLIT)
                with eng.Fori(LEFT, rounds) as i:
                    one(i, None, 0)
            tail()

        def tile_of(n, i):
            return n if routed else i

        def turns(u):
            return routed or u == units - 1

        with nc.Block() as block:
            @block.sync
            def _(sp):
                def load(t):
                    sp.dma_start(rows[:], src[bass.ds(t * TILE, TILE), :].rearrange("(b p) d -> p b d", p=P)).then_inc(S["row_in"], 16)
                load(0)
                if routed:
                    sp.dma_start(b2[:].rearrange("p e d -> p (e d)"), A["b2" + which].rearrange("e d -> (e d)").partition_broadcast(P)).then_inc(S["added_in"], 16)
                if not routed:
                    sp.dma_start(base[:], T["base"][0:TILE, :].rearrange("(b p) d -> p b d", p=P)).then_inc(S["added_in"], 16)

                def store(t):
                    sp.wait_ge(S["y_ready"], t + 1)
                    dst = T["y"] if routed else T["part"]
                    sp.dma_start(dst[bass.ds(t * TILE, TILE), :].rearrange("(b p) d -> p b d", p=P), out[:]).then_inc(S["y_stored"], 16)
                sp.wait_ge(S["x_turned"], 1)
                load(1)

                def tile(t):
                    sp.wait_ge(S["x_turned"], t + 1)
                    load(t + 1)
                    if not routed:
                        store(t - 1)
                    elif reached(t, 2):
                        store(t - 2)
                    if not routed:
                        sp.wait_ge(S["y_stored"], 16 * t)
                        sp.dma_start(base[:], T["base"][bass.ds(t * TILE, TILE), :].rearrange("(b p) d -> p b d", p=P)).then_inc(S["added_in"], 16)
                if R is None:
                    tile(1)
                    with sp.Fori(2, TILES) as t:
                        tile(t)
                    store(TILES - 2)
                else:
                    R.load_gain(nc, sp)
                    tile(1)
                    for second, begin in ((False, FIND), (True, SPLIT)):
                        if second:
                            tile(SPLIT - 1)
                        R.load(sp, 0, second)
                        tile(begin)
                        with sp.Fori(begin + 1, begin + EXPERTS) as t:
                            R.load(sp, t - begin, second)
                            tile(t)
                    with sp.Fori(LEFT, TILES) as t:
                        tile(t)
                store(TILES - 1)
                sp.wait_ge(S["y_stored"], 16 * TILES)
                sp.wait_ge(S["row_in"], 16 * (TILES + 1))
                if not routed:
                    sp.wait_ge(S["added_in"], 16 * TILES)

            @block.tensor
            def _(pe):
                def turn(t):
                    pe.wait_ge(S["row_in"], 16 * (t + 1))
                    for k in range(KD):
                        for b in range(BLK):
                            mm = pe.transpose(t_ps[:, k, b * P:(b + 1) * P], rows[:, b, k * P:(k + 1) * P], T["ident"][:])
                    mm.then_inc(S["x_turned"], 1)

                def up(n, u, i, e):
                    pe.wait_ge(S["xl_ready"], tile_of(n, i) + 1)
                    for p in range(4):
                        if reached(n, 1):
                            pe.wait_ge(S["gelu_done"], 4 * n + p - 3)
                        for j2 in range(2):
                            o = pair[p][:, j2, :]
                            col = slice((2 * p + j2) * P, (2 * p + j2 + 1) * P)
                            for k in range(KD):
                                pe.matmul(o, w1_at(e, HI, k, col), xh[:, k, :], start=k == 0, stop=False)
                                pe.matmul(o, w1_at(e, HI, k, col), xl[:, k, :], start=False, stop=False)
                                mm = pe.matmul(o, w1_at(e, LO, k, col), xh[:, k, :], start=False, stop=k == KD - 1)
                        mm.then_inc(S["h_done"], 1)

                def down(n, u, tile, e):
                    first, last = routed or u == 0, routed or u == units - 1
                    pe.wait_ge(S["h_ready"], 4 * n + 4)
                    if first and reached(tile, 1):
                        pe.wait_ge(S["y_ready"], tile)
                    q = u % 2
                    for j in range(HJ):
                        for b in range(BLK):
                            o, col = y_ps[:, b, :], slice(b * P, (b + 1) * P)
                            pe.matmul(o, hh[q][:, j, col], w2_at(e, HI, j), start=first and j == 0 and b == 0, stop=False)
                            pe.matmul(o, hh[q][:, j, col], w2_at(e, LO, j), start=False, stop=False)
                            mm = pe.matmul(o, hl[q][:, j, col], w2_at(e, HI, j), start=False, stop=last and j == HJ - 1 and b == BLK - 1)
                    if last:
                        mm.then_inc(S["y_done"], 1)

                def w1_at(e, part, k, col):
                    if routed:
                        return w1[:, bass.ds(e, 1), part, k, col].rearrange("p a c -> p (a c)")
                    return w1[:, e, part, k, col]

                def w2_at(e, part, j):
                    if routed:
                        return w2[:, bass.ds(e, 1), part, j, :].rearrange("p a c -> p (a c)")
                    return w2[:, e, part, j, :]

                def expert(n):
                    return pe.value_load(T["tile_expert"][0:1, bass.ds(n, 1)], min_val=0, max_val=EXPERTS - 1)

                def unit(n, u, i):
                    pu = (u - 1) % units
                    e = expert(n) if routed else u
                    before = (expert(n - 1) if reached(n, 1) else None) if routed else pu
                    up(n, u, i, e)
                    if turns(u):
                        turn(tile_of(n, i) + 1)
                    if reached(n, 1):
                        down(n - 1, pu, tile_of(n - 1, i if u else i - 1), before)
                turn(0)
                run(pe, unit, lambda: down(UNITS - 1, units - 1, TILES - 1, expert(UNITS - 1) if routed else units - 1))

            @block.scalar
            def _(act):
                def split(t):
                    act.wait_ge(S["x_turned"], t + 1)
                    act.activation(xh[:].rearrange("p k c -> p (k c)"), t_ps[:].rearrange("p k c -> p (k c)"), ACT.Copy, scale=X_SCALE).then_inc(S["xh_ready"], 1)

                def unit(n, u, i):
                    if routed:
                        e = act.value_load(T["tile_expert"][0:1, bass.ds(n, 1)], min_val=0, max_val=EXPERTS - 1)
                    for p in range(4):
                        act.wait_ge(S["h_done"], 4 * n + p + 1)
                        if reached(n, 1) or p >= 2:
                            act.wait_ge(S["h_ready"], 4 * n + p - 1)
                        for j2 in range(2):
                            j = 2 * p + j2
                            bias = b1[:, bass.ds(e * HJ + j, 1)] if routed else b1[:, u * HJ + j:u * HJ + j + 1]
                            last = act.activation(hf[p % 2][:, j2, :], pair[p][:, j2, :], ACT.Gelu, bias=bias, scale=scale[:, 1:2])
                        last.then_inc(S["gelu_done"], 1)
                    if turns(u):
                        split(tile_of(n, i) + 1)
                split(0)
                per = Weights.PARTS // units
                run(act, unit, lambda: None,
                    split=lambda e, u: [R.high(act, e, part) for part in range(u * per, (u + 1) * per)])

            @block.vector
            def _(dve):
                def split(t):
                    dve.wait_ge(S["xh_ready"], t + 1)
                    dve.scalar_tensor_tensor(xl[:].rearrange("p k c -> p (k c)"), t_ps[:].rearrange("p k c -> p (k c)"), X_SCALE,
                                             xh[:].rearrange("p k c -> p (k c)"), ALU.mult, ALU.subtract).then_inc(S["xl_ready"], 1)

                def finish(n, tile):
                    dve.wait_ge(S["y_done"], tile + 1)
                    if reached(tile, 1):
                        dve.wait_ge(S["y_stored"], 16 * tile)
                    if routed:
                        e = dve.value_load(T["tile_expert"][0:1, bass.ds(n, 1)], min_val=0, max_val=EXPERTS - 1)
                        for b in range(BLK):
                            last = dve.scalar_tensor_tensor(out[:, b, :], y_ps[:, b, :], scale[:, 4:5],
                                                            b2[:, bass.ds(e, 1), :].rearrange("p a d -> p (a d)"), ALU.mult, ALU.add)
                    else:
                        dve.wait_ge(S["added_in"], 16 * (tile + 1))
                        last = dve.scalar_tensor_tensor(out[:], y_ps[:], scale[:, 4:5], base[:], ALU.mult, ALU.add)
                    last.then_inc(S["y_ready"], 1)

                def unit(n, u, i):
                    q = u % 2
                    for p in range(4):
                        dve.wait_ge(S["gelu_done"], 4 * n + p + 1)
                        o = slice(2 * p, 2 * p + 2)
                        dve.tensor_scalar(hh[q][:, o, :], hf[p % 2][:], scale[:, 2:3], None, ALU.mult).then_inc(S["staged"], 1)
                        dve.wait_ge(S["staged"], 4 * n + p + 1)
                        dve.scalar_tensor_tensor(hl[q][:, o, :], hf[p % 2][:], scale[:, 2:3], hh[q][:, o, :],
                                                 ALU.mult, ALU.subtract).then_inc(S["h_ready"], 1)
                    if turns(u):
                        split(tile_of(n, i) + 1)
                    pu = (u - 1) % units
                    if reached(n, 1) and (routed or pu == units - 1):
                        finish(n - 1, tile_of(n - 1, i if u else i - 1))
                split(0)
                if routed:
                    dve.wait_ge(S["added_in"], 16)
                per = Weights.PARTS // units
                parts = lambda f: lambda e, u: [f(dve, e, part) for part in range(u * per, (u + 1) * per)]
                if R is None:
                    run(dve, unit, lambda: finish(UNITS - 1, TILES - 1))
                else:
                    run(dve, unit, lambda: finish(UNITS - 1, TILES - 1), parts(R.largest), (lambda: R.find_largest(dve), lambda: R.find_scales(dve)), parts(R.low))
                    dve.wait_ge(R.S["lo_done"], R.PARTS * EXPERTS)

            if not routed:
                @block.gpsimd
                def _(g):
                    scatter(g, nc, T, scattered, ctx)
                    R.reduce(g)


def scatter(g, nc, T, scattered, ctx):
    xr = [ctx.enter_context(nc.sbuf_tensor(f"sc_x{i}", [P, D], F32)) for i in range(2)]
    xr_in = [ctx.enter_context(nc.semaphore(f"sc_in{i}")) for i in range(2)]
    for t in range(TT):
        q = t % 2
        if t >= 2:
            g.wait_ge(scattered[q], 32 * (t // 2))
        g.dma_start(xr[q][:], T["xn"][t * P:(t + 1) * P, :]).then_inc(xr_in[q], 16)
        if t >= 1:
            send(g, T, xr, xr_in, scattered, t - 1)
    send(g, T, xr, xr_in, scattered, TT - 1)
    g.wait_ge(scattered[0], 32 * (TT // 2 + 1))
    g.wait_ge(scattered[1], 32 * (TT // 2))


def send(g, T, xr, xr_in, scattered, t):
    q = t % 2
    g.wait_ge(xr_in[q], 16 * (t // 2 + 1))
    for which in range(2):
        g.indirect_dma_start(T["xg"][:, :], bass.IndirectOffsetOnAxis(ap=T["slot"][:, which, t:t + 1], axis=0),
                             xr[q][:], None, bounds_check=NT * TILE - 1).then_inc(scattered[q], 16)


def combine(nc, T, out):
    with ExitStack() as ctx:
        RING = 4
        sb = lambda n, s, d=F32: ctx.enter_context(nc.sbuf_tensor(n, s, d))
        sem = lambda n: ctx.enter_context(nc.semaphore(n))
        part = [sb(f"c_part{i}", [P, D]) for i in range(RING)]
        ya = [sb(f"c_ya{i}", [P, D]) for i in range(RING)]
        yb = [sb(f"c_yb{i}", [P, D]) for i in range(RING)]
        part_in = [sem(f"c_part_in{i}") for i in range(RING)]
        y_in = [sem(f"c_y_in{i}") for i in range(RING)]
        stored = [sem(f"c_stored{i}") for i in range(RING)]
        done = sem("c_done")
        with nc.Block() as block:
            @block.gpsimd
            def _(g):
                for t in range(TT):
                    q = t % RING
                    if t >= RING:
                        g.wait_ge(y_in[q], 32 * (t // RING))
                        g.wait_ge(done, 2 * (t - RING + 1))
                    for which, y in ((0, ya), (1, yb)):
                        g.indirect_dma_start(y[q][:], None, T["y"][:, :], bass.IndirectOffsetOnAxis(ap=T["slot"][:, which, t:t + 1], axis=0),
                                             bounds_check=NT * TILE - 1).then_inc(y_in[q], 16)

            @block.sync
            def _(sp):
                for t in range(TT + 2):
                    if t < TT:
                        q = t % RING
                        if t >= RING:
                            sp.wait_ge(stored[q], 16 * (t // RING))
                        sp.dma_start(part[q][:], T["part"][t * P:(t + 1) * P, :]).then_inc(part_in[q], 16)
                    if t >= 2:
                        d = t - 2
                        sp.wait_ge(done, 2 * (d + 1))
                        sp.dma_start(out[d * P:(d + 1) * P, :], part[d % RING][:]).then_inc(stored[d % RING], 16)
                for q in range(RING):
                    sp.wait_ge(stored[q], 16 * len(range(q, TT, RING)))

            @block.vector
            def _(dve):
                for t in range(TT):
                    q = t % RING
                    dve.wait_ge(part_in[q], 16 * (t // RING + 1))
                    dve.wait_ge(y_in[q], 32 * (t // RING + 1))
                    dve.scalar_tensor_tensor(part[q][:], ya[q][:], T["gate"][:, 0, t:t + 1], part[q][:], ALU.mult, ALU.add).then_inc(done, 1)
                    dve.wait_ge(done, 2 * t + 1)
                    dve.scalar_tensor_tensor(part[q][:], yb[q][:], T["gate"][:, 1, t:t + 1], part[q][:], ALU.mult, ALU.add).then_inc(done, 1)


def early_fusion_block(nc, x, txt, tok_W, Wq, bq, Wk, bk, Wv, bv, Wo, bo, g_shared, W1_s, b1_s, W2_s, b2_s,
                       g_routed, W1_r, b1_r, W2_r, b2_r, centroids, out):
    A = {"Wq": Wq, "Wk": Wk, "Wv": Wv, "Wo": Wo, "bq": bq, "bk": bk, "bv": bv, "bo": bo, "centroids": centroids,
         "g_s": g_shared, "W1_s": W1_s, "b1_s": b1_s, "W2_s": W2_s, "b2_s": b2_s,
         "g_r": g_routed, "W1_r": W1_r, "b1_r": b1_r, "W2_r": W2_r, "b2_r": b2_r}
    with ExitStack() as ctx:
        sb = lambda n, s, d=F32: ctx.enter_context(nc.sbuf_tensor(n, s, d))
        rows = lambda n, count: nc.dram_tensor(n, [count, D], F32, kind="Internal").ap()
        T = {
            "ident": sb("ident", [P, P]),
            "slot": sb("slot", [P, TOP, TT], I32), "gate": sb("gate", [P, TOP, TT]),
            "tile_expert": sb("tile_expert", [P, NT], I32),
            "scale_s": sb("scale_s", [P, 5]), "scale_r": sb("scale_r", [P, 5]),
            "b1_s": sb("b1T_s", [P, SHARED * HJ]), "b1_r": sb("b1T_r", [P, EXPERTS * HJ]),
            "patch_h": rows("patch_h", BATCH * NPATCH), "h2": rows("h2_rows", TOKENS),
            "xn": rows("xn_rows", (GROUPS + 1) * TILE), "base": rows("base_rows", (GROUPS + 1) * TILE),
            "part": rows("part_rows", GROUPS * TILE),
            "xg": rows("slot_rows", (NT + 1) * TILE), "y": rows("y_rows", NT * TILE),
        }
        patches = nc.dram_tensor("patches", [BATCH * CHANNELS, IMAGE * IMAGE], F32, kind="Internal").ap()
        ident_done = ctx.enter_context(nc.semaphore("ident_done"))
        with nc.Block() as block:
            @block.gpsimd
            def _(g):
                g.memset(T["ident"][:], 0.0).then_inc(ident_done, 1)
                g.wait_ge(ident_done, 1)
                g.affine_select(out=T["ident"][:], in_=T["ident"][:], compare_op=ALU.not_equal, fill=1.0,
                                base=0, pattern=[[-1, P]], channel_multiplier=1).then_inc(ident_done, 1)
                g.wait_ge(ident_done, 2)
        w1s, w2s = sb("w1s", [P, SHARED, 2, KD, HID], F16), sb("w2s", [P, SHARED, 2, HJ, D], F16)
        with ExitStack() as attention_ctx:
            attention_inputs(nc, attention_ctx, T)
            patch_embed(nc, x, tok_W, patches, txt, A, T)
            attention(nc, A, T, w1s, w2s)
        router(nc, A, T, w1s, w2s)
        w1r, w2r = sb("w1r", [P, EXPERTS, 2, KD, HID], F16), sb("w2r", [P, EXPERTS, 2, HJ, D], F16)
        ffn(nc, A, T, "_s", w1s, w2s, GROUPS, SHARED, False, (w1r, w2r))
        ffn(nc, A, T, "_r", w1r, w2r, NT // 2, 2, True)
        combine(nc, T, out)


_INS = ['x', 'txt', 'L0_tok_W', 'L0_attn_Wq', 'L0_attn_bq', 'L0_attn_Wk', 'L0_attn_bk', 'L0_attn_Wv', 'L0_attn_bv',
        'L0_attn_Wo', 'L0_attn_bo', 'L0_ffn_g_shared', 'L0_ffn_W1_s', 'L0_ffn_b1_s', 'L0_ffn_W2_s', 'L0_ffn_b2_s',
        'L0_ffn_g_routed', 'L0_ffn_W1_r', 'L0_ffn_b1_r', 'L0_ffn_W2_r', 'L0_ffn_b2_r', 'L0_ffn_centroids']


def kernel(**inputs):
    import numpy as _np
    import concourse.bacc as _bacc
    from concourse import mybir as _mybir
    from concourse.bass_utils import run_bass_kernel_spmd as _run

    nc = _bacc.Bacc("TRN2", target_bir_lowering=False, num_devices=1)
    arrays, args = {}, []
    for name in _INS:
        a = _np.ascontiguousarray(inputs[name])
        arrays[f"in_{name}_dram"] = a
        args.append(nc.dram_tensor(f"in_{name}_dram", a.shape, _mybir.dt.from_np(a.dtype), kind="ExternalInput").ap())
    args.append(nc.dram_tensor("out_0_dram", (TOKENS, D), _mybir.dt.float32, kind="ExternalOutput").ap())
    early_fusion_block(nc, *args)
    r = _run(nc, [arrays], core_ids=[0])
    return _np.asarray(r.results[0]["out_0_dram"]).reshape(BATCH, SEQ, D)
```
